# Optimizing a Trainium2 kernel written in Bass

```python
import numpy as np
import jax
import jax.numpy as jnp

def _softmax(x, axis=-1):
    return jax.nn.softmax(x, axis=axis)

def _gelu(x):
    return jax.nn.gelu(x, approximate=True)

def _silu(x):
    return jax.nn.silu(x)

def _sigmoid(x):
    return jax.nn.sigmoid(x)

def _layernorm(x, axis=-1, eps=1e-05):
    m = jnp.mean(x, axis=axis, keepdims=True)
    v = jnp.var(x, axis=axis, keepdims=True)
    return (x - m) / jnp.sqrt(v + eps)

def _scatter_add(tgt, idx, src, axis=0):
    return tgt.at[idx].add(src)

def _segment_sum(src, seg, n):
    return jax.ops.segment_sum(src, seg, n)
kernel_name = 'mk_early_fusion_embed_d1_tok_img1024_r4_9761e1'

def setup_inputs(seed: int=0):
    np.random.seed(seed)
    _w = jnp.asarray

    def _rec_inputs():
        import jax
        import jax.numpy as jnp
        _rk = jax.random.key(seed)
        x = -0.00011082 + 0.999858 * jax.random.normal(jax.random.fold_in(_rk, 1), (8, 5, 128, 128), jnp.float32)
        x_txt = jax.random.randint(jax.random.fold_in(_rk, 51), (8, 32), 0, 31995, jnp.int32)
        return (x, x_txt)
    x, x_txt = _rec_inputs()

    def _L0_tok_setup():
        import jax, jax.numpy as jnp
        import numpy as np
        PATCH = 8
        EPS = 1e-05

        def _patchify(x):
            B, C, H, Wd = x.shape
            p = PATCH
            x = x.reshape(B, C, H // p, p, Wd // p, p)
            x = x.transpose(0, 2, 4, 1, 3, 5)
            return x.reshape(B, H // p * (Wd // p), C * p * p)
        key = jax.random.key(seed)
        k1, k2 = jax.random.split(key)
        B, C, H, W_ = (32, 5, 128, 128)
        in_feat, embed_dim = (C * PATCH * PATCH, 256)
        x = jax.random.normal(k1, (B, C, H, W_), dtype=jnp.float32)
        W = jax.random.normal(k2, (in_feat, embed_dim), dtype=jnp.float32) * (1.0 / np.sqrt(in_feat))
        gamma = jnp.ones((embed_dim,), dtype=jnp.float32)
        return {'x': x, 'W': W, 'gamma': gamma}
    _L0_tok_all = _L0_tok_setup()
    _L0_tok_in = {k: v for k, v in _L0_tok_all.items() if k in ('W', 'gamma')}
    del _L0_tok_all

    def _L0_txt_setup():
        import jax, jax.numpy as jnp
        import numpy as np
        NUM_EMBEDDINGS = 32000
        EMBEDDING_DIM = 256
        EPS = 1e-05
        key = jax.random.key(seed)
        k_w, k_idx = jax.random.split(key)
        weight = jax.random.normal(k_w, (NUM_EMBEDDINGS, EMBEDDING_DIM), dtype=jnp.float32)
        input = jax.random.randint(k_idx, (4, 1024), 0, NUM_EMBEDDINGS, dtype=jnp.int64)
        return {'input': input, 'weight': weight}
    _L0_txt_all = _L0_txt_setup()
    _L0_txt_in = {k: v for k, v in _L0_txt_all.items() if k in ('weight',)}
    del _L0_txt_all

    def _L0_attn_setup():
        import jax, jax.numpy as jnp
        import numpy as np
        DIM = 256
        N_HEADS = 16
        HEAD_DIM = DIM // N_HEADS
        D_LATENT = 64
        B, T = (1, 1024)
        key = jax.random.key(seed)
        ks = jax.random.split(key, 6)
        s = 0.02
        return {'x': jax.random.normal(ks[0], (B, T, DIM), dtype=jnp.float32), 'W_DKV': jax.random.normal(ks[1], (DIM, D_LATENT), dtype=jnp.float32) * s, 'W_UK': jax.random.normal(ks[2], (D_LATENT, DIM), dtype=jnp.float32) * s, 'W_UV': jax.random.normal(ks[3], (D_LATENT, DIM), dtype=jnp.float32) * s, 'W_UQ': jax.random.normal(ks[4], (DIM, DIM), dtype=jnp.float32) * s, 'W_O': jax.random.normal(ks[5], (DIM, DIM), dtype=jnp.float32) * s}
    _L0_attn_all = _L0_attn_setup()
    _L0_attn_in = {k: v for k, v in _L0_attn_all.items() if k in ('W_DKV', 'W_UK', 'W_UV', 'W_UQ', 'W_O')}
    del _L0_attn_all

    def _L0_ffn_setup():
        import jax, jax.numpy as jnp
        import numpy as np
        B, S, D, F, E = (2, 512, 256, 1024, 8)
        LN_EPS = 1e-05

        def _layer_norm(x, gamma, beta):
            mu = jnp.mean(x, axis=-1, keepdims=True)
            var = jnp.mean(jnp.square(x - mu), axis=-1, keepdims=True)
            return (x - mu) * jax.lax.rsqrt(var + LN_EPS) * gamma + beta
        key = jax.random.key(seed)
        ks = jax.random.split(key, 8)

        def xavier(k, shape):
            fan_in, fan_out = (shape[-1], shape[-2])
            a = jnp.sqrt(6.0 / (fan_in + fan_out))
            return jax.random.uniform(k, shape, jnp.float32, -a, a)
        return {'tgt': jax.random.normal(ks[0], (B, S, D), jnp.float32), 'Wr': xavier(ks[1], (E, D)), 'br': jnp.zeros((E,), jnp.float32), 'W1': xavier(ks[2], (E, F, D)), 'b1': jnp.zeros((E, F), jnp.float32), 'W2': xavier(ks[3], (E, D, F)), 'b2': jnp.zeros((E, D), jnp.float32), 'gamma': jnp.ones((D,), jnp.float32), 'beta': jnp.zeros((D,), jnp.float32)}
    _L0_ffn_all = _L0_ffn_setup()
    _L0_ffn_in = {k: v for k, v in _L0_ffn_all.items() if k in ('Wr', 'br', 'W1', 'b1', 'W2', 'b2', 'gamma', 'beta')}
    del _L0_ffn_all
    return {'x': x, 'x_txt': x_txt, 'L0_tok_W': _L0_tok_in['W'], 'L0_tok_gamma': _L0_tok_in['gamma'], 'L0_txt_weight': _L0_txt_in['weight'], 'L0_attn_W_DKV': _L0_attn_in['W_DKV'], 'L0_attn_W_UK': _L0_attn_in['W_UK'], 'L0_attn_W_UV': _L0_attn_in['W_UV'], 'L0_attn_W_UQ': _L0_attn_in['W_UQ'], 'L0_attn_W_O': _L0_attn_in['W_O'], 'L0_ffn_Wr': _L0_ffn_in['Wr'], 'L0_ffn_br': _L0_ffn_in['br'], 'L0_ffn_W1': _L0_ffn_in['W1'], 'L0_ffn_b1': _L0_ffn_in['b1'], 'L0_ffn_W2': _L0_ffn_in['W2'], 'L0_ffn_b2': _L0_ffn_in['b2'], 'L0_ffn_gamma': _L0_ffn_in['gamma'], 'L0_ffn_beta': _L0_ffn_in['beta']}

def reference(x, x_txt, L0_tok_W, L0_tok_gamma, L0_txt_weight, L0_attn_W_DKV, L0_attn_W_UK, L0_attn_W_UV, L0_attn_W_UQ, L0_attn_W_O, L0_ffn_Wr, L0_ffn_br, L0_ffn_W1, L0_ffn_b1, L0_ffn_W2, L0_ffn_b2, L0_ffn_gamma, L0_ffn_beta):
    import jax
    import jax.numpy as jnp

    def _L0_tok_ref(x, W, gamma):
        import jax, jax.numpy as jnp
        import numpy as np
        PATCH = 8
        EPS = 1e-05

        def _patchify(x):
            B, C, H, Wd = x.shape
            p = PATCH
            x = x.reshape(B, C, H // p, p, Wd // p, p)
            x = x.transpose(0, 2, 4, 1, 3, 5)
            return x.reshape(B, H // p * (Wd // p), C * p * p)
        tokens = _patchify(x)
        h = jnp.einsum('bnf,fd->bnd', tokens, W)
        mu = jnp.mean(h, axis=-1, keepdims=True)
        var = jnp.mean(jnp.square(h - mu), axis=-1, keepdims=True)
        out = (h - mu) * jax.lax.rsqrt(var + EPS) * gamma
        return out

    def _L0_txt_ref(input, weight):
        import jax, jax.numpy as jnp
        import numpy as np
        NUM_EMBEDDINGS = 32000
        EMBEDDING_DIM = 256
        EPS = 1e-05
        scale = 1.0 / jnp.maximum(jnp.mean(jnp.abs(weight)), EPS)
        quantized_weight = jnp.clip(jnp.round(weight * scale), -1.0, 1.0) / scale
        return quantized_weight[input]

    def _L0_attn_ref(x, W_DKV, W_UK, W_UV, W_UQ, W_O):
        import jax, jax.numpy as jnp
        import numpy as np
        DIM = 256
        N_HEADS = 16
        HEAD_DIM = DIM // N_HEADS
        D_LATENT = 64
        B, T = (1, 1024)
        b, t, d = x.shape
        h, hd = (N_HEADS, HEAD_DIM)
        c_kv = x @ W_DKV
        k = (c_kv @ W_UK).reshape(b, t, h, hd)
        v = (c_kv @ W_UV).reshape(b, t, h, hd)
        q = (x @ W_UQ).reshape(b, t, h, hd)
        scale = 1.0 / jnp.sqrt(jnp.asarray(hd, x.dtype))
        scores = jnp.einsum('bqhd,bkhd->bhqk', q, k) * scale
        causal = jnp.tril(jnp.ones((t, t), dtype=bool))
        scores = jnp.where(causal, scores, jnp.asarray(-jnp.inf, scores.dtype))
        probs = jax.nn.softmax(scores, axis=-1)
        ctx = jnp.einsum('bhqk,bkhd->bqhd', probs, v).reshape(b, t, d)
        return ctx @ W_O

    def _L0_ffn_ref(tgt, Wr, br, W1, b1, W2, b2, gamma, beta):
        import jax, jax.numpy as jnp
        import numpy as np
        B, S, D, F, E = (2, 512, 256, 1024, 8)
        LN_EPS = 1e-05

        def _layer_norm(x, gamma, beta):
            mu = jnp.mean(x, axis=-1, keepdims=True)
            var = jnp.mean(jnp.square(x - mu), axis=-1, keepdims=True)
            return (x - mu) * jax.lax.rsqrt(var + LN_EPS) * gamma + beta
        logits = jnp.einsum('bsd,ed->bse', tgt, Wr) + br
        top_v, top_i = jax.lax.top_k(logits, 2)
        top_w = jax.nn.softmax(top_v, axis=-1)
        n_exp = logits.shape[-1]
        router_w = jnp.sum(jax.nn.one_hot(top_i, n_exp, dtype=top_w.dtype) * top_w[..., None], axis=-2)
        h = jnp.einsum('bsd,efd->bsef', tgt, W1) + b1
        h = jax.nn.relu(h)
        o = jnp.einsum('bsef,edf->bsed', h, W2) + b2
        tgt2 = jnp.einsum('bsed,bse->bsd', o, router_w)
        return _layer_norm(tgt + tgt2, gamma, beta)
    h = _L0_tok_ref(x, L0_tok_W, L0_tok_gamma)
    h = jnp.concatenate([h, _L0_txt_ref(x_txt, L0_txt_weight)], axis=1)
    h = h + _L0_attn_ref(_layernorm(h, axis=-1), L0_attn_W_DKV, L0_attn_W_UK, L0_attn_W_UV, L0_attn_W_UQ, L0_attn_W_O)
    h = h + _L0_ffn_ref(_layernorm(h, axis=-1), L0_ffn_Wr, L0_ffn_br, L0_ffn_W1, L0_ffn_b1, L0_ffn_W2, L0_ffn_b2, L0_ffn_gamma, L0_ffn_beta)
    return h

_drawn_inputs = setup_inputs


def setup_inputs(seed=0):
    import zlib

    import numpy as np

    out = dict(_drawn_inputs(seed))
    spreads = {'L0_tok_gamma': (1.0, 0.2),
     'L0_ffn_br': (0.0, 0.615),
     'L0_ffn_b1': (0.0, 0.8),
     'L0_ffn_b2': (0.0, 0.8),
     'L0_ffn_gamma': (1.0, 0.6),
     'L0_ffn_beta': (0.0, 0.679)}
    factors = {'L0_attn_W_DKV': 8.0,
     'L0_attn_W_UK': 8.0,
     'L0_attn_W_UV': 8.0,
     'L0_attn_W_UQ': 8.0,
     'L0_attn_W_O': 8.0}
    for name, (base, spread) in spreads.items():
        noise = np.random.default_rng([zlib.crc32(name.encode()), seed]).standard_normal(out[name].shape)
        drawn = base * np.exp(spread * noise) if base else spread * noise
        out[name] = jnp.asarray(drawn.astype(out[name].dtype))
    for name, factor in factors.items():
        out[name] = (out[name] * factor).astype(out[name].dtype)
    return out
```

```python
from contextlib import ExitStack

import concourse.bass as bass
from concourse import mybir

F32 = mybir.dt.float32
BF16 = mybir.dt.bfloat16
I32 = mybir.dt.int32
ALU = mybir.AluOpType
ACT = mybir.ActivationFunctionType
AX = mybir.AxisListType

P = 128
EPS = 1e-5
NEG = -1e30


def early_fusion_kernel(nc, x_patches, text_ids, tok_w, tok_gamma, table, w_dkv, w_uk, w_uv, w_uq, w_o,
                        w_router, b_router, w1, b1, w2, b2, gamma, beta, out):
    B, FEAT, NI = x_patches.shape
    D = tok_w.shape[1]
    V = table.shape[0]
    NT = text_ids.shape[0] * text_ids.shape[1] // B
    T = NI + NT
    LAT = w_dkv.shape[1]
    HD = 16
    H = D // HD
    E, FF = w1.shape[1], w1.shape[3]
    DC, FC = D // P, FF // P
    IT = NI // P
    TILES = B * T // P
    TT = TILES - B * IT
    PB = P // NT
    TOP = 2
    NBLK = TOP * TILES + E
    KF = [(0, P), (P, P), (2 * P, FEAT - 2 * P)]
    CHUNK = V * D // P // 32
    NCH = 32
    HH = H // 2
    assert D == 256 and NI == 256 and T == 288 and H == 16 and P // HD == HH and NBLK % 2 == 0

    ctx = ExitStack()
    with ctx:
        def sb(name, shape, dt=F32):
            return ctx.enter_context(nc.sbuf_tensor(name, shape, dt))

        def sem(name):
            return ctx.enter_context(nc.semaphore(name))

        bank = [ctx.enter_context(nc.psum_tensor(f"bank{i}", [P, 512], F32)) for i in range(8)]
        b_score, b_turn, b_ctx, b_misc = bank[0:4], bank[4:6], bank[6], bank[7]

        n2_dram = nc.dram_tensor("n2_rows", [TILES * P, D], F32).ap()
        y_dram = nc.dram_tensor("expert_rows", [NBLK * P, D], F32).ap()

        region = sb("region", [P, E * DC * FF + E * FC * D])
        w1_sb = region[:, 0:E * DC * FF].rearrange("p (e k f) -> p e k f", e=E, k=DC)
        w2_sb = region[:, E * DC * FF:].rearrange("p (e c d) -> p e c d", e=E, c=FC)
        chunk = region[:, 0:4 * CHUNK].rearrange("p (s c) -> p s c", s=4)
        o = E * DC * FF
        q_all = region[:, o:o + 2 * B * T].rearrange("p (f b t) -> p f b t", f=2, b=B)
        k_all = region[:, o + 2 * B * T:o + 4 * B * T].rearrange("p (f b t) -> p f b t", f=2, b=B)
        v_all = region[:, o + 4 * B * T:o + 4 * B * T + B * 3 * D].rearrange("p (b k d) -> p b k d", b=B, k=3)

        o += 4 * B * T + B * 3 * D
        emb = region[:, o:o + TT * D].rearrange("p (t d) -> p t d", t=TT)
        hr = region[:, o + TT * D:o + TT * D + IT * D].rearrange("p (t d) -> p t d", t=IT)

        k_cur = region[:, o:o + 2 * T].rearrange("p (f t) -> p f t", f=2)

        h_all = sb("h_all", [P, TILES, D])
        scratch = sb("scratch", [P, E * FF])
        q_mask = scratch[:, 0:2 * HH * T].rearrange("p (f s t) -> p f s t", f=2, s=HH)
        o = 2 * HH * T
        probs = scratch[:, o:o + 4 * 512].rearrange("p (s c) -> p s c", s=4)
        o += 4 * 512
        v_mask = scratch[:, o:o + 3 * 2 * D].rearrange("p (k a d) -> p k a d", k=3, a=2)
        o = 4 * CHUNK
        pt_img = region[:, o:o + 2 * HH * 3 * P].rearrange("p (f h c q) -> p f h c q", f=2, h=HH, c=3)
        o += 2 * HH * 3 * P
        pt_txt = region[:, o:o + 2 * 2 * 3 * P].rearrange("p (f g c q) -> p f g c q", f=2, g=2, c=3)

        o += 2 * 2 * 3 * P
        mask_a = region[:, o:o + 256].bitcast(BF16).rearrange("p (h k) -> p h k", h=4)
        mask_b = region[:, o + 256:o + 512].bitcast(BF16).rearrange("p (h k) -> p h k", h=2)
        mask_d = region[:, o + 512:o + 512 + T // 2].bitcast(BF16)

        work = sb("work", [P, 6544])
        used = [0]

        def carve(rows, *shape):
            n = 1
            for d in shape:
                n *= d
            v = work[0:rows, used[0]:used[0] + n]
            used[0] += n
            if len(shape) == 1:
                return v
            names = "abc"[:len(shape)]
            return v.rearrange(f"p ({' '.join(names)}) -> p {' '.join(names)}", **dict(zip(names, shape)))

        ctx_t = carve(P, 2, NI)
        ctx_txt = carve(P, 2, B, NT)
        xt = carve(P, 2, 3, NI)
        wtok = carve(P, 3, D)
        wq_sb = carve(P, DC, D)
        wo_sb = carve(P, DC, D)
        wdkv_sb = carve(P, DC, LAT)
        wuk_sb = carve(LAT, D)
        wuv_sb = carve(LAT, D)
        wr_sb = carve(P, DC, E)
        n_t = carve(P, DC, NI)
        c_t = carve(LAT, NI)
        gam_tok = carve(P, D)
        n1 = carve(P, IT, D)
        br_bc = sb("br_bc", [P, E])
        stats = sb("stats", [P, IT, 6])
        mv = sb("mv", [P, IT, 2])
        vare = sb("vare", [P, IT])
        rstd = sb("rstd", [P, IT])
        neghalf = sb("neghalf", [P, IT])
        eps = sb("eps", [P, IT])
        mv2 = sb("mv2", [P, TILES, 2])
        rstd2 = sb("rstd2", [P, TILES])
        ident = sb("ident", [P, P])
        ident_bf = sb("ident_bf", [P, P], BF16)
        negm = sb("negm", [P, 4, 4])
        psums = sb("psums", [P, 4, 4])
        rsum = sb("rsum", [P, 4, 4])
        part = sb("part", [P, NCH])
        psum_abs = sb("psum_abs", [P, 1])
        scl = sb("scl", [P, 4])
        ones = sb("ones", [P, P])
        tid = sb("tid", [P, TT], I32)
        logit = sb("logit", [P, TILES, E])

        s_const, s_w, s_id = sem("s_const"), sem("s_w"), sem("s_id")
        s_chunk = [sem(f"s_chunk{i}") for i in range(4)]
        s_scan_d, s_scan_a = sem("s_scan_d"), sem("s_scan_a")
        s_xt = [sem(f"s_xt{i}") for i in range(2)]
        s_tok, s_mv, s_rstd = sem("s_tok"), sem("s_mv"), sem("s_rstd")
        s_n1, s_nt, s_nte, s_c, s_ce = sem("s_n1"), sem("s_nt"), sem("s_nte"), sem("s_c"), sem("s_ce")
        s_q, s_qe, s_k, s_ke, s_v, s_ve = (sem(f"s_{n}") for n in ("q", "qe", "k", "ke", "v", "ve"))
        s_emb, s_abs, s_scl = sem("s_emb"), sem("s_abs"), sem("s_scl")
        s_qm = [sem(f"s_qm{i}") for i in range(2)]
        s_vm, s_S, s_max, s_exp, s_rc, s_P, s_T = (sem(f"s_{n}") for n in ("vm", "S", "max", "exp", "rc", "P", "T"))
        s_te_d, s_te_a, s_pv, s_cx, s_o = (sem(f"s_{n}") for n in ("te_d", "te_a", "pv", "cx", "o"))
        s_mv2, s_rstd2, s_n2, s_n2t, s_n2te, s_lg, s_lge, s_n2st = (
            sem(f"s_{n}") for n in ("mv2", "rstd2", "n2", "n2t", "n2te", "lg", "lge", "n2st"))

        NCONST = 9 * 16
        block = ctx.enter_context(nc.Block())
        UNITS = 16
        LAG = 3

        def unit(u):
            g, kind = u // 4, "ABCD"[u % 4]
            return kind, 4 * g + (2 if kind == "C" else 0), {"A": 4, "B": 2, "C": 2, "D": 4}[kind]

        NV = TILES * E
        one_slot = work[:, 0:2304].bitcast(BF16).rearrange("p (n s) -> p n s", n=TOP * TILES)
        one_blk = work[:, 2304:2304 + TOP * TILES * NBLK].bitcast(BF16).rearrange(
            "p (n a b) -> p n a b", n=TOP * TILES, a=2)
        tmp = [work[:, 3888 + i * NV:3888 + (i + 1) * NV] for i in range(13)]
        keep = work[:, 5776:6032]
        gather_idx = keep[:, 0:NBLK].bitcast(I32)
        expert_of = keep[:, NBLK:2 * NBLK].bitcast(I32)
        pos_idx = keep[:, 2 * NBLK:2 * NBLK + TOP * TILES].bitcast(I32).rearrange("p (k t) -> p k t", k=TOP)
        o = 2 * NBLK + TOP * TILES
        top_w = keep[:, o:o + TOP * TILES].rearrange("p (k t) -> p k t", k=TOP)
        o += TOP * TILES
        gi = keep[:, o:o + 2].bitcast(I32)
        gi2 = keep[:, o + 2:o + 6].bitcast(I32).rearrange("p (s k) -> p s k", s=2)
        mvf = keep[:, o + 6:o + 10].rearrange("p (s k) -> p s k", s=2)
        rstdf = keep[:, o + 10:o + 12]
        statf = keep[:, o + 12:o + 24].rearrange("p (s k) -> p s k", s=2)
        gam, bet = work[:, 6032:6032 + D], work[:, 6288:6288 + D]
        hs = work[:, 0:FF]
        h_t = work[:, FF:2 * FF].rearrange("p (c n) -> p c n", c=FC)
        xg = work[:, 2 * FF:2 * FF + 2 * D].rearrange("p (s d) -> p s d", s=2)
        o = 2 * FF + 2 * D
        xg_t = work[:, o:o + DC * P].rearrange("p (k n) -> p k n", k=DC)
        ys = work[:, o + D:o + 3 * D].rearrange("p (s d) -> p s d", s=2)
        b2_bc = work[:, o + 3 * D:o + 3 * D + E * D].rearrange("p (e d) -> p e d", e=E)
        b1_bc = scratch[:].rearrange("p (e f) -> p e f", e=E)
        yg = work[:, 0:4 * D].rearrange("p (s k d) -> p s k d", s=2, k=TOP)
        z = work[:, 4 * D:6 * D].rearrange("p (s d) -> p s d", s=2)

        s_lw, s_b2, s_dc, s_dp, s_dl, s_de = (sem(f"s_{n}") for n in ("lw", "b2", "dc", "dp", "dl", "de"))
        s_oh, s_ip, s_idx, s_blk = (sem(f"s_{n}") for n in ("oh", "ip", "idx", "blk"))
        s_xg = [sem(f"s_xg{i}") for i in range(2)]
        s_xgt, s_xgte, s_w1, s_hs, s_t8, s_ht, s_w2, s_ys = (
            sem(f"s_{n}") for n in ("xgt", "xgte", "w1", "hs", "t8", "ht", "w2", "ys"))
        s_yst = [sem(f"s_yst{i}") for i in range(2)]
        s_g = [sem(f"s_g{i}") for i in range(2)]
        s_ost = [sem(f"s_ost{i}") for i in range(2)]
        s_z, s_mvf, s_rf, s_zg, s_zo = (sem(f"s_{n}") for n in ("z", "mvf", "rf", "zg", "zo"))
        pref_ps, tot_ps, idx_ps = b_ctx[:, 0:NV], b_ctx[:, NV:2 * NV], b_misc[:, 0:2 * NBLK]
        hid, turned, y_ps, xt_ps = bank[0:2], bank[2:4], bank[4], bank[5]

        def tail_sp(sp):
            sp.wait_ge(s_pv, 2 * B)
            sp.wait_ge(s_cx, 2 * B)
            for e in range(E):
                sp.dma_start(w1_sb[:, e], w1[:, e]).then_inc(s_lw, 16)
                sp.dma_start(w2_sb[:, e], w2[:, e]).then_inc(s_lw, 16)
            sp.dma_start(b1_bc, b1.broadcast_to([P, E * FF])).then_inc(s_lw, 16)
            sp.wait_ge(s_idx, 1)
            sp.wait_ge(s_n2st, 16 * (B + 1))
            sp.dma_start(b2_bc, b2.broadcast_to([P, E * D])).then_inc(s_b2, 16)
            sp.dma_start(gam, gamma.broadcast_to([P, D])).then_inc(s_b2, 16)
            sp.dma_start(bet, beta.broadcast_to([P, D])).then_inc(s_b2, 16)
            with sp.Fori(0, NBLK // 2) as i:
                for par in range(2):
                    n = i * 2 + par
                    sp.wait_ge(s_ys, n + 1)
                    sp.dma_start(y_dram[bass.ds(n * P, P), :], ys[:, par, :]).then_inc(s_yst[par], 16)
            with sp.Fori(0, B) as i:
                for par in range(2):
                    sp.wait_ge(s_zo, 2 * i + par + 1)
                    sp.dma_start(out[i, par * P:par * P + P, :], z[:, par, :]).then_inc(s_ost[par], 16)
            for par in range(2):
                sp.wait_ge(s_zo, 2 * B + par + 1)
                for j in range(PB):
                    sp.dma_start(out[par * PB + j, NI:T, :], z[NT * j:NT * j + NT, par, :]).then_inc(s_ost[par], 16)
            for par in range(2):
                sp.wait_ge(s_ost[par], 16 * (B + PB))

        def tail_pool(pool):
            pool.wait_ge(s_lge, B + 1)
            io_i = tmp[0][:, 0:P].bitcast(I32)
            nc.gpsimd.iota(io_i, [[1, P]], base=0, channel_multiplier=0)
            nc.gpsimd.iota(tmp[1][:, 0:1].bitcast(I32), [[0, 1]], base=0, channel_multiplier=1)
            nc.gpsimd.memset(tmp[3], 1.0)
            pool.drain()
            nc.gpsimd.tensor_copy(tmp[2][:, 0:P], io_i)
            nc.gpsimd.tensor_copy(tmp[1][:, 1:2], tmp[1][:, 0:1].bitcast(I32))
            nc.gpsimd.affine_select(tmp[4][:, 0:P], ones[:], [[1, P]], ALU.is_ge, 0.0, base=-1, channel_multiplier=-1)
            nc.gpsimd.memset(tmp[3].rearrange("p (e t) -> p e t", e=E)[:, :, 0:1], 0.0)
            pool.drain()
            nc.gpsimd.tensor_scalar(tmp[5][:, 0:E], tmp[2][:, 0:E], -1.0, float(E), ALU.mult, ALU.add)
            nc.gpsimd.tensor_scalar(tmp[5][:, E:E + TILES], tmp[2][:, 0:TILES], float(P), None, ALU.mult
                                    ).then_inc(s_dc, 1)

            def gather(n, par, first):
                if not first:
                    pool.wait_ge(s_xgt, n - 1)
                nc.gpsimd.tensor_copy(gi[:, par:par + 1], gather_idx[:, bass.ds(n, 1)])
                pool.drain()
                nc.gpsimd.indirect_dma_start(xg[:, par, :], None, n2_dram,
                                             bass.IndirectOffsetOnAxis(gi[:, par:par + 1], 0)).then_inc(s_xg[par], 16)

            pool.wait_ge(s_idx, 1)
            pool.wait_ge(s_n2st, 16 * (B + 1))
            gather(0, 0, True)
            gather(1, 1, True)
            with pool.Fori(1, NBLK // 2) as i:
                gather(i * 2, 0, False)
                gather(i * 2 + 1, 1, False)

            def final_gather(t, par, first):
                if not first:
                    pool.wait_ge(s_z, t - 1)
                nc.gpsimd.tensor_copy(gi2[:, par, :], pos_idx[:, :, t])
                pool.drain()
                for k in range(TOP):
                    nc.gpsimd.indirect_dma_start(yg[:, par, k, :], None, y_dram,
                                                 bass.IndirectOffsetOnAxis(gi2[:, par, k:k + 1], 0)
                                                 ).then_inc(s_g[par], 16)

            def final_norm(i, last):
                for par in range(2):
                    t = i * 2 + par
                    pool.wait_ge(s_mvf, t + 1)
                    nc.gpsimd.tensor_tensor(vare[:, par:par + 1], mvf[:, par, 1:2], eps[:, 0:1], ALU.add)
                    pool.drain()
                    nc.gpsimd.tensor_tensor(rstdf[:, par:par + 1], vare[:, par:par + 1], neghalf[:, 0:1], ALU.pow
                                            ).then_inc(s_rf, 1)
                    if not last:
                        final_gather(t + 2, par, False)
                for par in range(2):
                    t = i * 2 + par
                    pool.wait_ge(s_zg, t + 1)
                    nc.gpsimd.tensor_tensor(z[:, par, :], z[:, par, :], bet, ALU.add)
                    pool.drain()
                    nc.gpsimd.tensor_tensor(z[:, par, :], z[:, par, :], h_all[:, t, :], ALU.add).then_inc(s_zo, 1)

            for par in range(2):
                pool.wait_ge(s_yst[par], 16 * (NBLK // 2))
            pool.wait_ge(s_b2, 48)
            final_gather(0, 0, True)
            final_gather(1, 1, True)
            with pool.Fori(0, TILES // 2 - 1) as i:
                final_norm(i, False)
            final_norm(TILES // 2 - 1, True)

        def tail_act(act):
            act.wait_ge(s_dl, 1)
            nc.scalar.activation(tmp[7][:, TILES:2 * TILES], tmp[7][:, 0:TILES], ACT.Exp).then_inc(s_de, 1)

            def rows_t(n, first):
                act.wait_ge(s_xgt, n + 1)
                if not first:
                    act.wait_ge(s_w1, n)
                nc.scalar.activation(xg_t.rearrange("p k n -> p (k n)"), xt_ps[:, 0:DC * P], ACT.Copy
                                     ).then_inc(s_xgte, 1)

            def hidden_t(n, first):
                act.wait_ge(s_t8, n + 1)
                if not first:
                    act.wait_ge(s_w2, n)
                for i in range(2):
                    last = nc.scalar.activation(h_t[:, 4 * i:4 * i + 4, :].rearrange("p c n -> p (c n)"),
                                                turned[i][:], ACT.Relu)
                last.then_inc(s_ht, 1)

            act.wait_ge(s_idx, 1)
            rows_t(0, True)
            rows_t(1, False)
            hidden_t(0, True)
            with act.Fori(1, NBLK - 1) as n:
                rows_t(n + 1, False)
                hidden_t(n, False)
            hidden_t(NBLK - 1, False)

        def tail_dve(dve):
            A = "p (t e) -> p t e"
            iota, e8, thr = tmp[2][:, 0:P], tmp[5][:, 0:E], tmp[5][:, E:E + TILES]
            pcol, notfirst = tmp[1][:, 1:2], tmp[3]
            ones_p = (tmp[6], tmp[8])
            cut = tmp[9]
            m = tmp[7]
            small = tmp[10]
            row8 = e8[:, None, :].broadcast_to([P, TILES, E])
            dve.wait_ge(s_dc, 1)
            dve.drain()

            def pick(src, value, onehot):
                nc.vector.tensor_reduce(value, src, AX.X, ALU.max)
                dve.drain()
                nc.vector.tensor_tensor(onehot, src, value[:, :, None].broadcast_to([P, TILES, E]), ALU.is_ge)
                dve.drain()
                nc.vector.tensor_tensor(onehot, onehot, row8, ALU.mult)
                dve.drain()
                nc.vector.tensor_reduce(small[:, 0:TILES], onehot, AX.X, ALU.max)
                dve.drain()
                nc.vector.tensor_tensor(onehot, row8, small[:, 0:TILES, None].broadcast_to([P, TILES, E]),
                                        ALU.is_equal)
                dve.drain()

            o1, o2_ = (t.rearrange(A, t=TILES) for t in ones_p)
            pick(logit[:], small[:, 36:36 + TILES], o1)
            nc.vector.scalar_tensor_tensor(cut, ones_p[0], -3e38, logit[:].rearrange("p t e -> p (t e)"),
                                           ALU.mult, ALU.add)
            dve.drain()
            pick(cut.rearrange(A, t=TILES), small[:, 72:72 + TILES], o2_)
            nc.vector.tensor_tensor(cut, ones_p[0], ones_p[1], ALU.add).then_inc(s_oh, 1)
            nc.vector.tensor_tensor(m[:, 0:TILES], small[:, 72:72 + TILES], small[:, 36:36 + TILES], ALU.subtract
                                    ).then_inc(s_dl, 1)
            dve.wait_ge(s_de, 1)
            nc.vector.tensor_scalar(m[:, 36:36 + TILES], m[:, TILES:2 * TILES], 1.0, None, ALU.add)
            dve.drain()
            nc.vector.reciprocal(top_w[:, 0, :], m[:, 36:36 + TILES])
            dve.drain()
            nc.vector.tensor_tensor(top_w[:, 1, :], m[:, TILES:2 * TILES], top_w[:, 0, :], ALU.mult)
            dve.wait_ge(s_dp, 1)
            tot, incl, cnt = tmp[11], tmp[12], tmp[10][:, 0:E]
            nc.vector.tensor_copy(tot.rearrange("p (e t) -> p t e", e=E), tot_ps.rearrange(A, t=TILES))
            dve.drain()
            nc.vector.tensor_tensor_scan(incl, notfirst, tot, 0.0, ALU.mult, ALU.add)
            dve.drain()
            nc.vector.tensor_tensor(tot, incl, tot, ALU.subtract)
            nc.vector.tensor_copy(cnt, incl.rearrange("p (e t) -> p e t", e=E)[:, :, TILES - 1])
            dve.drain()
            nc.vector.tensor_tensor(cut.rearrange("p (e t) -> p e t", e=E), cnt[:, :, None].broadcast_to([P, E, TILES]),
                                    thr[:, None, :].broadcast_to([P, E, TILES]), ALU.is_gt)
            dve.drain()
            nb, ends, base = small[:, E:2 * E], small[:, 2 * E:3 * E], small[:, 3 * E:4 * E]
            nc.vector.tensor_reduce(nb, cut.rearrange("p (e t) -> p e t", e=E), AX.X, ALU.add)
            dve.drain()
            nc.vector.tensor_tensor_scan(ends, ones[:, 0:E], nb, 0.0, ALU.mult, ALU.add)
            dve.drain()
            nc.vector.tensor_tensor(base, ends, nb, ALU.subtract)
            dve.drain()
            nc.vector.scalar_tensor_tensor(tot.rearrange("p (e t) -> p e t", e=E),
                                           base[:, :, None].broadcast_to([P, E, TILES]), float(P),
                                           tot.rearrange("p (e t) -> p e t", e=E), ALU.mult, ALU.add)
            dve.drain()
            nc.vector.tensor_tensor(cut.rearrange(A, t=TILES), pref_ps.rearrange(A, t=TILES),
                                    tot.rearrange("p (e t) -> p t e", e=E), ALU.add)
            dve.drain()
            for k in range(TOP):
                nc.vector.tensor_tensor(ones_p[k], ones_p[k], cut, ALU.mult)
            dve.drain()
            for k in range(TOP):
                nc.vector.tensor_reduce(m[:, k * TILES:(k + 1) * TILES], (o1, o2_)[k], AX.X, ALU.add)
            dve.drain()
            flat = pos_idx.rearrange("p k t -> p (k t)")
            nc.vector.tensor_copy(flat, m[:, 0:TOP * TILES])
            dve.drain()
            ti = tmp[12].bitcast(I32)
            nc.vector.tensor_scalar(ti[:, 0:36], flat, P - 1, None, ALU.bitwise_and)
            nc.vector.tensor_scalar(ti[:, 36:72], flat, 7, None, ALU.logical_shift_right)
            dve.drain()
            nc.vector.tensor_copy(m[:, 0:72], ti[:, 0:72])
            dve.drain()
            N = TOP * TILES
            nc.vector.tensor_tensor(one_slot, iota[:, None, :].broadcast_to([P, N, P]),
                                    m[:, 0:N, None].broadcast_to([P, N, P]), ALU.is_equal)
            nc.vector.tensor_tensor(one_blk[:, :, 0, :], iota[:, None, 0:NBLK].broadcast_to([P, N, NBLK]),
                                    m[:, N:2 * N, None].broadcast_to([P, N, NBLK]), ALU.is_equal)
            dve.drain()
            nc.vector.tensor_scalar(one_blk[:, :, 1, :], one_blk[:, :, 0, :], pcol, None, ALU.mult)
            dve.drain()
            for k in range(TOP):
                last = nc.vector.tensor_tensor(one_blk[:, k * TILES:(k + 1) * TILES, 0, :],
                                               one_blk[:, k * TILES:(k + 1) * TILES, 0, :],
                                               iota[:, 0:TILES, None].broadcast_to([P, TILES, NBLK]), ALU.mult)
            last.then_inc(s_ip, 1)
            for b0, bn, dst in ((0, TILES, 0), (TILES, TILES, TILES), (2 * TILES, NBLK - 2 * TILES, 2 * TILES)):
                nc.vector.tensor_tensor(cut[:, 0:bn * E].rearrange("p (b e) -> p b e", e=E),
                                        iota[:, b0:b0 + bn, None].broadcast_to([P, bn, E]),
                                        ends[:, None, :].broadcast_to([P, bn, E]), ALU.is_ge)
                dve.drain()
                nc.vector.tensor_reduce(small[:, 40 + b0:40 + b0 + bn],
                                        cut[:, 0:bn * E].rearrange("p (b e) -> p b e", e=E), AX.X, ALU.add)
                dve.drain()
            nc.vector.tensor_scalar(expert_of, small[:, 40:40 + NBLK], float(E - 1), None, ALU.min).then_inc(s_blk, 1)
            dve.wait_ge(s_ip, 2)
            nc.vector.tensor_copy(m[:, 0:2 * NBLK], idx_ps)
            dve.drain()
            nc.vector.scalar_tensor_tensor(gather_idx, m[:, 0:NBLK], float(P), m[:, NBLK:2 * NBLK],
                                           ALU.mult, ALU.add).then_inc(s_idx, 1)

            def hidden(n):
                e = dve.value_load(expert_of[0:1, bass.ds(n, 1)], min_val=0, max_val=E - 1)
                dve.wait_ge(s_w1, n + 1)
                for i in range(2):
                    last = nc.vector.tensor_tensor(hs[:, 512 * i:512 * i + 512], hid[i][:],
                                                   b1_bc[:, e, 512 * i:512 * i + 512], ALU.add)
                last.then_inc(s_hs, 1)

            def rows_out(n, par, first):
                e = dve.value_load(expert_of[0:1, bass.ds(n, 1)], min_val=0, max_val=E - 1)
                dve.wait_ge(s_w2, n + 1)
                if not first:
                    dve.wait_ge(s_yst[par], n // 2 * 16 if isinstance(n, int) else (n - par) * 8)
                nc.vector.tensor_tensor(ys[:, par, :], y_ps[:, 0:D], b2_bc[:, e, :], ALU.add).then_inc(s_ys, 1)

            dve.wait_ge(s_blk, 1)
            dve.wait_ge(s_lw, 16 * (2 * E + 1))
            dve.wait_ge(s_b2, 48)
            hidden(0)
            hidden(1)
            rows_out(0, 0, True)
            hidden(2)
            rows_out(1, 1, True)
            with dve.Fori(1, NBLK // 2 - 1) as i:
                for par in range(2):
                    n = i * 2 + par
                    hidden(n + 1)
                    rows_out(n, par, False)
            hidden(NBLK - 1)
            rows_out(NBLK - 2, 0, False)
            rows_out(NBLK - 1, 1, False)

            def final(i, first):
                for par in range(2):
                    t = i * 2 + par
                    if not first:
                        dve.wait_ge(s_ost[par], i * 16)
                    nc.vector.tensor_scalar(z[:, par, :], h_all[:, t, :], mv2[:, t, 0:1], rstd2[:, bass.ds(t, 1)],
                                            ALU.subtract, ALU.mult)
                dve.drain()
                for k in range(TOP):
                    for par in range(2):
                        t = i * 2 + par
                        dve.wait_ge(s_g[par], (i + 1) * (16 * TOP))
                        last = nc.vector.scalar_tensor_tensor(z[:, par, :], yg[:, par, k, :],
                                                              top_w[:, k, bass.ds(t, 1)], z[:, par, :],
                                                              ALU.mult, ALU.add)
                        if k == TOP - 1:
                            last.then_inc(s_z, 1)
                    dve.drain()
                for par in range(2):
                    nc.vector.bn_stats(statf[:, par, :], z[:, par, :])
                dve.drain()
                for par in range(2):
                    nc.vector.bn_aggr(mvf[:, par, :], statf[:, par, :]).then_inc(s_mvf, 1)
                for par in range(2):
                    dve.wait_ge(s_rf, i * 2 + par + 1)
                    nc.vector.tensor_scalar(z[:, par, :], z[:, par, :], mvf[:, par, 0:1], rstdf[:, par:par + 1],
                                            ALU.subtract, ALU.mult)
                dve.drain()
                for par in range(2):
                    nc.vector.tensor_tensor(z[:, par, :], z[:, par, :], gam, ALU.mult).then_inc(s_zg, 1)

            for par in range(2):
                dve.wait_ge(s_yst[par], 16 * (NBLK // 2))
            final(0, True)
            with dve.Fori(1, TILES // 2) as i:
                final(i, False)

        def tail_pe(pe):
            pe.wait_ge(s_oh, 1)
            nc.tensor.matmul(pref_ps, tmp[4][:, 0:P], tmp[9], start=True, stop=True)
            nc.tensor.matmul(tot_ps, ones[:], tmp[9], start=True, stop=True).then_inc(s_dp, 1)
            pe.wait_ge(s_ip, 1)
            N = TOP * TILES
            for n in range(N):
                last = nc.tensor.matmul(idx_ps, one_slot[:, n, :], one_blk[:, n, :, :], start=(n == 0), stop=(n == N - 1))
            last.then_inc(s_ip, 1)

            def rows_t(n, par):
                pe.wait_ge(s_xg[par], n // 2 * 16 + 16 if isinstance(n, int) else (n - par) * 8 + 16)
                for k in range(DC):
                    last = nc.tensor.transpose(xt_ps[:, k * P:k * P + P], xg[:, par, k * P:k * P + P], ident[:])
                last.then_inc(s_xgt, 1)

            def load_e(n):
                return pe.value_load(expert_of[0:1, bass.ds(n, 1)], min_val=0, max_val=E - 1)

            def up(n, first):
                e = load_e(n)
                pe.wait_ge(s_xgte, n + 1)
                if not first:
                    pe.wait_ge(s_hs, n)
                for i in range(2):
                    for k in range(DC):
                        last = nc.tensor.matmul(hid[i][:], xg_t[:, k, :], w1_sb[:, e, k, 512 * i:512 * i + 512],
                                                start=(k == 0), stop=(k == DC - 1))
                last.then_inc(s_w1, 1)

            def down(n, first):
                e = load_e(n)
                pe.wait_ge(s_ht, n + 1)
                if not first:
                    pe.wait_ge(s_ys, n)
                for c in range(FC):
                    last = nc.tensor.matmul(y_ps[:, 0:D], h_t[:, c, :], w2_sb[:, e, c, :], start=(c == 0),
                                            stop=(c == FC - 1))
                last.then_inc(s_w2, 1)

            def hidden_turn(n):
                pe.wait_ge(s_hs, n + 1)
                for c in range(FC):
                    last = nc.tensor.transpose(turned[c // 4][:, c % 4 * P:c % 4 * P + P], hs[:, c * P:c * P + P],
                                               ident[:])
                last.then_inc(s_t8, 1)

            pe.wait_ge(s_blk, 1)
            pe.wait_ge(s_lw, 16 * (2 * E + 1))
            rows_t(0, 0)
            up(0, True)
            rows_t(1, 1)
            hidden_turn(0)
            up(1, False)
            rows_t(2, 0)
            down(0, True)
            hidden_turn(1)
            with pe.Fori(1, NBLK // 2 - 1) as i:
                for par in range(2):
                    n = i * 2 + par
                    up(n, False)
                    rows_t(n + 1, 1 - par)
                    down(n - 1, False)
                    hidden_turn(n)
            n = NBLK - 2
            up(n, False)
            rows_t(n + 1, 1)
            down(n - 1, False)
            hidden_turn(n)
            up(n + 1, False)
            down(n, False)
            hidden_turn(n + 1)
            down(n + 1, False)

        @block.sync
        def _(sp):
            for kc, (f0, fn) in enumerate(KF):
                sp.dma_start(wtok[0:fn, kc, :], tok_w[f0:f0 + fn, :]).then_inc(s_w, 16)
            sp.dma_start(gam_tok[:], tok_gamma.broadcast_to([P, D])).then_inc(s_const, 16)

            def load_x(b, par):
                sp.dma_start(xt[:, par, 0:2, :], x_patches[b, 0:2 * P, :].rearrange("(k p) n -> p k n", p=P)
                             ).then_inc(s_xt[par], 16)
                sp.dma_start(xt[0:KF[2][1], par, 2, :], x_patches[b, 2 * P:FEAT, :]).then_inc(s_xt[par], 16)

            load_x(0, 0)
            sp.dma_start(wq_sb[:], w_uq.rearrange("(k p) n -> p k n", p=P)).then_inc(s_const, 16)
            sp.dma_start(wdkv_sb[:], w_dkv.rearrange("(k p) n -> p k n", p=P)).then_inc(s_const, 16)
            sp.dma_start(wuk_sb[:], w_uk).then_inc(s_const, 16)
            sp.dma_start(wuv_sb[:], w_uv).then_inc(s_const, 16)
            sp.dma_start(wo_sb[:], w_o.rearrange("(k p) n -> p k n", p=P)).then_inc(s_const, 16)
            sp.dma_start(wr_sb[:], w_router).then_inc(s_const, 16)
            sp.dma_start(br_bc[:], b_router.broadcast_to([P, E])).then_inc(s_const, 16)
            sp.dma_start(tid[:], text_ids).then_inc(s_const, 16)
            load_x(1, 1)

            table_c = table.rearrange("(c r) d -> c (r d)", c=NCH).rearrange("c (p x) -> c p x", p=P)

            def load_chunks(b, first):
                for s in range(4):
                    if not first:
                        sp.wait_ge(s_scan_d if s < 2 else s_scan_a, 2 * (b - 1) + s % 2 + 1)
                    sp.dma_start(chunk[:, s, :], table_c[b * 4 + s]).then_inc(s_chunk[s], 16)

            load_chunks(0, True)
            load_chunks(1, False)
            with sp.Fori(1, B // 2) as i:
                for par in range(2):
                    b = i * 2 + par
                    sp.wait_ge(s_tok, b - 1)
                    load_x(b, par)
                    load_chunks(b, False)

            def fill_q(b, first):
                for hf in range(2):
                    if not first:
                        sp.wait_ge(s_S, (b - 1) * UNITS + 8 * hf + 8)
                    for s in range(HH):
                        r = slice(HD * s, HD * s + HD)
                        sp.dma_start(q_mask[r, hf, s, :], q_all[r, hf, b, :]).then_inc(s_qm[hf], 16)
                    sp.dma_start(k_cur[:, hf, :], k_all[:, hf, b, :]).then_inc(s_qm[hf], 16)

            def store_n2(b):
                sp.wait_ge(s_n2, b + 1)
                sp.dma_start(n2_dram[bass.ds(b * (IT * P), IT * P), :].rearrange("(i p) d -> p i d", p=P),
                             n1[:]).then_inc(s_n2st, 16)

            sp.wait_ge(s_qe, B + 1)
            sp.wait_ge(s_ke, B + 1)
            sp.wait_ge(s_id, 1)
            fill_q(0, True)
            with sp.Fori(1, B) as b:
                fill_q(b, False)
                store_n2(b - 1)
            store_n2(B - 1)
            store_n2(B)
            tail_sp(sp)

        @block.gpsimd
        def _(pool):
            nc.gpsimd.memset(neghalf[:], -0.5)
            nc.gpsimd.memset(eps[:], EPS)
            nc.gpsimd.memset(ones[:], 1.0)
            nc.gpsimd.memset(v_mask, 0.0)
            nc.gpsimd.memset(q_mask, 0.0)
            nc.gpsimd.memset(ident[:], 0.0)
            nc.gpsimd.memset(mask_a[:], 0.0)
            nc.gpsimd.memset(mask_b[:], 0.0)
            nc.gpsimd.memset(mask_d[:], 0.0)
            pool.drain()
            nc.gpsimd.affine_select(ident[:], ident[:], [[-1, P]], ALU.not_equal, 1.0, base=0, channel_multiplier=1)
            nc.gpsimd.affine_select(mask_a[:], mask_a[:], [[0, 4], [-1, P]], ALU.is_ge, NEG, base=0,
                                    channel_multiplier=1)
            nc.gpsimd.affine_select(mask_b[:], mask_b[:], [[0, 2], [-1, 2 * P]], ALU.is_ge, NEG, base=P,
                                    channel_multiplier=1)
            for j in range(4):
                r = slice(NT * j, NT * j + NT)
                pool.drain()
                nc.gpsimd.affine_select(mask_d[r, :], mask_d[r, :], [[-1, T]], ALU.is_ge, NEG, base=NI,
                                        channel_multiplier=1)
            pool.drain()
            nc.gpsimd.tensor_copy(ident_bf[:], ident[:]).then_inc(s_id, 1)

            def inv_std(var, res, n):
                nc.gpsimd.tensor_tensor(vare[:, 0:n], var, eps[:, 0:n], ALU.add)
                pool.drain()
                return nc.gpsimd.tensor_tensor(res, vare[:, 0:n], neghalf[:, 0:n], ALU.pow)

            def front(b):
                for n in range(2):
                    pool.wait_ge(s_mv, 2 * b + n + 1)
                    inv_std(mv[:, :, 1], rstd[:], IT).then_inc(s_rstd, 1)

            with pool.Fori(0, B) as b:
                front(b)
            pool.wait_ge(s_const, NCONST)
            for j in range(TT):
                nc.gpsimd.indirect_dma_start(emb[:, j, :], None, table, bass.IndirectOffsetOnAxis(tid[:, j:j + 1], 0)
                                             ).then_inc(s_emb, 16)
            pool.wait_ge(s_mv, 2 * B + 1)
            inv_std(mv[:, :, 1], rstd[:], IT).then_inc(s_rstd, 1)

            def fill_v(b, hf, first):
                if not first:
                    pool.wait_ge(s_pv, 2 * (b - 1) + hf + 1)
                for par in range(2):
                    for rows, kt in ((slice(0, P), slice(0, 2)), (slice(0, NT), slice(2, 3))):
                        last = nc.gpsimd.tensor_copy(
                            v_mask[rows, kt, par, hf * P:hf * P + P].rearrange("p k (j z) -> p k j z", z=32)[
                                :, :, :, HD * par:HD * par + HD],
                            v_all[rows, b, kt, hf * P:hf * P + P].rearrange("p k (j z) -> p k j z", z=32)[
                                :, :, :, HD * par:HD * par + HD])
                last.then_inc(s_vm, 1)

            def body(b, cur, prev):
                if cur:
                    fill_v(b, 0, not prev)
                for u in range(UNITS):
                    if cur:
                        kind, h0, n = unit(u)
                        w = {"A": P, "B": 2 * P, "C": 2 * P, "D": T}[kind]
                        pool.wait_ge(s_rc, b * UNITS + u + 1)
                        m = 1 if kind == "D" else n
                        p = probs[:, u % 4, 0:m * w].rearrange("p (h k) -> p h k", h=m)
                        nc.gpsimd.tensor_tensor(p, p, rsum[:, u % 4, 0:m, None].broadcast_to([P, m, w]), ALU.mult
                                                ).then_inc(s_P, 1)
                        if u == 5:
                            fill_v(b, 1, not prev)
                    if u == 8 and prev:
                        pool.wait_ge(s_mv2, b)
                        inv_std(mv[:, :, 1], rstd[:], IT).then_inc(s_rstd2, 1)

            pool.wait_ge(s_ve, B + 1)
            body(0, True, False)
            with pool.Fori(1, B) as b:
                body(b, True, True)
            body(B, False, True)
            pool.wait_ge(s_mv2, B + 1)
            inv_std(mv[:, :, 1], rstd[:], TT).then_inc(s_rstd2, 1)
            tail_pool(pool)

        @block.scalar
        def _(act):
            def scan(b):
                for s in (2, 3):
                    act.wait_ge(s_chunk[s], 16 * (b + 1))
                    nc.scalar.activation(chunk[:, s, :], chunk[:, s, :], ACT.Abs,
                                         accum_out=part[:, bass.ds(b * 4 + s, 1)]).then_inc(s_scan_a, 1)

            def evacuate(b):
                act.wait_ge(s_nt, b + 1)
                nc.scalar.activation(n_t[:].rearrange("p k n -> p (k n)"), b_turn[0][:], ACT.Copy).then_inc(s_nte, 1)
                act.wait_ge(s_c, b + 1)
                nc.scalar.activation(c_t[:], b_ctx[0:LAT, 0:NI], ACT.Copy).then_inc(s_ce, 1)
                act.wait_ge(s_q, b + 1)

            SC = float(HD) ** -0.5
            with act.Fori(0, B // 2) as i:
                for par in range(2):
                    b = i * 2 + par
                    scan(b)
                    evacuate(b)
                    nc.scalar.activation(q_all[:, :, b, 0:NI], b_score[0][:].rearrange("p (f n) -> p f n", f=2),
                                         ACT.Copy, scale=SC).then_inc(s_qe, 1)
            evacuate(B)
            nc.scalar.activation(q_all[:, :, :, NI:T], b_score[0][:].rearrange("p (f b n) -> p f b n", f=2, b=B),
                                 ACT.Copy, scale=SC).then_inc(s_qe, 1)

            def body(b, cur, prev):
                for u in range(UNITS):
                    kind, h0, n = unit(u)
                    if cur:
                        act.wait_ge(s_max, b * UNITS + u + 1)
                        if prev or u >= 4:
                            act.wait_ge(s_T, b * UNITS + u - 3)
                        w = {"A": P, "B": 2 * P, "C": 2 * P, "D": T}[kind]
                        for k in range(1 if kind == "D" else n):
                            last = nc.scalar.activation(probs[:, u % 4, k * w:k * w + w],
                                                        b_score[u % 4][:, k * w:k * w + w], ACT.Exp,
                                                        bias=negm[:, u % 4, k:k + 1],
                                                        accum_out=psums[:, u % 4, k:k + 1])
                        last.then_inc(s_exp, 1)
                    evac_turn(b, u, cur, prev)
                    if u == 4 and prev:
                        evac_ctx(b - 1, 1)
                    if u == 12 and cur:
                        evac_ctx(b, 0)
                    if u == 12 and prev:
                        act.wait_ge(s_n2t, b)
                        nc.scalar.activation(n_t[:].rearrange("p k n -> p (k n)"), b_misc[:], ACT.Copy
                                             ).then_inc(s_n2te, 1)

            def evac_turn(b, u, cur, prev):
                v = u - 4
                if v % 2 == 0 or not (cur if v >= 0 else prev):
                    return
                bb = b if v >= 0 else b - 1
                v = v % UNITS
                hf = v // 8
                act.wait_ge(s_T, bb * UNITS + v + 1)
                if cur_b_not_first(b, u, prev):
                    act.wait_ge(s_pv, 2 * (bb - 1) + hf + 1)
                kind, h0, n = unit(v)
                if kind == "B":
                    nc.scalar.activation(pt_img[:, hf, h0 % HH:h0 % HH + 2, 1:3, :],
                                         b_turn[1][:].rearrange("p (h c q) -> p h c q", h=2, c=2),
                                         ACT.Copy).then_inc(s_te_a, 1)
                else:
                    g = h0 // 4 % 2
                    nc.scalar.activation(pt_txt[:, hf, g, 0:2, :], b_turn[1][:, 0:2 * P].rearrange(
                        "p (c q) -> p c q", c=2), ACT.Copy)
                    nc.scalar.activation(pt_txt[0:NT, hf, g, 2, :], b_turn[1][0:NT, 2 * P:3 * P], ACT.Copy
                                         ).then_inc(s_te_a, 1)

            def cur_b_not_first(b, u, prev):
                if u >= 4:
                    return prev
                return not (isinstance(b, int) and b == 1)

            def evac_ctx(b, hf):
                act.wait_ge(s_pv, 2 * b + hf + 1)
                if not (isinstance(b, int) and b == 0):
                    act.wait_ge(s_o, b)
                nc.scalar.activation(ctx_t[:, hf, :], b_ctx[:, 0:NI], ACT.Copy)
                nc.scalar.activation(ctx_txt[:, hf, b, :], b_ctx[:, NI:T], ACT.Copy).then_inc(s_cx, 1)

            body(0, True, False)
            body(1, True, True)
            with act.Fori(2, B) as b:
                body(b, True, True)
            body(B, False, True)
            act.wait_ge(s_n2t, B + 1)
            nc.scalar.activation(n_t[:].rearrange("p k n -> p (k n)"), b_misc[:], ACT.Copy).then_inc(s_n2te, 1)
            tail_act(act)

        @block.vector
        def _(dve):
            def scan(b, s):
                dve.wait_ge(s_chunk[s], 16 * (b + 1))
                nc.vector.tensor_reduce(part[:, bass.ds(b * 4 + s, 1)], chunk[:, s, :], AX.X, ALU.add,
                                        apply_absolute_value=True).then_inc(s_scan_d, 1)

            def norm_stats(src, into):
                for i in range(IT):
                    nc.vector.bn_stats(stats[:, i, :], src[i])
                dve.drain()
                for i in range(IT):
                    last = nc.vector.bn_aggr(into[:, i, :], stats[:, i, :])
                return last

            def second_norm(b, t0, first_count):
                norm_stats([h_all[:, t0 + i, :] for i in range(IT)], mv).then_inc(s_mv, 1)
                dve.wait_ge(s_rstd, first_count)
                for i in range(IT):
                    last = nc.vector.tensor_scalar(n1[:, i, :], h_all[:, t0 + i, :], mv[:, i, 0:1],
                                                   rstd[:, i:i + 1], ALU.subtract, ALU.mult)
                last.then_inc(s_n1, 1)

            dve.wait_ge(s_const, NCONST)
            with dve.Fori(0, B) as b:
                scan(b, 0)
                dve.wait_ge(s_tok, b + 1)
                norm_stats([b_misc[:, i * D:i * D + D] for i in range(IT)], mv).then_inc(s_mv, 1)
                dve.wait_ge(s_rstd, 2 * b + 1)
                for i in range(IT):
                    nc.vector.tensor_scalar(hr[:, i, :], b_misc[:, i * D:i * D + D], mv[:, i, 0:1],
                                            rstd[:, i:i + 1], ALU.subtract, ALU.mult)
                dve.drain()
                for i in range(IT):
                    nc.vector.tensor_tensor(h_all[:, b * IT + i, :], hr[:, i, :], gam_tok[:], ALU.mult)
                dve.drain()
                second_norm(b, b * IT, 2 * b + 2)
                scan(b, 1)
                dve.wait_ge(s_k, b + 1)
                nc.vector.tensor_copy(k_all[:, :, b, 0:NI], b_score[1][:].rearrange("p (f n) -> p f n", f=2)
                                      ).then_inc(s_ke, 1)
                dve.wait_ge(s_v, b + 1)
                nc.vector.tensor_copy(v_all[:, b, 0:2, :], b_score[2][:].rearrange("p (k d) -> p k d", k=2)
                                      ).then_inc(s_ve, 1)

            dve.wait_ge(s_scan_a, 2 * B)
            dve.drain()
            nc.vector.tensor_reduce(psum_abs[:], part[:], AX.X, ALU.add).then_inc(s_abs, 1)
            dve.wait_ge(s_scl, 1)
            nc.vector.tensor_scalar(scl[:, 0:1], b_misc[:, 0:1], 1.0 / (V * D), EPS, ALU.mult, ALU.max)
            dve.drain()
            nc.vector.reciprocal(scl[:, 1:2], scl[:, 0:1])
            dve.drain()
            nc.vector.reciprocal(scl[:, 2:3], scl[:, 1:2])
            dve.wait_ge(s_emb, 16 * TT)
            dve.drain()
            nc.vector.tensor_scalar(hr[:], emb[:], scl[:, 1:2], 0.5, ALU.mult, ALU.is_gt)
            nc.vector.tensor_scalar(n1[:], emb[:], scl[:, 1:2], -0.5, ALU.mult, ALU.is_lt)
            dve.drain()
            nc.vector.tensor_tensor(hr[:], hr[:], n1[:], ALU.subtract)
            dve.drain()
            nc.vector.tensor_scalar(h_all[:, B * IT:TILES, :], hr[:], scl[:, 2:3], None, ALU.mult)
            dve.drain()
            second_norm(B, B * IT, 2 * B + 1)
            dve.wait_ge(s_k, B + 1)
            nc.vector.tensor_copy(k_all[:, :, :, NI:T], b_score[1][:].rearrange("p (f b n) -> p f b n", f=2, b=B)
                                  ).then_inc(s_ke, 1)
            dve.wait_ge(s_v, B + 1)
            for i, bk in enumerate((b_score[2], b_score[3], b_misc, b_turn[1])):
                last = nc.vector.tensor_copy(v_all[0:NT, 2 * i:2 * i + 2, 2, :],
                                             bk[0:NT, :].rearrange("p (k d) -> p k d", k=2))
            last.then_inc(s_ve, 1)

            def body(b, cur, prev):
                for u in range(UNITS):
                    kind, h0, n = unit(u)
                    if cur:
                        dve.wait_ge(s_S, b * UNITS + u + 1)
                        src = b_score[u % 4][:, 0:T] if kind == "D" else \
                            b_score[u % 4][:].rearrange("p (h k) -> p h k", h=n)
                        m = 1 if kind == "D" else n
                        nc.vector.tensor_reduce(negm[:, u % 4, 0:m], src, AX.X, ALU.max, negate=True
                                                ).then_inc(s_max, 1)
                        if u > 0:
                            recip(b, u - 1)
                    if u == 0 and prev:
                        recip(b - 1, UNITS - 1)
                    evac_turn(b, u, cur, prev)
                    if prev and u == 7:
                        after_attention(b - 1, (b - 1) * IT)
                    if prev and u == 10:
                        after_norm(b - 1, (b - 1) * IT)
                    if prev and u == 15:
                        router_logits(b - 1, (b - 1) * IT)

            def recip(b, u):
                kind, _, n = unit(u)
                m = 1 if kind == "D" else n
                dve.wait_ge(s_exp, b * UNITS + u + 1)
                if not (isinstance(b, int) and b == 0 and u < 4):
                    dve.wait_ge(s_P, b * UNITS + u - 3)
                nc.vector.reciprocal(rsum[:, u % 4, 0:m], psums[:, u % 4, 0:m]).then_inc(s_rc, 1)

            def evac_turn(b, u, cur, prev):
                v = u - 4
                if v % 2 or not (cur if v >= 0 else prev):
                    return
                bb = b if v >= 0 else b - 1
                not_first = prev if v >= 0 else not (isinstance(b, int) and b == 1)
                v = v % UNITS
                hf = v // 8
                dve.wait_ge(s_T, bb * UNITS + v + 1)
                if not_first:
                    dve.wait_ge(s_pv, 2 * (bb - 1) + hf + 1)
                kind, h0, n = unit(v)
                if kind == "A":
                    nc.vector.tensor_copy(pt_img[:, hf, h0 % HH:h0 % HH + 4, 0, :],
                                          b_turn[0][:].rearrange("p (h q) -> p h q", h=4)).then_inc(s_te_d, 1)
                else:
                    nc.vector.tensor_copy(pt_img[:, hf, h0 % HH:h0 % HH + 2, 1:3, :],
                                          b_turn[0][:].rearrange("p (h c q) -> p h c q", h=2, c=2)
                                          ).then_inc(s_te_d, 1)

            def after_attention(b, t0):
                dve.wait_ge(s_o, b + 1)
                for i in range(IT):
                    nc.vector.tensor_tensor(h_all[:, t0 + i, :], b_misc[:, i * D:i * D + D], h_all[:, t0 + i, :],
                                            ALU.add)
                dve.drain()
                for i in range(IT):
                    nc.vector.bn_stats(stats[:, i, :], h_all[:, t0 + i, :])
                dve.drain()
                for i in range(IT):
                    last = nc.vector.bn_aggr(mv[:, i, :], stats[:, i, :])
                dve.drain()
                nc.vector.tensor_copy(mv2[:, bass.ds(t0, IT), :], mv[:]).then_inc(s_mv2, 1)

            def after_norm(b, t0):
                dve.wait_ge(s_rstd2, b + 1)
                if not (isinstance(b, int) and b == 0):
                    dve.wait_ge(s_n2st, 16 * b)
                nc.vector.tensor_copy(rstd2[:, bass.ds(t0, IT)], rstd[:])
                for i in range(IT):
                    last = nc.vector.tensor_scalar(n1[:, i, :], h_all[:, t0 + i, :], mv[:, i, 0:1],
                                                   rstd[:, i:i + 1], ALU.subtract, ALU.mult)
                last.then_inc(s_n2, 1)

            def router_logits(b, t0):
                dve.wait_ge(s_lg, b + 1)
                for i in range(IT):
                    last = nc.vector.tensor_tensor(logit[:, t0 + i, :], b_misc[:, i * E:i * E + E], br_bc[:], ALU.add)
                last.then_inc(s_lge, 1)

            body(0, True, False)
            body(1, True, True)
            with dve.Fori(2, B) as b:
                body(b, True, True)
            body(B, False, True)
            after_attention(B, B * IT)
            after_norm(B, B * IT)
            router_logits(B, B * IT)
            tail_dve(dve)

        @block.tensor
        def _(pe):
            pe.wait_ge(s_w, 16 * 3)

            def transposes(src, dst):
                for k in range(DC):
                    for i in range(IT):
                        last = nc.tensor.transpose(dst[:, k * NI + i * P:k * NI + i * P + P],
                                                   src[:, i, k * P:k * P + P], ident[:])
                return last

            def projections(b):
                pe.wait_ge(s_n1, b + 1)
                transposes(n1, b_turn[0]).then_inc(s_nt, 1)
                pe.wait_ge(s_nte, b + 1)
                for k in range(DC):
                    last = nc.tensor.matmul(b_ctx[0:LAT, 0:NI], wdkv_sb[:, k, :], n_t[:, k, :],
                                            start=(k == 0), stop=(k == DC - 1))
                last.then_inc(s_c, 1)
                for f in range(2):
                    for k in range(DC):
                        last = nc.tensor.matmul(b_score[0][:, f * NI:f * NI + NI], wq_sb[:, k, f * P:f * P + P],
                                                n_t[:, k, :], start=(k == 0), stop=(k == DC - 1))
                last.then_inc(s_q, 1)
                pe.wait_ge(s_ce, b + 1)
                for f in range(2):
                    last = nc.tensor.matmul(b_score[1][:, f * NI:f * NI + NI], wuk_sb[:, f * P:f * P + P], c_t[:],
                                            start=True, stop=True)
                last.then_inc(s_k, 1)

            pe.wait_ge(s_const, NCONST)
            pe.wait_ge(s_id, 1)

            def front(i, par, first):
                b = i * 2 + par
                pe.wait_ge(s_xt[par], i * 32 + 32)
                if not first:
                    pe.wait_ge(s_n1, b)
                for t in range(IT):
                    for kc, (_, fn) in enumerate(KF):
                        last = nc.tensor.matmul(b_misc[:, t * D:t * D + D], xt[0:fn, par, kc, t * P:t * P + P],
                                                wtok[0:fn, kc, :], start=(kc == 0), stop=(kc == len(KF) - 1))
                last.then_inc(s_tok, 1)
                if not first:
                    pe.wait_ge(s_qe, b)
                    pe.wait_ge(s_ke, b)
                    pe.wait_ge(s_ve, b)
                projections(b)
                for t in range(IT):
                    last = nc.tensor.matmul(b_score[2][:, t * D:t * D + D], c_t[:, t * P:t * P + P], wuv_sb[:],
                                            start=True, stop=True)
                last.then_inc(s_v, 1)

            front(0, 0, True)
            front(0, 1, False)
            with pe.Fori(1, B // 2) as i:
                front(i, 0, False)
                front(i, 1, False)

            pe.wait_ge(s_abs, 1)
            nc.tensor.matmul(b_misc[:, 0:1], ones[:], psum_abs[:], start=True, stop=True).then_inc(s_scl, 1)
            pe.wait_ge(s_qe, B)
            pe.wait_ge(s_ke, B)
            pe.wait_ge(s_ve, B)
            projections(B)
            for i, bk in enumerate((b_score[2], b_score[3], b_misc, b_turn[1])):
                for j in range(2):
                    b = 2 * i + j
                    last = nc.tensor.matmul(bk[0:NT, j * D:j * D + D], c_t[:, b * NT:b * NT + NT], wuv_sb[:],
                                            start=True, stop=True)
            last.then_inc(s_v, 1)
            pe.wait_ge(s_qe, B + 1)
            pe.wait_ge(s_ke, B + 1)
            pe.wait_ge(s_ve, B + 1)

            def scores(b, u, first):
                kind, h0, n = unit(u)
                hf = h0 // HH
                if not (first and u < 4):
                    pe.wait_ge(s_exp, b * UNITS + u - 3)
                if u % 8 == 0:
                    pe.wait_ge(s_qm[hf], (b + 1) * (16 * (HH + 1)))
                bk = b_score[u % 4]
                mask = {"A": mask_a, "B": mask_b, "C": mask_b}.get(kind)
                if kind == "D":
                    nc.tensor.matmul(bk[:, 0:T], ident_bf[:], mask_d[:], start=True, stop=False,
                                     skip_group_check=True)
                else:
                    nc.tensor.matmul(bk[:], ident_bf[:], mask[:].rearrange("p h k -> p (h k)"), start=True,
                                     stop=False, skip_group_check=True)
                for j in range(n):
                    s = (h0 + j) % HH
                    if kind == "A":
                        last = nc.tensor.matmul(bk[:, j * P:j * P + P], q_mask[:, hf, s, 0:P],
                                                k_cur[:, hf, 0:P], start=False, stop=True, skip_group_check=True)
                    elif kind == "D":
                        last = nc.tensor.matmul(bk[NT * j:NT * j + NT, 0:T], q_mask[:, hf, s, NI:T],
                                                k_cur[:, hf, :], start=False, stop=True, skip_group_check=True)
                    else:
                        last = nc.tensor.matmul(bk[:, j * NI:j * NI + NI], q_mask[:, hf, s, P:NI],
                                                k_cur[:, hf, 0:NI], start=False, stop=True, skip_group_check=True)
                last.then_inc(s_S, 1)

            def turn(b, u, first):
                kind, h0, n = unit(u)
                pe.wait_ge(s_P, b * UNITS + u + 1)
                if not (first and u < 2):
                    pe.wait_ge(s_te_d if u % 2 == 0 else s_te_a, b * 8 + u // 2)
                bk = b_turn[u % 2]
                if kind == "D":
                    nc.tensor.transpose(bk[:, 0:P], probs[:, u % 4, 0:P], ident[:])
                    nc.tensor.transpose(bk[:, P:2 * P], probs[:, u % 4, P:2 * P], ident[:])
                    last = nc.tensor.transpose(bk[0:NT, 2 * P:3 * P], probs[:, u % 4, NI:T], ident[:])
                else:
                    for j in range(4):
                        last = nc.tensor.transpose(bk[:, j * P:j * P + P], probs[:, u % 4, j * P:j * P + P], ident[:])
                last.then_inc(s_T, 1)

            def weigh_values(b, hf, first):
                pe.wait_ge(s_te_d, b * 8 + 4 * hf + 4)
                pe.wait_ge(s_te_a, b * 8 + 4 * hf + 4)
                pe.wait_ge(s_vm, b * 2 + hf + 1)
                if not (first and hf == 0):
                    pe.wait_ge(s_cx, b * 2 + hf)
                for kt in range(2):
                    for par in range(2):
                        for j in range(4):
                            w = v_mask[:, kt, par, hf * P + 32 * j:hf * P + 32 * j + 32]
                            r = slice(32 * j, 32 * j + 32)
                            if kt == 0:
                                nc.tensor.matmul(b_ctx[r, 0:NI], w, pt_img[:, hf, 2 * j + par, 0:2, :],
                                                 start=(par == 0), stop=False, skip_group_check=True)
                            else:
                                nc.tensor.matmul(b_ctx[r, P:NI], w, pt_img[:, hf, 2 * j + par, 2, :],
                                                 start=False, stop=False, skip_group_check=True)
                for kt in range(3):
                    for par in range(2):
                        for j in range(4):
                            h = 2 * j + par
                            n = P if kt < 2 else NT
                            last = nc.tensor.matmul(
                                b_ctx[32 * j:32 * j + 32, NI:T],
                                v_mask[0:n, kt, par, hf * P + 32 * j:hf * P + 32 * j + 32],
                                pt_txt[0:n, hf, h // 4, kt, NT * (h % 4):NT * (h % 4) + NT],
                                start=False, stop=(kt == 2 and par == 1), skip_group_check=True)
                last.then_inc(s_pv, 1)

            def project_out(b, src, first):
                pe.wait_ge(s_cx, b * 2 + 2)
                if not first:
                    pe.wait_ge(s_lge, b)
                for i in range(IT):
                    for f in range(2):
                        last = nc.tensor.matmul(b_misc[:, i * D:i * D + D], src(f, i), wo_sb[:, f, :],
                                                start=(f == 0), stop=(f == 1))
                last.then_inc(s_o, 1)

            def turn_norm(b):
                pe.wait_ge(s_n2, b + 1)
                transposes(n1, b_misc).then_inc(s_n2t, 1)

            def router(b):
                pe.wait_ge(s_n2te, b + 1)
                for i in range(IT):
                    for k in range(DC):
                        last = nc.tensor.matmul(b_misc[:, i * E:i * E + E], n_t[:, k, i * P:i * P + P], wr_sb[:, k, :],
                                                start=(k == 0), stop=(k == DC - 1))
                last.then_inc(s_lg, 1)

            def body(b, cur, prev):
                for u in range(UNITS):
                    if cur:
                        scores(b, u, not prev)
                    if u < LAG and prev:
                        turn(b - 1, UNITS - LAG + u, False)
                    if u >= LAG and cur:
                        turn(b, u - LAG, not prev)
                    if u == 3 and prev:
                        weigh_values(b - 1, 1, False)
                    if u == 11 and cur:
                        weigh_values(b, 0, not prev)
                    if u == 5 and prev:
                        project_out(b - 1, lambda f, i: ctx_t[:, f, i * P:i * P + P], isinstance(b, int) and b == 1)
                    if u == 11 and prev:
                        turn_norm(b - 1)
                    if u == 14 and prev:
                        router(b - 1)

            body(0, True, False)
            body(1, True, True)
            with pe.Fori(2, B) as b:
                body(b, True, True)
            body(B, False, True)
            pe.wait_ge(s_lge, B)
            for i in range(TT):
                for f in range(2):
                    last = nc.tensor.matmul(b_misc[:, i * D:i * D + D],
                                            ctx_txt[:, f, i * PB:i * PB + PB, :].rearrange("p b n -> p (b n)"),
                                            wo_sb[:, f, :], start=(f == 0), stop=(f == 1))
            last.then_inc(s_o, 1)
            turn_norm(B)
            router(B)
            tail_pe(pe)


def kernel(**inputs):
    import numpy as np
    import concourse.bacc as bacc
    from concourse.bass_utils import run_bass_kernel_spmd

    lay = np.ascontiguousarray
    x = np.asarray(inputs["x"])
    B, C, HT, WD = x.shape
    p = 8
    rows, cols = HT // p, WD // p
    w1, w2 = np.asarray(inputs["L0_ffn_W1"]), np.asarray(inputs["L0_ffn_W2"])
    E, FF, D = w1.shape
    args = {
        "x_patches": x.reshape(B, C, rows, p, cols, p).transpose(0, 1, 3, 5, 2, 4).reshape(B, C * p * p, rows * cols),
        "text_ids": np.asarray(inputs["x_txt"]).reshape(-1, P).T,
        "tok_w": inputs["L0_tok_W"],
        "tok_gamma": np.asarray(inputs["L0_tok_gamma"]).reshape(1, -1),
        "table": inputs["L0_txt_weight"],
        "w_dkv": inputs["L0_attn_W_DKV"],
        "w_uk": inputs["L0_attn_W_UK"],
        "w_uv": inputs["L0_attn_W_UV"],
        "w_uq": inputs["L0_attn_W_UQ"],
        "w_o": inputs["L0_attn_W_O"],
        "w_router": np.asarray(inputs["L0_ffn_Wr"]).T.reshape(D // P, P, E).transpose(1, 0, 2),
        "b_router": np.asarray(inputs["L0_ffn_br"]).reshape(1, -1),
        "w1": w1.transpose(2, 0, 1).reshape(D // P, P, E, FF).transpose(1, 2, 0, 3),
        "b1": np.asarray(inputs["L0_ffn_b1"]).reshape(1, -1),
        "w2": w2.transpose(2, 0, 1).reshape(FF // P, P, E, D).transpose(1, 2, 0, 3),
        "b2": np.asarray(inputs["L0_ffn_b2"]).reshape(1, -1),
        "gamma": np.asarray(inputs["L0_ffn_gamma"]).reshape(1, -1),
        "beta": np.asarray(inputs["L0_ffn_beta"]).reshape(1, -1),
    }
    nc = bacc.Bacc("TRN2", target_bir_lowering=False, num_devices=1)
    arrays, aps = {}, {}
    for name, a in args.items():
        arrays[name] = lay(np.asarray(a))
        aps[name] = nc.dram_tensor(name, arrays[name].shape, mybir.dt.from_np(arrays[name].dtype),
                                   kind="ExternalInput").ap()
    T = rows * cols + np.asarray(inputs["x_txt"]).shape[1]
    out = nc.dram_tensor("out", (B, T, D), F32, kind="ExternalOutput").ap()
    early_fusion_kernel(nc, out=out, **aps)
    return run_bass_kernel_spmd(nc, [arrays], core_ids=[0]).results[0]["out"]
```

```python
from contextlib import ExitStack

import concourse.bass as bass
from concourse import mybir

F32 = mybir.dt.float32
BF16 = mybir.dt.bfloat16
I32 = mybir.dt.int32
ALU = mybir.AluOpType
ACT = mybir.ActivationFunctionType
AX = mybir.AxisListType

P = 128
EPS = 1e-5
NEG = -1e30


def early_fusion_kernel(nc, x_patches, text_ids, tok_w, tok_gamma, table, w_dkv, w_uk, w_uv, w_uq, w_o,
                        w_router, b_router, w1, b1, w2, b2, gamma, beta, out):
    B, FEAT, NI = x_patches.shape
    D = tok_w.shape[1]
    V = table.shape[0]
    NT = text_ids.shape[0] * text_ids.shape[1] // B
    T = NI + NT
    LAT = w_dkv.shape[1]
    HD = 16
    H = D // HD
    E, FF = w1.shape[1], w1.shape[3]
    DC, FC = D // P, FF // P
    IT = NI // P
    TILES = B * T // P
    TT = TILES - B * IT
    PB = P // NT
    TOP = 2
    NBLK = (TOP * TILES * P + E * (P - 1)) // P
    KF = [(0, P), (P, P), (2 * P, FEAT - 2 * P)]
    CHUNK = V * D // P // 32
    NCH = 32
    HH = H // 2
    assert D == 256 and NI == 256 and T == 288 and H == 16 and P // HD == HH and NBLK % 2 == 1

    ctx = ExitStack()
    with ctx:
        def sb(name, shape, dt=F32):
            return ctx.enter_context(nc.sbuf_tensor(name, shape, dt))

        def sem(name):
            return ctx.enter_context(nc.semaphore(name))

        bank = [ctx.enter_context(nc.psum_tensor(f"bank{i}", [P, 512], F32)) for i in range(8)]
        b_score, b_turn, b_ctx, b_misc = bank[0:4], bank[4:6], bank[6], bank[7]
        b_emb = (b_misc, b_turn[1])

        n2_dram = nc.dram_tensor("n2_rows", [TILES * P, D], F32).ap()
        y_dram = nc.dram_tensor("expert_rows", [NBLK * P, D], F32).ap()

        region = sb("region", [P, E * DC * FF + E * FC * D])
        w1_sb = region[:, 0:E * DC * FF].rearrange("p (e k f) -> p e k f", e=E, k=DC)
        w2_sb = region[:, E * DC * FF:].rearrange("p (e c d) -> p e c d", e=E, c=FC)
        chunk = region[:, 0:4 * CHUNK].rearrange("p (s c) -> p s c", s=4)
        o = E * DC * FF
        q_all = region[:, o:o + 2 * B * T].rearrange("p (f b t) -> p f b t", f=2, b=B)
        k_all = region[:, o + 2 * B * T:o + 4 * B * T].rearrange("p (f b t) -> p f b t", f=2, b=B)
        v_all = region[:, o + 4 * B * T:o + 4 * B * T + B * 3 * D].rearrange("p (b k d) -> p b k d", b=B, k=3)

        o += 4 * B * T + B * 3 * D
        emb = region[:, o:o + TT * D].rearrange("p (t d) -> p t d", t=TT)
        hr = region[:, o + TT * D:o + TT * D + IT * D].rearrange("p (t d) -> p t d", t=IT)

        k_cur = region[:, o:o + 2 * T].rearrange("p (f t) -> p f t", f=2)

        h_all = sb("h_all", [P, TILES, D])
        scratch = sb("scratch", [P, E * FF])
        q_mask = scratch[:, 0:2 * HH * T].rearrange("p (f s t) -> p f s t", f=2, s=HH)
        o = 2 * HH * T
        probs = scratch[:, o:o + 4 * 512].rearrange("p (s c) -> p s c", s=4)
        o += 4 * 512
        v_mask = scratch[:, o:o + 3 * 2 * D].rearrange("p (k a d) -> p k a d", k=3, a=2)
        o = 4 * CHUNK
        pt_img = region[:, o:o + 2 * HH * 3 * P].rearrange("p (f h c q) -> p f h c q", f=2, h=HH, c=3)
        o += 2 * HH * 3 * P
        pt_txt = region[:, o:o + 2 * 2 * 3 * P].rearrange("p (f g c q) -> p f g c q", f=2, g=2, c=3)

        o += 2 * 2 * 3 * P
        mask_a = region[:, o:o + 256].bitcast(BF16).rearrange("p (h k) -> p h k", h=4)
        mask_b = region[:, o + 256:o + 512].bitcast(BF16).rearrange("p (h k) -> p h k", h=2)
        mask_d = region[:, o + 512:o + 512 + T // 2].bitcast(BF16)

        work = sb("work", [P, 6544])
        used = [0]

        def carve(rows, *shape):
            n = 1
            for d in shape:
                n *= d
            v = work[0:rows, used[0]:used[0] + n]
            used[0] += n
            if len(shape) == 1:
                return v
            names = "abc"[:len(shape)]
            return v.rearrange(f"p ({' '.join(names)}) -> p {' '.join(names)}", **dict(zip(names, shape)))

        ctx_t = carve(P, 2, NI)
        ctx_txt = carve(P, 2, B, NT)
        xt = carve(P, 2, 3, NI)
        wtok = carve(P, 3, D)
        wq_sb = carve(P, DC, D)
        wo_sb = carve(P, DC, D)
        wdkv_sb = carve(P, DC, LAT)
        wuk_sb = carve(LAT, D)
        wuv_sb = carve(LAT, D)
        wr_sb = carve(P, DC, E)
        n_t = carve(P, DC, NI)
        c_t = carve(LAT, NI)
        gam_tok = carve(P, D)
        n1 = carve(P, IT, D)
        br_bc = sb("br_bc", [P, E])
        stats = sb("stats", [P, IT, 6])
        mv = sb("mv", [P, IT, 2])
        mv_emb = sb("mv_emb", [P, IT, 2])
        vare_emb = sb("vare_emb", [P, IT])
        stats_emb = sb("stats_emb", [P, IT, 6])
        vare = sb("vare", [P, IT])
        rstd = sb("rstd", [P, IT])
        rstd_emb = sb("rstd_emb", [P, IT])
        neghalf = sb("neghalf", [P, IT])
        eps = sb("eps", [P, IT])
        mv2 = sb("mv2", [P, TILES, 2])
        rstd2 = sb("rstd2", [P, TILES])
        ident = sb("ident", [P, P])
        ident_bf = sb("ident_bf", [P, P], BF16)
        negm = sb("negm", [P, 4, 4])
        psums = sb("psums", [P, 4, 4])
        rsum = sb("rsum", [P, 4, 4])
        part = sb("part", [P, NCH])
        psum_abs = sb("psum_abs", [P, 1])
        scl = sb("scl", [P, 4])
        ones = sb("ones", [P, P])
        tid = sb("tid", [P, TT], I32)
        logit = sb("logit", [P, TILES, E])

        s_const, s_w, s_id = sem("s_const"), sem("s_w"), sem("s_id")
        s_chunk = [sem(f"s_chunk{i}") for i in range(4)]
        s_scan_d, s_scan_a = sem("s_scan_d"), sem("s_scan_a")
        s_xt = [sem(f"s_xt{i}") for i in range(2)]
        s_tok, s_mv, s_rstd = sem("s_tok"), sem("s_mv"), sem("s_rstd")
        s_n1, s_nt, s_nte, s_c, s_ce = sem("s_n1"), sem("s_nt"), sem("s_nte"), sem("s_c"), sem("s_ce")
        s_q, s_qe, s_k, s_ke, s_v, s_ve = (sem(f"s_{n}") for n in ("q", "qe", "k", "ke", "v", "ve"))
        s_emb, s_abs, s_scl = sem("s_emb"), sem("s_abs"), sem("s_scl")
        s_qm = [sem(f"s_qm{i}") for i in range(2)]
        s_vm, s_S, s_max, s_exp, s_rc, s_P, s_T = (sem(f"s_{n}") for n in ("vm", "S", "max", "exp", "rc", "P", "T"))
        s_te_d, s_te_a, s_pv, s_cx, s_o = (sem(f"s_{n}") for n in ("te_d", "te_a", "pv", "cx", "o"))
        s_mv2, s_rstd2, s_n2, s_n2t, s_n2te, s_lg, s_lge, s_n2st = (
            sem(f"s_{n}") for n in ("mv2", "rstd2", "n2", "n2t", "n2te", "lg", "lge", "n2st"))

        NCONST = 9 * 16
        block = ctx.enter_context(nc.Block())
        UNITS = 16
        LAG = 3

        AT_PV0, AT_PV1 = (12, 13, 15), (4, 5, 7)
        AT_OUT, AT_SUM, AT_NORM, AT_N2T, AT_ROUTE = 8, 9, 10, 12, 14

        def unit(u):
            g, kind = u // 4, "ABCD"[u % 4]
            return kind, 4 * g + (2 if kind == "C" else 0), {"A": 4, "B": 2, "C": 2, "D": 4}[kind]

        NV = TILES * E
        W1_EARLY = 4 * CHUNK // (DC * FF)
        W2_EARLY = 4 * B * T // (FC * D)
        W2_MID = (4 * B * T + B * 3 * D) // (FC * D)
        one_slot = work[:, 0:2304].bitcast(BF16).rearrange("p (n s) -> p n s", n=TOP * TILES)
        one_blk = work[:, 2304:2304 + TOP * TILES * NBLK].bitcast(BF16).rearrange(
            "p (n a b) -> p n a b", n=TOP * TILES, a=2)
        tmp = [work[:, 3888 + i * NV:3888 + (i + 1) * NV] for i in range(13)]
        keep = work[:, 5776:6032]
        gather_idx = keep[:, 0:NBLK].bitcast(I32)
        expert_of = keep[:, NBLK:2 * NBLK].bitcast(I32)
        pos_idx = keep[:, 2 * NBLK:2 * NBLK + TOP * TILES].bitcast(I32).rearrange("p (k t) -> p k t", k=TOP)
        o = 2 * NBLK + TOP * TILES
        top_w = keep[:, o:o + TOP * TILES].rearrange("p (k t) -> p k t", k=TOP)
        o += TOP * TILES
        gi = keep[:, o:o + 2].bitcast(I32)
        RING = 3
        GROUPS = TILES // IT
        o += 2
        final_idx = keep[:, o:o + RING * TOP * IT].bitcast(I32).rearrange("p (s k i) -> p s k i", s=RING, k=TOP)
        o += RING * TOP * IT
        mvf = keep[:, o:o + RING * IT * 2].rearrange("p (s i k) -> p s i k", s=RING, i=IT)
        o += RING * IT * 2
        varf = keep[:, o:o + RING * IT].rearrange("p (s i) -> p s i", s=RING)
        o += RING * IT
        rstdf = keep[:, o:o + RING * IT].rearrange("p (s i) -> p s i", s=RING)
        o += RING * IT
        statf = keep[:, o:o + IT * 6].rearrange("p (i k) -> p i k", i=IT)
        assert o + IT * 6 <= 256 and GROUPS % RING == 0
        gam, bet = work[:, 6032:6032 + D], work[:, 6288:6288 + D]
        h_t = work[:, 0:2 * FF].rearrange("p (s c n) -> p s c n", s=2, c=FC)
        xg = work[:, 2 * FF:2 * FF + 2 * D].rearrange("p (s d) -> p s d", s=2)
        o = 2 * FF + 2 * D
        xg_t = work[:, o:o + DC * P].rearrange("p (k n) -> p k n", k=DC)
        ys = work[:, o + D:o + 3 * D].rearrange("p (s d) -> p s d", s=2)
        b2_bc = work[:, o + 3 * D:o + 3 * D + E * D].rearrange("p (e d) -> p e d", e=E)
        w1_cur = scratch[:, 0:2 * DC * FF].rearrange("p (s k f) -> p s k f", s=2, k=DC)
        o = 2 * DC * FF
        b1_sb = scratch[:, o:o + E * FC].rearrange("p (e c) -> p e c", e=E)
        o += E * FC
        b1_cur = scratch[:, o:o + 2 * FC].rearrange("p (s c) -> p s c", s=2)
        z = region[:, 0:TILES * D].rearrange("p (t d) -> p t d", t=TILES)
        o = TILES * D
        yg = region[:, o:o + RING * TOP * IT * D].rearrange("p (s k i d) -> p s k i d", s=RING, k=TOP, i=IT)
        assert o + RING * TOP * IT * D <= E * DC * FF

        s_lw, s_b2, s_dc, s_dp, s_dl, s_de = (sem(f"s_{n}") for n in ("lw", "b2", "dc", "dp", "dl", "de"))
        s_oh, s_ip, s_idx, s_blk = (sem(f"s_{n}") for n in ("oh", "ip", "idx", "blk"))
        s_xg = [sem(f"s_xg{i}") for i in range(2)]
        s_xgt, s_xgte, s_w1, s_wcur, s_ht, s_w2, s_ys = (
            sem(f"s_{n}") for n in ("xgt", "xgte", "w1", "wcur", "ht", "w2", "ys"))
        s_yst = [sem(f"s_yst{i}") for i in range(2)]
        s_g = [sem(f"s_g{i}") for i in range(RING)]
        s_gb, s_n2back, s_out = sem("s_gb"), sem("s_n2back"), sem("s_out")
        s_z, s_mvf, s_rf, s_zo = (sem(f"s_{n}") for n in ("z", "mvf", "rf", "zo"))
        pref_ps, tot_ps, idx_ps = b_ctx[:, 0:NV], b_ctx[:, NV:2 * NV], b_misc[:, 0:2 * NBLK]
        hid, y_ps, xt_ps = (bank[0:2], bank[2:4]), (bank[4], bank[6]), bank[5]

        def load_w1(sp, first, last):
            for e in range(first, last):
                sp.dma_start(w1_sb[:, e], w1[:, e]).then_inc(s_lw, 16)

        def load_w2(sp, first, last):
            for e in range(first, last):
                sp.dma_start(w2_sb[:, e], w2[:, e]).then_inc(s_lw, 16)

        def tail_sp(sp):
            sp.wait_ge(s_pv, 2 * B)
            sp.wait_ge(s_cx, 2 * B)
            load_w1(sp, W1_EARLY, E)
            load_w2(sp, W2_MID, E)
            sp.dma_start(b1_sb, b1).then_inc(s_lw, 16)
            sp.wait_ge(s_n2, B + 1)
            sp.dma_start(n2_dram[B * IT * P:, :].rearrange("(i p) d -> p i d", p=P), n1[:]).then_inc(s_n2st, 16)
            sp.wait_ge(s_n2st, 16 * (B + 1))
            sp.wait_ge(s_n2t, B + 1)
            sp.dma_start(gam, gamma.broadcast_to([P, D])).then_inc(s_gb, 16)
            sp.dma_start(bet, beta.broadcast_to([P, D])).then_inc(s_gb, 16)
            sp.wait_ge(s_idx, 1)
            sp.dma_start(b2_bc, b2.broadcast_to([P, E * D])).then_inc(s_b2, 16)

            def store_y(n, par):
                sp.wait_ge(s_ys, n + 1)
                sp.dma_start(y_dram[bass.ds(n * P, P), :], ys[:, par, :]).then_inc(s_yst[par], 16)

            with sp.Fori(0, NBLK // 2) as i:
                for par in range(2):
                    store_y(i * 2 + par, par)
            store_y(NBLK - 1, 0)
            with sp.Fori(0, B) as b:
                sp.wait_ge(s_zo, b + 1)
                sp.dma_start(out[b, 0:NI, :].rearrange("(i p) d -> p i d", p=P), z[:, bass.ds(b * IT, IT), :]
                             ).then_inc(s_out, 16)
            sp.wait_ge(s_zo, GROUPS)
            for i in range(TT):
                for j in range(PB):
                    sp.dma_start(out[i * PB + j, NI:T, :], z[NT * j:NT * j + NT, B * IT + i, :]).then_inc(s_out, 16)
            sp.wait_ge(s_out, 16 * (B + TT * PB))

        def tail_pool(pool):
            pool.wait_ge(s_lge, B + 1)
            io_i = tmp[0][:, 0:P].bitcast(I32)
            nc.gpsimd.iota(io_i, [[1, P]], base=0, channel_multiplier=0)
            nc.gpsimd.iota(tmp[1][:, 0:1].bitcast(I32), [[0, 1]], base=0, channel_multiplier=1)
            nc.gpsimd.memset(tmp[3], 1.0)
            pool.drain()
            nc.gpsimd.tensor_copy(tmp[2][:, 0:P], io_i)
            nc.gpsimd.tensor_copy(tmp[1][:, 1:2], tmp[1][:, 0:1].bitcast(I32))
            nc.gpsimd.affine_select(tmp[4][:, 0:P], ones[:], [[1, P]], ALU.is_ge, 0.0, base=-1, channel_multiplier=-1)
            nc.gpsimd.memset(tmp[3].rearrange("p (e t) -> p e t", e=E)[:, :, 0:1], 0.0)
            pool.drain()
            nc.gpsimd.tensor_scalar(tmp[5][:, 0:E], tmp[2][:, 0:E], -1.0, float(E), ALU.mult, ALU.add)
            nc.gpsimd.tensor_scalar(tmp[5][:, E:E + TILES], tmp[2][:, 0:TILES], float(P), None, ALU.mult
                                    ).then_inc(s_dc, 1)

            def gather(n, par, first):
                if not first:
                    pool.wait_ge(s_xgt, n - 1)
                nc.gpsimd.tensor_copy(gi[:, par:par + 1], gather_idx[:, bass.ds(n, 1)])
                pool.drain()
                nc.gpsimd.indirect_dma_start(xg[:, par, :], None, n2_dram,
                                             bass.IndirectOffsetOnAxis(gi[:, par:par + 1], 0)).then_inc(s_xg[par], 16)

            pool.wait_ge(s_idx, 1)
            pool.wait_ge(s_n2st, 16 * (B + 1))
            gather(0, 0, True)
            gather(1, 1, True)
            with pool.Fori(1, NBLK // 2) as i:
                gather(i * 2, 0, False)
                gather(i * 2 + 1, 1, False)
            gather(NBLK - 1, 0, False)

            def expert_rows(g, s, first):
                if not first:
                    pool.wait_ge(s_z, g - RING + 1)
                nc.gpsimd.tensor_copy(final_idx[:, s], pos_idx[:, :, bass.ds(g * IT, IT)])
                pool.drain()
                for i in range(IT):
                    for k in range(TOP):
                        nc.gpsimd.indirect_dma_start(yg[:, s, k, i, :], None, y_dram,
                                                     bass.IndirectOffsetOnAxis(final_idx[:, s, k, i:i + 1], 0)
                                                     ).then_inc(s_g[s], 16)

            def final_rstd(g, s):
                pool.wait_ge(s_mvf, g + 1)
                nc.gpsimd.tensor_tensor(rstdf[:, s, :], varf[:, s, :], neghalf[:], ALU.pow).then_inc(s_rf, 1)

            for par in range(2):
                pool.wait_ge(s_yst[par], 16 * ((NBLK + 1 - par) // 2))
            pool.wait_ge(s_w1, NBLK)
            for s in range(RING):
                expert_rows(s, s, True)
            with pool.Fori(0, GROUPS // RING - 1) as i:
                for s in range(RING):
                    final_rstd(i * RING + s, s)
                    expert_rows(i * RING + RING + s, s, False)
            for s in range(RING):
                final_rstd(GROUPS - RING + s, s)

        def tail_act(act):
            act.wait_ge(s_dl, 1)
            nc.scalar.activation(tmp[7][:, TILES:2 * TILES], tmp[7][:, 0:TILES], ACT.Exp).then_inc(s_de, 1)

            def rows_t(n, first):
                act.wait_ge(s_xgt, n + 1)
                if not first:
                    act.wait_ge(s_w1, n)
                nc.scalar.activation(xg_t.rearrange("p k n -> p (k n)"), xt_ps[:, 0:DC * P], ACT.Copy
                                     ).then_inc(s_xgte, 1)

            def hidden(n, par, first):
                act.wait_ge(s_w1, n + 1)
                if not first:
                    act.wait_ge(s_w2, n - 1)
                for c in range(FC):
                    last = nc.scalar.activation(h_t[:, par, c, :], hid[par][c // 4][:, c % 4 * P:c % 4 * P + P],
                                                ACT.Relu, bias=b1_cur[:, par, c:c + 1])
                last.then_inc(s_ht, 1)

            act.wait_ge(s_idx, 1)
            rows_t(0, True)
            rows_t(1, False)
            hidden(0, 0, True)
            rows_t(2, False)
            hidden(1, 1, True)
            with act.Fori(1, NBLK // 2) as i:
                for par in range(2):
                    rows_t(i * 2 + par + 1, False)
                    hidden(i * 2 + par, par, False)
            hidden(NBLK - 1, 0, False)
            act.wait_ge(s_w1, NBLK)
            act.dma_start(z, n2_dram.rearrange("(t p) d -> p t d", p=P)).then_inc(s_n2back, 16)

        def tail_dve(dve):
            A = "p (t e) -> p t e"
            iota, e8, thr = tmp[2][:, 0:P], tmp[5][:, 0:E], tmp[5][:, E:E + TILES]
            pcol, notfirst = tmp[1][:, 1:2], tmp[3]
            ones_p = (tmp[6], tmp[8])
            cut = tmp[9]
            m = tmp[7]
            small = tmp[10]
            row8 = e8[:, None, :].broadcast_to([P, TILES, E])
            dve.wait_ge(s_dc, 1)
            dve.drain()

            def pick(src, value, onehot):
                nc.vector.tensor_reduce(value, src, AX.X, ALU.max)
                dve.drain()
                nc.vector.tensor_tensor(onehot, src, value[:, :, None].broadcast_to([P, TILES, E]), ALU.is_ge)
                dve.drain()
                nc.vector.tensor_tensor(onehot, onehot, row8, ALU.mult)
                dve.drain()
                nc.vector.tensor_reduce(small[:, 0:TILES], onehot, AX.X, ALU.max)
                dve.drain()
                nc.vector.tensor_tensor(onehot, row8, small[:, 0:TILES, None].broadcast_to([P, TILES, E]),
                                        ALU.is_equal)
                dve.drain()

            o1, o2_ = (t.rearrange(A, t=TILES) for t in ones_p)
            pick(logit[:], small[:, 36:36 + TILES], o1)
            nc.vector.scalar_tensor_tensor(cut, ones_p[0], -3e38, logit[:].rearrange("p t e -> p (t e)"),
                                           ALU.mult, ALU.add)
            dve.drain()
            pick(cut.rearrange(A, t=TILES), small[:, 72:72 + TILES], o2_)
            nc.vector.tensor_tensor(cut, ones_p[0], ones_p[1], ALU.add).then_inc(s_oh, 1)
            nc.vector.tensor_tensor(m[:, 0:TILES], small[:, 72:72 + TILES], small[:, 36:36 + TILES], ALU.subtract
                                    ).then_inc(s_dl, 1)
            dve.wait_ge(s_de, 1)
            nc.vector.tensor_scalar(m[:, 36:36 + TILES], m[:, TILES:2 * TILES], 1.0, None, ALU.add)
            dve.drain()
            nc.vector.reciprocal(top_w[:, 0, :], m[:, 36:36 + TILES])
            dve.drain()
            nc.vector.tensor_tensor(top_w[:, 1, :], m[:, TILES:2 * TILES], top_w[:, 0, :], ALU.mult)
            dve.wait_ge(s_dp, 1)
            tot, incl, cnt = tmp[11], tmp[12], tmp[10][:, 0:E]
            nc.vector.tensor_copy(tot.rearrange("p (e t) -> p t e", e=E), tot_ps.rearrange(A, t=TILES))
            dve.drain()
            nc.vector.tensor_tensor_scan(incl, notfirst, tot, 0.0, ALU.mult, ALU.add)
            dve.drain()
            nc.vector.tensor_tensor(tot, incl, tot, ALU.subtract)
            nc.vector.tensor_copy(cnt, incl.rearrange("p (e t) -> p e t", e=E)[:, :, TILES - 1])
            dve.drain()
            nc.vector.tensor_tensor(cut.rearrange("p (e t) -> p e t", e=E), cnt[:, :, None].broadcast_to([P, E, TILES]),
                                    thr[:, None, :].broadcast_to([P, E, TILES]), ALU.is_gt)
            dve.drain()
            nb, ends, base = small[:, E:2 * E], small[:, 2 * E:3 * E], small[:, 3 * E:4 * E]
            nc.vector.tensor_reduce(nb, cut.rearrange("p (e t) -> p e t", e=E), AX.X, ALU.add)
            dve.drain()
            nc.vector.tensor_tensor_scan(ends, ones[:, 0:E], nb, 0.0, ALU.mult, ALU.add)
            dve.drain()
            nc.vector.tensor_tensor(base, ends, nb, ALU.subtract)
            dve.drain()
            nc.vector.scalar_tensor_tensor(tot.rearrange("p (e t) -> p e t", e=E),
                                           base[:, :, None].broadcast_to([P, E, TILES]), float(P),
                                           tot.rearrange("p (e t) -> p e t", e=E), ALU.mult, ALU.add)
            dve.drain()
            nc.vector.tensor_tensor(cut.rearrange(A, t=TILES), pref_ps.rearrange(A, t=TILES),
                                    tot.rearrange("p (e t) -> p t e", e=E), ALU.add)
            dve.drain()
            for k in range(TOP):
                nc.vector.tensor_tensor(ones_p[k], ones_p[k], cut, ALU.mult)
            dve.drain()
            for k in range(TOP):
                nc.vector.tensor_reduce(m[:, k * TILES:(k + 1) * TILES], (o1, o2_)[k], AX.X, ALU.add)
            dve.drain()
            flat = pos_idx.rearrange("p k t -> p (k t)")
            nc.vector.tensor_copy(flat, m[:, 0:TOP * TILES])
            dve.drain()
            ti = tmp[12].bitcast(I32)
            nc.vector.tensor_scalar(ti[:, 0:36], flat, P - 1, None, ALU.bitwise_and)
            nc.vector.tensor_scalar(ti[:, 36:72], flat, 7, None, ALU.logical_shift_right)
            dve.drain()
            nc.vector.tensor_copy(m[:, 0:72], ti[:, 0:72])
            dve.drain()
            N = TOP * TILES
            nc.vector.tensor_tensor(one_slot, iota[:, None, :].broadcast_to([P, N, P]),
                                    m[:, 0:N, None].broadcast_to([P, N, P]), ALU.is_equal)
            nc.vector.tensor_tensor(one_blk[:, :, 0, :], iota[:, None, 0:NBLK].broadcast_to([P, N, NBLK]),
                                    m[:, N:2 * N, None].broadcast_to([P, N, NBLK]), ALU.is_equal)
            dve.drain()
            nc.vector.tensor_scalar(one_blk[:, :, 1, :], one_blk[:, :, 0, :], pcol, None, ALU.mult)
            dve.drain()
            for k in range(TOP):
                last = nc.vector.tensor_tensor(one_blk[:, k * TILES:(k + 1) * TILES, 0, :],
                                               one_blk[:, k * TILES:(k + 1) * TILES, 0, :],
                                               iota[:, 0:TILES, None].broadcast_to([P, TILES, NBLK]), ALU.mult)
            last.then_inc(s_ip, 1)
            for b0, bn, dst in ((0, TILES, 0), (TILES, TILES, TILES), (2 * TILES, NBLK - 2 * TILES, 2 * TILES)):
                nc.vector.tensor_tensor(cut[:, 0:bn * E].rearrange("p (b e) -> p b e", e=E),
                                        iota[:, b0:b0 + bn, None].broadcast_to([P, bn, E]),
                                        ends[:, None, :].broadcast_to([P, bn, E]), ALU.is_ge)
                dve.drain()
                nc.vector.tensor_reduce(small[:, 40 + b0:40 + b0 + bn],
                                        cut[:, 0:bn * E].rearrange("p (b e) -> p b e", e=E), AX.X, ALU.add)
                dve.drain()
            nc.vector.tensor_scalar(expert_of, small[:, 40:40 + NBLK], float(E - 1), None, ALU.min).then_inc(s_blk, 1)
            dve.wait_ge(s_ip, 2)
            nc.vector.tensor_copy(m[:, 0:2 * NBLK], idx_ps)
            dve.drain()
            nc.vector.scalar_tensor_tensor(gather_idx, m[:, 0:NBLK], float(P), m[:, NBLK:2 * NBLK],
                                           ALU.mult, ALU.add).then_inc(s_idx, 1)

            def weights_of(n, par, first):
                e = dve.value_load(expert_of[0:1, bass.ds(n, 1)], min_val=0, max_val=E - 1)
                if not first:
                    dve.wait_ge(s_ht, n - 1)
                nc.vector.tensor_scalar(b1_cur[:, par, :], b1_sb[:, e, :], 1.0, None, ALU.mult)
                nc.vector.tensor_scalar(w1_cur[:, par], w1_sb[:, e], 1.0, None, ALU.mult).then_inc(s_wcur, 1)

            def rows_out(n, par, first):
                e = dve.value_load(expert_of[0:1, bass.ds(n, 1)], min_val=0, max_val=E - 1)
                dve.wait_ge(s_w2, n + 1)
                if not first:
                    dve.wait_ge(s_yst[par], n // 2 * 16 if isinstance(n, int) else (n - par) * 8)
                nc.vector.tensor_tensor(ys[:, par, :], y_ps[par][:, 0:D], b2_bc[:, e, :], ALU.add).then_inc(s_ys, 1)

            dve.wait_ge(s_gb, 32)
            nc.vector.tensor_tensor(h_all[:], h_all[:], bet[:, None, :].broadcast_to([P, TILES, D]), ALU.add)
            dve.wait_ge(s_blk, 1)
            dve.wait_ge(s_lw, 16 * (2 * E + 1))
            weights_of(0, 0, True)
            weights_of(1, 1, True)
            dve.wait_ge(s_b2, 16)
            weights_of(2, 0, False)
            rows_out(0, 0, True)
            weights_of(3, 1, False)
            rows_out(1, 1, True)
            with dve.Fori(1, (NBLK - 3) // 2) as i:
                for par in range(2):
                    n = i * 2 + par
                    weights_of(n + 2, par, False)
                    rows_out(n, par, False)
            weights_of(NBLK - 1, 0, False)
            rows_out(NBLK - 3, 0, False)
            rows_out(NBLK - 2, 1, False)
            rows_out(NBLK - 1, 0, False)

            def combine(g, s, i):
                dve.wait_ge(s_g[s], (i + 1) * (16 * TOP * IT))
                for k in range(TOP):
                    for j in range(IT):
                        t = g * IT + j
                        last = nc.vector.scalar_tensor_tensor(z[:, t, :], yg[:, s, k, j, :],
                                                              top_w[:, k, bass.ds(t, 1)], z[:, t, :],
                                                              ALU.mult, ALU.add)
                    if k == TOP - 1:
                        last.then_inc(s_z, 1)
                    dve.drain()
                for j in range(IT):
                    nc.vector.bn_stats(statf[:, j, :], z[:, g * IT + j, :])
                dve.drain()
                for j in range(IT):
                    nc.vector.bn_aggr(mvf[:, s, j, :], statf[:, j, :])
                dve.drain()
                nc.vector.tensor_tensor(varf[:, s, :], mvf[:, s, :, 1], eps[:], ALU.add).then_inc(s_mvf, 1)

            def finish(g, s):
                dve.wait_ge(s_rf, g + 1)
                for j in range(IT):
                    nc.vector.tensor_scalar(z[:, g * IT + j, :], z[:, g * IT + j, :], mvf[:, s, j, 0:1],
                                            rstdf[:, s, j:j + 1], ALU.subtract, ALU.mult)
                dve.drain()
                rows = bass.ds(g * IT, IT)
                nc.vector.tensor_tensor(z[:, rows, :], z[:, rows, :], gam[:, None, :].broadcast_to([P, IT, D]), ALU.mult)
                dve.drain()
                nc.vector.tensor_tensor(z[:, rows, :], z[:, rows, :], h_all[:, rows, :], ALU.add).then_inc(s_zo, 1)

            dve.wait_ge(s_n2back, 16)
            combine(0, 0, 0)
            with dve.Fori(0, GROUPS // RING - 1) as i:
                for s in range(RING):
                    g = i * RING + s
                    combine(g + 1, (s + 1) % RING, i + (s + 1) // RING)
                    finish(g, s)
            for s in range(RING):
                g = GROUPS - RING + s
                if s + 1 < RING:
                    combine(g + 1, s + 1, GROUPS // RING - 1)
                finish(g, s)

        def tail_pe(pe):
            pe.wait_ge(s_oh, 1)
            nc.tensor.matmul(pref_ps, tmp[4][:, 0:P], tmp[9], start=True, stop=True)
            nc.tensor.matmul(tot_ps, ones[:], tmp[9], start=True, stop=True).then_inc(s_dp, 1)
            pe.wait_ge(s_ip, 1)
            N = TOP * TILES
            for n in range(N):
                last = nc.tensor.matmul(idx_ps, one_slot[:, n, :], one_blk[:, n, :, :], start=(n == 0), stop=(n == N - 1))
            last.then_inc(s_ip, 1)

            def rows_t(n, par):
                pe.wait_ge(s_xg[par], n // 2 * 16 + 16 if isinstance(n, int) else (n - par) * 8 + 16)
                if not (isinstance(n, int) and n == 0):
                    pe.wait_ge(s_xgte, n)
                for k in range(DC):
                    last = nc.tensor.transpose(xt_ps[:, k * P:k * P + P], xg[:, par, k * P:k * P + P], ident[:])
                last.then_inc(s_xgt, 1)

            def up(n, par, first):
                pe.wait_ge(s_xgte, n + 1)
                pe.wait_ge(s_wcur, n + 1)
                if not first:
                    pe.wait_ge(s_ht, n - 1)
                for c in range(FC):
                    for k in range(DC):
                        last = nc.tensor.matmul(hid[par][c // 4][:, c % 4 * P:c % 4 * P + P],
                                                w1_cur[:, par, k, c * P:c * P + P], xg_t[:, k, :],
                                                start=(k == 0), stop=(k == DC - 1))
                last.then_inc(s_w1, 1)

            def down(n, par, first):
                e = pe.value_load(expert_of[0:1, bass.ds(n, 1)], min_val=0, max_val=E - 1)
                pe.wait_ge(s_ht, n + 1)
                if not first:
                    pe.wait_ge(s_ys, n - 1)
                for c in range(FC):
                    last = nc.tensor.matmul(y_ps[par][:, 0:D], h_t[:, par, c, :], w2_sb[:, e, c, :], start=(c == 0),
                                            stop=(c == FC - 1))
                last.then_inc(s_w2, 1)

            pe.wait_ge(s_blk, 1)
            pe.wait_ge(s_lw, 16 * (2 * E + 1))
            rows_t(0, 0)
            up(0, 0, True)
            rows_t(1, 1)
            up(1, 1, True)
            rows_t(2, 0)
            down(0, 0, True)
            up(2, 0, False)
            rows_t(3, 1)
            down(1, 1, True)
            with pe.Fori(1, (NBLK - 3) // 2) as i:
                for par in range(2):
                    n = i * 2 + par
                    up(n + 1, 1 - par, False)
                    rows_t(n + 2, par)
                    down(n, par, False)
            up(NBLK - 2, 1, False)
            rows_t(NBLK - 1, 0)
            down(NBLK - 3, 0, False)
            up(NBLK - 1, 0, False)
            down(NBLK - 2, 1, False)
            down(NBLK - 1, 0, False)

        @block.sync
        def _(sp):
            for kc, (f0, fn) in enumerate(KF):
                sp.dma_start(wtok[0:fn, kc, :], tok_w[f0:f0 + fn, :]).then_inc(s_w, 16)
            sp.dma_start(gam_tok[:], tok_gamma.broadcast_to([P, D])).then_inc(s_const, 16)

            def load_x(b, par):
                sp.dma_start(xt[:, par, 0:2, :], x_patches[b, 0:2 * P, :].rearrange("(k p) n -> p k n", p=P)
                             ).then_inc(s_xt[par], 16)
                sp.dma_start(xt[0:KF[2][1], par, 2, :], x_patches[b, 2 * P:FEAT, :]).then_inc(s_xt[par], 16)

            load_x(0, 0)
            sp.dma_start(wq_sb[:], w_uq.rearrange("(k p) n -> p k n", p=P)).then_inc(s_const, 16)
            sp.dma_start(wdkv_sb[:], w_dkv.rearrange("(k p) n -> p k n", p=P)).then_inc(s_const, 16)
            sp.dma_start(wuk_sb[:], w_uk).then_inc(s_const, 16)
            sp.dma_start(wuv_sb[:], w_uv).then_inc(s_const, 16)
            sp.dma_start(wo_sb[:], w_o.rearrange("(k p) n -> p k n", p=P)).then_inc(s_const, 16)
            sp.dma_start(wr_sb[:], w_router).then_inc(s_const, 16)
            sp.dma_start(br_bc[:], b_router.broadcast_to([P, E])).then_inc(s_const, 16)
            sp.dma_start(tid[:], text_ids).then_inc(s_const, 16)
            load_x(1, 1)

            table_c = table.rearrange("(c r) d -> c (r d)", c=NCH).rearrange("c (p x) -> c p x", p=P)

            def load_chunks(b, first):
                for s in range(4):
                    if not first:
                        sp.wait_ge(s_scan_d if s < 2 else s_scan_a, 2 * (b - 1) + s % 2 + 1)
                    sp.dma_start(chunk[:, s, :], table_c[b * 4 + s]).then_inc(s_chunk[s], 16)

            load_chunks(0, True)
            with sp.Fori(0, B // 2 - 1) as i:
                for par in range(2):
                    b = i * 2 + par + 1
                    sp.wait_ge(s_tok, b)
                    load_x(b + 1, par)
                    load_chunks(b, False)
            load_chunks(B - 1, False)

            def fill_q(b, hf, first):
                if not first:
                    sp.wait_ge(s_S, (b - 1) * UNITS + 8 * hf + 8)
                sp.dma_start(k_cur[:, hf, :], k_all[:, hf, b, :]).then_inc(s_qm[hf], 16)
                for s in range(HH):
                    r = slice(HD * s, HD * s + HD)
                    sp.dma_start(q_mask[r, hf, s, :], q_all[r, hf, b, :]).then_inc(s_qm[hf], 16)

            def store_n2(b):
                sp.wait_ge(s_n2, b + 1)
                sp.dma_start(n2_dram[bass.ds(b * (IT * P), IT * P), :].rearrange("(i p) d -> p i d", p=P),
                             n1[:]).then_inc(s_n2st, 16)

            sp.wait_ge(s_qe, B + 1)
            sp.wait_ge(s_ke, B + 1)
            sp.wait_ge(s_id, 1)
            fill_q(0, 0, True)
            fill_q(0, 1, True)
            fill_q(1, 0, False)
            sp.wait_ge(s_scan_d, 2 * B)
            sp.wait_ge(s_scan_a, 2 * B)
            load_w1(sp, 0, W1_EARLY)
            with sp.Fori(1, B - 1) as b:
                fill_q(b, 1, False)
                fill_q(b + 1, 0, False)
                store_n2(b - 1)
            fill_q(B - 1, 1, False)
            store_n2(B - 2)
            for hf in range(2):
                sp.wait_ge(s_qm[hf], B * 16 * (HH + 1))
            load_w2(sp, 0, W2_EARLY)
            sp.wait_ge(s_vm, 2 * B)
            load_w2(sp, W2_EARLY, W2_MID)
            store_n2(B - 1)
            tail_sp(sp)

        @block.gpsimd
        def _(pool):
            nc.gpsimd.memset(neghalf[:], -0.5)
            nc.gpsimd.memset(eps[:], EPS)
            nc.gpsimd.memset(ones[:], 1.0)
            nc.gpsimd.memset(v_mask, 0.0)
            nc.gpsimd.memset(q_mask, 0.0)
            nc.gpsimd.memset(ident[:], 0.0)
            nc.gpsimd.memset(mask_a[:], 0.0)
            nc.gpsimd.memset(mask_b[:], 0.0)
            nc.gpsimd.memset(mask_d[:], 0.0)
            pool.drain()
            nc.gpsimd.affine_select(ident[:], ident[:], [[-1, P]], ALU.not_equal, 1.0, base=0, channel_multiplier=1)
            nc.gpsimd.affine_select(mask_a[:], mask_a[:], [[0, 4], [-1, P]], ALU.is_ge, NEG, base=0,
                                    channel_multiplier=1)
            nc.gpsimd.affine_select(mask_b[:], mask_b[:], [[0, 2], [-1, 2 * P]], ALU.is_ge, NEG, base=P,
                                    channel_multiplier=1)
            for j in range(4):
                r = slice(NT * j, NT * j + NT)
                pool.drain()
                nc.gpsimd.affine_select(mask_d[r, :], mask_d[r, :], [[-1, T]], ALU.is_ge, NEG, base=NI,
                                        channel_multiplier=1)
            pool.drain()
            nc.gpsimd.tensor_copy(ident_bf[:], ident[:]).then_inc(s_id, 1)

            def inv_std(var, via, res):
                nc.gpsimd.tensor_tensor(via[:], var, eps[:], ALU.add)
                pool.drain()
                return nc.gpsimd.tensor_tensor(res, via[:], neghalf[:], ALU.pow)

            with pool.Fori(0, B) as b:
                pool.wait_ge(s_mv, 2 * b + 1)
                inv_std(mv_emb[:, :, 1], vare_emb, rstd_emb[:]).then_inc(s_rstd, 1)
                pool.wait_ge(s_mv, 2 * b + 2)
                inv_std(mv[:, :, 1], vare, rstd[:]).then_inc(s_rstd, 1)
            pool.wait_ge(s_const, NCONST)
            for j in range(TT):
                nc.gpsimd.indirect_dma_start(emb[:, j, :], None, table, bass.IndirectOffsetOnAxis(tid[:, j:j + 1], 0)
                                             ).then_inc(s_emb, 16)
            pool.wait_ge(s_mv, 2 * B + 1)
            inv_std(mv[:, :, 1], vare, rstd[:]).then_inc(s_rstd, 1)

            def fill_v(b, hf, part, first):
                if part == 0 and not first:
                    pool.wait_ge(s_pv, 2 * (b - 1) + hf + 1)
                par, (rows, kt) = part % 2, ((slice(0, P), slice(0, 2)), (slice(0, NT), slice(2, 3)))[part // 2]
                last = nc.gpsimd.tensor_copy(
                    v_mask[rows, kt, par, hf * P:hf * P + P].rearrange("p k (j z) -> p k j z", z=32)[
                        :, :, :, HD * par:HD * par + HD],
                    v_all[rows, b, kt, hf * P:hf * P + P].rearrange("p k (j z) -> p k j z", z=32)[
                        :, :, :, HD * par:HD * par + HD])
                if part == 3:
                    last.then_inc(s_vm, 1)

            def body(b, cur, prev):
                for u in range(UNITS):
                    if cur:
                        kind, h0, n = unit(u)
                        w = {"A": P, "B": 2 * P, "C": 2 * P, "D": T}[kind]
                        pool.wait_ge(s_rc, b * UNITS + u + 1)
                        m = 1 if kind == "D" else n
                        p = probs[:, u % 4, 0:m * w].rearrange("p (h k) -> p h k", h=m)
                        nc.gpsimd.tensor_tensor(p, p, rsum[:, u % 4, 0:m, None].broadcast_to([P, m, w]), ALU.mult
                                                ).then_inc(s_P, 1)
                        if u in range(2, 6):
                            fill_v(b, 0, u - 2, not prev)
                        if u in range(9, 13):
                            fill_v(b, 1, u - 9, not prev)
                    if u == AT_NORM and prev:
                        pool.wait_ge(s_mv2, b)
                        inv_std(mv[:, :, 1], vare, rstd[:]).then_inc(s_rstd2, 1)

            pool.wait_ge(s_ve, B + 1)
            body(0, True, False)
            with pool.Fori(1, B) as b:
                body(b, True, True)
            body(B, False, True)
            pool.wait_ge(s_mv2, B + 1)
            inv_std(mv[:, :, 1], vare, rstd[:]).then_inc(s_rstd2, 1)
            tail_pool(pool)

        @block.scalar
        def _(act):
            def scan(b, s):
                act.wait_ge(s_chunk[s], 16 * (b + 1))
                nc.scalar.activation(chunk[:, s, :], chunk[:, s, :], ACT.Abs,
                                     accum_out=part[:, bass.ds(b * 4 + s, 1)]).then_inc(s_scan_a, 1)

            def evacuate(b):
                act.wait_ge(s_nt, b + 1)
                nc.scalar.activation(n_t[:].rearrange("p k n -> p (k n)"), b_turn[0][:], ACT.Copy).then_inc(s_nte, 1)
                act.wait_ge(s_c, b + 1)
                nc.scalar.activation(c_t[:], b_ctx[0:LAT, 0:NI], ACT.Copy).then_inc(s_ce, 1)
                act.wait_ge(s_q, b + 1)

            SC = float(HD) ** -0.5
            with act.Fori(0, B) as b:
                scan(b, 2)
                evacuate(b)
                nc.scalar.activation(q_all[:, :, b, 0:NI], b_score[0][:].rearrange("p (f n) -> p f n", f=2),
                                     ACT.Copy, scale=SC).then_inc(s_qe, 1)
                scan(b, 3)
            evacuate(B)
            nc.scalar.activation(q_all[:, :, :, NI:T], b_score[0][:].rearrange("p (f b n) -> p f b n", f=2, b=B),
                                 ACT.Copy, scale=SC).then_inc(s_qe, 1)

            def body(b, cur, prev):
                for u in range(UNITS):
                    kind, h0, n = unit(u)
                    if cur:
                        act.wait_ge(s_max, b * UNITS + u + 1)
                        if prev or u >= 4:
                            act.wait_ge(s_T, b * UNITS + u - 3)
                        w = {"A": P, "B": 2 * P, "C": 2 * P, "D": T}[kind]
                        for k in range(1 if kind == "D" else n):
                            last = nc.scalar.activation(probs[:, u % 4, k * w:k * w + w],
                                                        b_score[u % 4][:, k * w:k * w + w], ACT.Exp,
                                                        bias=negm[:, u % 4, k:k + 1],
                                                        accum_out=psums[:, u % 4, k:k + 1])
                        last.then_inc(s_exp, 1)
                    evac_turn(b, u, cur, prev)
                    if u == 1 and prev:
                        evac_ctx(b - 1, 0)
                    if u == AT_PV1[2] and prev:
                        evac_ctx(b - 1, 1)
                    if u == AT_N2T and prev:
                        act.wait_ge(s_n2t, b)
                        nc.scalar.activation(n_t[:].rearrange("p k n -> p (k n)"), b_misc[:], ACT.Copy
                                             ).then_inc(s_n2te, 1)

            def evac_turn(b, u, cur, prev):
                v = u - 4
                if v % 2 == 0 or not (cur if v >= 0 else prev):
                    return
                bb = b if v >= 0 else b - 1
                v = v % UNITS
                hf = v // 8
                act.wait_ge(s_T, bb * UNITS + v + 1)
                if cur_b_not_first(b, u, prev):
                    act.wait_ge(s_pv, 2 * (bb - 1) + hf + 1)
                kind, h0, n = unit(v)
                if kind == "B":
                    nc.scalar.activation(pt_img[:, hf, h0 % HH:h0 % HH + 2, 1:3, :],
                                         b_turn[1][:].rearrange("p (h c q) -> p h c q", h=2, c=2),
                                         ACT.Copy).then_inc(s_te_a, 1)
                else:
                    g = h0 // 4 % 2
                    nc.scalar.activation(pt_txt[:, hf, g, 0:2, :], b_turn[1][:, 0:2 * P].rearrange(
                        "p (c q) -> p c q", c=2), ACT.Copy)
                    nc.scalar.activation(pt_txt[0:NT, hf, g, 2, :], b_turn[1][0:NT, 2 * P:3 * P], ACT.Copy
                                         ).then_inc(s_te_a, 1)

            def cur_b_not_first(b, u, prev):
                if u >= 4:
                    return prev
                return not (isinstance(b, int) and b == 1)

            def evac_ctx(b, hf):
                act.wait_ge(s_pv, 2 * b + hf + 1)
                if not (isinstance(b, int) and b == 0):
                    act.wait_ge(s_o, b)
                nc.scalar.activation(ctx_t[:, hf, :], b_ctx[:, 0:NI], ACT.Copy)
                nc.scalar.activation(ctx_txt[:, hf, b, :], b_ctx[:, NI:T], ACT.Copy).then_inc(s_cx, 1)

            body(0, True, False)
            body(1, True, True)
            with act.Fori(2, B) as b:
                body(b, True, True)
            body(B, False, True)
            act.wait_ge(s_n2t, B + 1)
            nc.scalar.activation(n_t[:].rearrange("p k n -> p (k n)"), b_misc[:], ACT.Copy).then_inc(s_n2te, 1)
            tail_act(act)

        @block.vector
        def _(dve):
            def scan(b, s):
                dve.wait_ge(s_chunk[s], 16 * (b + 1))
                nc.vector.tensor_reduce(part[:, bass.ds(b * 4 + s, 1)], chunk[:, s, :], AX.X, ALU.add,
                                        apply_absolute_value=True).then_inc(s_scan_d, 1)

            def norm_stats(src, via, into):
                for i in range(IT):
                    nc.vector.bn_stats(via[:, i, :], src[i])
                dve.drain()
                for i in range(IT):
                    last = nc.vector.bn_aggr(into[:, i, :], via[:, i, :])
                return last

            def embed_stats(b, par):
                dve.wait_ge(s_tok, b + 1)
                norm_stats([b_emb[par][:, i * D:i * D + D] for i in range(IT)], stats_emb, mv_emb).then_inc(s_mv, 1)

            def embed_norm(b, par):
                dve.wait_ge(s_rstd, 2 * b + 1)
                for i in range(IT):
                    nc.vector.tensor_scalar(hr[:, i, :], b_emb[par][:, i * D:i * D + D], mv_emb[:, i, 0:1],
                                            rstd_emb[:, i:i + 1], ALU.subtract, ALU.mult)
                dve.drain()
                nc.vector.tensor_tensor(h_all[:, bass.ds(b * IT, IT), :], hr[:],
                                        gam_tok[:, None, :].broadcast_to([P, IT, D]), ALU.mult)
                dve.drain()
                h_stats(b * IT)

            def h_stats(t0):
                norm_stats([h_all[:, t0 + i, :] for i in range(IT)], stats, mv).then_inc(s_mv, 1)

            def attention_norm(t0, count, b):
                dve.wait_ge(s_rstd, count)
                for i in range(IT):
                    last = nc.vector.tensor_scalar(n1[:, i, :], h_all[:, t0 + i, :], mv[:, i, 0:1],
                                                   rstd[:, i:i + 1], ALU.subtract, ALU.mult)
                last.then_inc(s_n1, 1)

            def front(b, par, last):
                if not last:
                    embed_stats(b + 1, 1 - par)
                attention_norm(b * IT, 2 * b + 2, b)
                scan(b, 0)
                if not last:
                    embed_norm(b + 1, 1 - par)
                scan(b, 1)
                dve.wait_ge(s_k, b + 1)
                nc.vector.tensor_copy(k_all[:, :, b, 0:NI], b_score[1][:].rearrange("p (f n) -> p f n", f=2)
                                      ).then_inc(s_ke, 1)
                dve.wait_ge(s_v, b + 1)
                nc.vector.tensor_copy(v_all[:, b, 0:2, :], b_score[2][:].rearrange("p (k d) -> p k d", k=2)
                                      ).then_inc(s_ve, 1)

            dve.wait_ge(s_const, NCONST)
            embed_stats(0, 0)
            embed_norm(0, 0)
            with dve.Fori(0, B // 2 - 1) as i:
                front(i * 2, 0, False)
                front(i * 2 + 1, 1, False)
            front(B - 2, 0, False)
            front(B - 1, 1, True)

            dve.wait_ge(s_scan_a, 2 * B)
            dve.drain()
            nc.vector.tensor_reduce(psum_abs[:], part[:], AX.X, ALU.add).then_inc(s_abs, 1)
            dve.wait_ge(s_scl, 1)
            nc.vector.tensor_scalar(scl[:, 0:1], b_misc[:, 0:1], 1.0 / (V * D), EPS, ALU.mult, ALU.max)
            dve.drain()
            nc.vector.reciprocal(scl[:, 1:2], scl[:, 0:1])
            dve.drain()
            nc.vector.reciprocal(scl[:, 2:3], scl[:, 1:2])
            dve.wait_ge(s_emb, 16 * TT)
            dve.drain()
            nc.vector.tensor_scalar(hr[:], emb[:], scl[:, 1:2], 0.5, ALU.mult, ALU.is_gt)
            nc.vector.tensor_scalar(n1[:], emb[:], scl[:, 1:2], -0.5, ALU.mult, ALU.is_lt)
            dve.drain()
            nc.vector.tensor_tensor(hr[:], hr[:], n1[:], ALU.subtract)
            dve.drain()
            nc.vector.tensor_scalar(h_all[:, B * IT:TILES, :], hr[:], scl[:, 2:3], None, ALU.mult)
            dve.drain()
            h_stats(B * IT)
            attention_norm(B * IT, 2 * B + 1, B)
            dve.wait_ge(s_k, B + 1)
            nc.vector.tensor_copy(k_all[:, :, :, NI:T], b_score[1][:].rearrange("p (f b n) -> p f b n", f=2, b=B)
                                  ).then_inc(s_ke, 1)
            dve.wait_ge(s_v, B + 1)
            for i, bk in enumerate((b_score[2], b_score[3], b_misc, b_turn[1])):
                last = nc.vector.tensor_copy(v_all[0:NT, 2 * i:2 * i + 2, 2, :],
                                             bk[0:NT, :].rearrange("p (k d) -> p k d", k=2))
            last.then_inc(s_ve, 1)

            def body(b, cur, prev):
                for u in range(UNITS):
                    kind, h0, n = unit(u)
                    if cur:
                        dve.wait_ge(s_S, b * UNITS + u + 1)
                        src = b_score[u % 4][:, 0:T] if kind == "D" else \
                            b_score[u % 4][:].rearrange("p (h k) -> p h k", h=n)
                        m = 1 if kind == "D" else n
                        nc.vector.tensor_reduce(negm[:, u % 4, 0:m], src, AX.X, ALU.max, negate=True
                                                ).then_inc(s_max, 1)
                        if u > 0:
                            recip(b, u - 1)
                    if u == 0 and prev:
                        recip(b - 1, UNITS - 1)
                    evac_turn(b, u, cur, prev)
                    if prev and u == AT_SUM:
                        after_attention(b - 1, (b - 1) * IT)
                    if prev and u == AT_NORM + 1:
                        after_norm(b - 1, (b - 1) * IT)
                    if prev and u == 15:
                        router_logits(b - 1, (b - 1) * IT)

            def recip(b, u):
                kind, _, n = unit(u)
                m = 1 if kind == "D" else n
                dve.wait_ge(s_exp, b * UNITS + u + 1)
                if not (isinstance(b, int) and b == 0 and u < 4):
                    dve.wait_ge(s_P, b * UNITS + u - 3)
                nc.vector.reciprocal(rsum[:, u % 4, 0:m], psums[:, u % 4, 0:m]).then_inc(s_rc, 1)

            def evac_turn(b, u, cur, prev):
                v = u - 4
                if v % 2 or not (cur if v >= 0 else prev):
                    return
                bb = b if v >= 0 else b - 1
                not_first = prev if v >= 0 else not (isinstance(b, int) and b == 1)
                v = v % UNITS
                hf = v // 8
                dve.wait_ge(s_T, bb * UNITS + v + 1)
                if not_first:
                    dve.wait_ge(s_pv, 2 * (bb - 1) + hf + 1)
                kind, h0, n = unit(v)
                if kind == "A":
                    nc.vector.tensor_copy(pt_img[:, hf, h0 % HH:h0 % HH + 4, 0, :],
                                          b_turn[0][:].rearrange("p (h q) -> p h q", h=4)).then_inc(s_te_d, 1)
                else:
                    nc.vector.tensor_copy(pt_img[:, hf, h0 % HH:h0 % HH + 2, 1:3, :],
                                          b_turn[0][:].rearrange("p (h c q) -> p h c q", h=2, c=2)
                                          ).then_inc(s_te_d, 1)

            def after_attention(b, t0):
                dve.wait_ge(s_o, b + 1)
                for i in range(IT):
                    nc.vector.tensor_tensor(h_all[:, t0 + i, :], b_misc[:, i * D:i * D + D], h_all[:, t0 + i, :],
                                            ALU.add)
                dve.drain()
                for i in range(IT):
                    nc.vector.bn_stats(stats[:, i, :], h_all[:, t0 + i, :])
                dve.drain()
                for i in range(IT):
                    last = nc.vector.bn_aggr(mv[:, i, :], stats[:, i, :])
                dve.drain()
                nc.vector.tensor_copy(mv2[:, bass.ds(t0, IT), :], mv[:]).then_inc(s_mv2, 1)

            def after_norm(b, t0):
                dve.wait_ge(s_rstd2, b + 1)
                if not (isinstance(b, int) and b == 0):
                    dve.wait_ge(s_n2st, 16 * b)
                nc.vector.tensor_copy(rstd2[:, bass.ds(t0, IT)], rstd[:])
                for i in range(IT):
                    last = nc.vector.tensor_scalar(n1[:, i, :], h_all[:, t0 + i, :], mv[:, i, 0:1],
                                                   rstd[:, i:i + 1], ALU.subtract, ALU.mult)
                last.then_inc(s_n2, 1)

            def router_logits(b, t0):
                dve.wait_ge(s_lg, b + 1)
                for i in range(IT):
                    last = nc.vector.tensor_tensor(logit[:, t0 + i, :], b_misc[:, i * E:i * E + E], br_bc[:], ALU.add)
                last.then_inc(s_lge, 1)

            body(0, True, False)
            body(1, True, True)
            with dve.Fori(2, B) as b:
                body(b, True, True)
            body(B, False, True)
            after_attention(B, B * IT)
            after_norm(B, B * IT)
            router_logits(B, B * IT)
            tail_dve(dve)

        @block.tensor
        def _(pe):
            pe.wait_ge(s_w, 16 * 3)

            def transposes(src, dst):
                for k in range(DC):
                    for i in range(IT):
                        last = nc.tensor.transpose(dst[:, k * NI + i * P:k * NI + i * P + P],
                                                   src[:, i, k * P:k * P + P], ident[:])
                return last

            def projections(b, embed_next=None):
                pe.wait_ge(s_n1, b + 1)
                transposes(n1, b_turn[0]).then_inc(s_nt, 1)
                if embed_next:
                    embed_next()
                pe.wait_ge(s_nte, b + 1)
                for k in range(DC):
                    last = nc.tensor.matmul(b_ctx[0:LAT, 0:NI], wdkv_sb[:, k, :], n_t[:, k, :],
                                            start=(k == 0), stop=(k == DC - 1))
                last.then_inc(s_c, 1)
                if not (isinstance(b, int) and b == 0):
                    pe.wait_ge(s_qe, b)
                    pe.wait_ge(s_ke, b)
                    pe.wait_ge(s_ve, b)
                for f in range(2):
                    for k in range(DC):
                        last = nc.tensor.matmul(b_score[0][:, f * NI:f * NI + NI], wq_sb[:, k, f * P:f * P + P],
                                                n_t[:, k, :], start=(k == 0), stop=(k == DC - 1))
                last.then_inc(s_q, 1)
                pe.wait_ge(s_ce, b + 1)
                for f in range(2):
                    last = nc.tensor.matmul(b_score[1][:, f * NI:f * NI + NI], wuk_sb[:, f * P:f * P + P], c_t[:],
                                            start=True, stop=True)
                last.then_inc(s_k, 1)

            pe.wait_ge(s_const, NCONST)
            pe.wait_ge(s_id, 1)

            def embed(b, par):
                pe.wait_ge(s_xt[par], (b - par) * 16 + 32)
                for t in range(IT):
                    for kc, (_, fn) in enumerate(KF):
                        last = nc.tensor.matmul(b_emb[par][:, t * D:t * D + D], xt[0:fn, par, kc, t * P:t * P + P],
                                                wtok[0:fn, kc, :], start=(kc == 0), stop=(kc == len(KF) - 1))
                last.then_inc(s_tok, 1)

            def values(b):
                for t in range(IT):
                    last = nc.tensor.matmul(b_score[2][:, t * D:t * D + D], c_t[:, t * P:t * P + P], wuv_sb[:],
                                            start=True, stop=True)
                last.then_inc(s_v, 1)

            embed(0, 0)
            embed(1, 1)
            projections(0, embed_next=lambda: embed(2, 0))
            values(0)
            projections(1, embed_next=lambda: embed(3, 1))
            values(1)
            with pe.Fori(1, B // 2 - 1) as i:
                for par in range(2):
                    b = i * 2 + par
                    projections(b, embed_next=lambda: embed(b + 2, par))
                    values(b)
            for b in (B - 2, B - 1):
                projections(b)
                values(b)

            pe.wait_ge(s_abs, 1)
            nc.tensor.matmul(b_misc[:, 0:1], ones[:], psum_abs[:], start=True, stop=True).then_inc(s_scl, 1)
            projections(B)
            for i, bk in enumerate((b_score[2], b_score[3], b_misc, b_turn[1])):
                for j in range(2):
                    b = 2 * i + j
                    last = nc.tensor.matmul(bk[0:NT, j * D:j * D + D], c_t[:, b * NT:b * NT + NT], wuv_sb[:],
                                            start=True, stop=True)
            last.then_inc(s_v, 1)
            pe.wait_ge(s_qe, B + 1)
            pe.wait_ge(s_ke, B + 1)
            pe.wait_ge(s_ve, B + 1)

            def scores(b, u, first):
                kind, h0, n = unit(u)
                hf = h0 // HH
                if not (first and u < 4):
                    pe.wait_ge(s_exp, b * UNITS + u - 3)
                if u % 8 == 0:
                    pe.wait_ge(s_qm[hf], (b + 1) * (16 * (HH + 1)))
                bk = b_score[u % 4]
                mask = {"A": mask_a, "B": mask_b, "C": mask_b}.get(kind)
                if kind == "D":
                    nc.tensor.matmul(bk[:, 0:T], ident_bf[:], mask_d[:], start=True, stop=False,
                                     skip_group_check=True)
                else:
                    nc.tensor.matmul(bk[:], ident_bf[:], mask[:].rearrange("p h k -> p (h k)"), start=True,
                                     stop=False, skip_group_check=True)
                for j in range(n):
                    s = (h0 + j) % HH
                    if kind == "A":
                        last = nc.tensor.matmul(bk[:, j * P:j * P + P], q_mask[:, hf, s, 0:P],
                                                k_cur[:, hf, 0:P], start=False, stop=True, skip_group_check=True)
                    elif kind == "D":
                        last = nc.tensor.matmul(bk[NT * j:NT * j + NT, 0:T], q_mask[:, hf, s, NI:T],
                                                k_cur[:, hf, :], start=False, stop=True, skip_group_check=True)
                    else:
                        last = nc.tensor.matmul(bk[:, j * NI:j * NI + NI], q_mask[:, hf, s, P:NI],
                                                k_cur[:, hf, 0:NI], start=False, stop=True, skip_group_check=True)
                last.then_inc(s_S, 1)

            def turn(b, u, first):
                kind, h0, n = unit(u)
                pe.wait_ge(s_P, b * UNITS + u + 1)
                if not (first and u < 2):
                    pe.wait_ge(s_te_d if u % 2 == 0 else s_te_a, b * 8 + u // 2)
                bk = b_turn[u % 2]
                if kind == "D":
                    nc.tensor.transpose(bk[:, 0:P], probs[:, u % 4, 0:P], ident[:])
                    nc.tensor.transpose(bk[:, P:2 * P], probs[:, u % 4, P:2 * P], ident[:])
                    last = nc.tensor.transpose(bk[0:NT, 2 * P:3 * P], probs[:, u % 4, NI:T], ident[:])
                else:
                    for j in range(4):
                        last = nc.tensor.transpose(bk[:, j * P:j * P + P], probs[:, u % 4, j * P:j * P + P], ident[:])
                last.then_inc(s_T, 1)

            def weigh_values(b, hf, first, step):
                if step == 0:
                    pe.wait_ge(s_te_d, b * 8 + 4 * hf + 4)
                    pe.wait_ge(s_te_a, b * 8 + 4 * hf + 4)
                    pe.wait_ge(s_vm, b * 2 + hf + 1)
                    if not (first and hf == 0):
                        pe.wait_ge(s_cx, b * 2 + hf)
                for kt in {0: (0,), 1: (1,), 2: (0, 1, 2)}[step]:
                    for par in range(2):
                        for j in range(4):
                            n = P if kt < 2 else NT
                            h = 2 * j + par
                            w = v_mask[0:n, kt, par, hf * P + 32 * j:hf * P + 32 * j + 32]
                            r = slice(32 * j, 32 * j + 32)
                            if step == 0:
                                nc.tensor.matmul(b_ctx[r, 0:NI], w, pt_img[:, hf, h, 0:2, :],
                                                 start=(par == 0), stop=False, skip_group_check=True)
                            elif step == 1:
                                nc.tensor.matmul(b_ctx[r, P:NI], w, pt_img[:, hf, h, 2, :],
                                                 start=False, stop=False, skip_group_check=True)
                            else:
                                last = nc.tensor.matmul(
                                    b_ctx[r, NI:T], w, pt_txt[0:n, hf, h // 4, kt, NT * (h % 4):NT * (h % 4) + NT],
                                    start=False, stop=(kt == 2 and par == 1), skip_group_check=True)
                if step == 2:
                    last.then_inc(s_pv, 1)

            def project_out(b, src, first):
                pe.wait_ge(s_cx, b * 2 + 2)
                if not first:
                    pe.wait_ge(s_lge, b)
                for i in range(IT):
                    for f in range(2):
                        last = nc.tensor.matmul(b_misc[:, i * D:i * D + D], src(f, i), wo_sb[:, f, :],
                                                start=(f == 0), stop=(f == 1))
                last.then_inc(s_o, 1)

            def turn_norm(b):
                pe.wait_ge(s_n2, b + 1)
                transposes(n1, b_misc).then_inc(s_n2t, 1)

            def router(b):
                pe.wait_ge(s_n2te, b + 1)
                for i in range(IT):
                    for k in range(DC):
                        last = nc.tensor.matmul(b_misc[:, i * E:i * E + E], n_t[:, k, i * P:i * P + P], wr_sb[:, k, :],
                                                start=(k == 0), stop=(k == DC - 1))
                last.then_inc(s_lg, 1)

            def body(b, cur, prev):
                for u in range(UNITS):
                    if cur:
                        scores(b, u, not prev)
                    if u < LAG and prev:
                        turn(b - 1, UNITS - LAG + u, False)
                    if u >= LAG and cur:
                        turn(b, u - LAG, not prev)
                    if u in AT_PV1 and prev:
                        weigh_values(b - 1, 1, False, AT_PV1.index(u))
                    if u in AT_PV0 and cur:
                        weigh_values(b, 0, not prev, AT_PV0.index(u))
                    if u == AT_OUT and prev:
                        project_out(b - 1, lambda f, i: ctx_t[:, f, i * P:i * P + P], isinstance(b, int) and b == 1)
                    if u == AT_N2T and prev:
                        turn_norm(b - 1)
                    if u == AT_ROUTE and prev:
                        router(b - 1)

            body(0, True, False)
            body(1, True, True)
            with pe.Fori(2, B) as b:
                body(b, True, True)
            body(B, False, True)
            pe.wait_ge(s_lge, B)
            for i in range(TT):
                for f in range(2):
                    last = nc.tensor.matmul(b_misc[:, i * D:i * D + D],
                                            ctx_txt[:, f, i * PB:i * PB + PB, :].rearrange("p b n -> p (b n)"),
                                            wo_sb[:, f, :], start=(f == 0), stop=(f == 1))
            last.then_inc(s_o, 1)
            turn_norm(B)
            router(B)
            tail_pe(pe)


def kernel(**inputs):
    import numpy as np
    import concourse.bacc as bacc
    from concourse.bass_utils import run_bass_kernel_spmd

    lay = np.ascontiguousarray
    x = np.asarray(inputs["x"])
    B, C, HT, WD = x.shape
    p = 8
    rows, cols = HT // p, WD // p
    w1, w2 = np.asarray(inputs["L0_ffn_W1"]), np.asarray(inputs["L0_ffn_W2"])
    E, FF, D = w1.shape
    args = {
        "x_patches": x.reshape(B, C, rows, p, cols, p).transpose(0, 1, 3, 5, 2, 4).reshape(B, C * p * p, rows * cols),
        "text_ids": np.asarray(inputs["x_txt"]).reshape(-1, P).T,
        "tok_w": inputs["L0_tok_W"],
        "tok_gamma": np.asarray(inputs["L0_tok_gamma"]).reshape(1, -1),
        "table": inputs["L0_txt_weight"],
        "w_dkv": inputs["L0_attn_W_DKV"],
        "w_uk": inputs["L0_attn_W_UK"],
        "w_uv": inputs["L0_attn_W_UV"],
        "w_uq": inputs["L0_attn_W_UQ"],
        "w_o": inputs["L0_attn_W_O"],
        "w_router": np.asarray(inputs["L0_ffn_Wr"]).T.reshape(D // P, P, E).transpose(1, 0, 2),
        "b_router": np.asarray(inputs["L0_ffn_br"]).reshape(1, -1),
        "w1": w1.transpose(2, 0, 1).reshape(D // P, P, E, FF).transpose(1, 2, 0, 3),
        "b1": np.asarray(inputs["L0_ffn_b1"]).reshape(E, FF // P, P).transpose(2, 0, 1),
        "w2": w2.transpose(2, 0, 1).reshape(FF // P, P, E, D).transpose(1, 2, 0, 3),
        "b2": np.asarray(inputs["L0_ffn_b2"]).reshape(1, -1),
        "gamma": np.asarray(inputs["L0_ffn_gamma"]).reshape(1, -1),
        "beta": np.asarray(inputs["L0_ffn_beta"]).reshape(1, -1),
    }
    nc = bacc.Bacc("TRN2", target_bir_lowering=False, num_devices=1)
    arrays, aps = {}, {}
    for name, a in args.items():
        arrays[name] = lay(np.asarray(a))
        aps[name] = nc.dram_tensor(name, arrays[name].shape, mybir.dt.from_np(arrays[name].dtype),
                                   kind="ExternalInput").ap()
    T = rows * cols + np.asarray(inputs["x_txt"]).shape[1]
    out = nc.dram_tensor("out", (B, T, D), F32, kind="ExternalOutput").ap()
    early_fusion_kernel(nc, out=out, **aps)
    return run_bass_kernel_spmd(nc, [arrays], core_ids=[0]).results[0]["out"]
```

```python
from contextlib import ExitStack

import concourse.bass as bass
from concourse import mybir

F32 = mybir.dt.float32
BF16 = mybir.dt.bfloat16
I32 = mybir.dt.int32
ALU = mybir.AluOpType
ACT = mybir.ActivationFunctionType
AX = mybir.AxisListType

P = 128
EPS = 1e-5
NEG = -1e30


def early_fusion_kernel(nc, x_patches, text_ids, tok_w, tok_gamma, table, w_dkv, w_uk, w_uv, w_uq, w_o,
                        w_router, b_router, w1, b1, w2, b2, gamma, beta, out):
    B, FEAT, NI = x_patches.shape
    D = tok_w.shape[1]
    V = table.shape[0]
    NT = text_ids.shape[0] * text_ids.shape[1] // B
    T = NI + NT
    LAT = w_dkv.shape[1]
    HD = 16
    H = D // HD
    E, FF = w1.shape[1], w1.shape[3]
    DC, FC = D // P, FF // P
    IT = NI // P
    TILES = B * T // P
    TT = TILES - B * IT
    PB = P // NT
    TOP = 2
    NBLK = (TOP * TILES * P + E * (P - 1)) // P
    KF = [(0, P), (P, P), (2 * P, FEAT - 2 * P)]
    CHUNK = V * D // P // 32
    NCH = 32
    HH = H // 2
    assert D == 256 and NI == 256 and T == 288 and H == 16 and P // HD == HH and NBLK % 2 == 1

    ctx = ExitStack()
    with ctx:
        def sb(name, shape, dt=F32):
            return ctx.enter_context(nc.sbuf_tensor(name, shape, dt))

        def sem(name):
            return ctx.enter_context(nc.semaphore(name))

        bank = [ctx.enter_context(nc.psum_tensor(f"bank{i}", [P, 512], F32)) for i in range(8)]
        b_score, b_turn, b_ctx, b_misc = bank[0:4], bank[4:6], bank[6], bank[7]
        b_text_v = (b_score[2], b_score[3], b_turn[0], b_turn[1])
        b_emb = (b_misc, b_turn[1])

        n2_dram = nc.dram_tensor("n2_rows", [TILES * P, D], F32).ap()
        PAIRS = TOP * TILES * P
        qk_dram = nc.dram_tensor("qk_parts", [B, 6, D, NI], BF16).ap()
        Q_PART, K_PART = (0, 0, 0, 1, 1, 1, 2, 2), (3, 4, 5, 3, 4, 5, 3, 4)
        y_dram = nc.dram_tensor("expert_rows", [PAIRS + NBLK * P, D], F32).ap()

        region = sb("region", [P, E * DC * FF + E * FC * D])
        w1_sb = region[:, 0:E * DC * FF].rearrange("p (e k f) -> p e k f", e=E, k=DC)
        w2_sb = region[:, E * DC * FF:].rearrange("p (e c d) -> p e c d", e=E, c=FC)
        chunk = region[:, 0:2 * CHUNK].rearrange("p (s c) -> p s c", s=2)
        o = E * DC * FF
        q_text = region[:, o:o + 2 * B * NT].rearrange("p (f b t) -> p f b t", f=2, b=B)
        oo = o + 2 * B * NT
        rest = region[:, oo:oo + 4 * NI].rearrange("p (c x) -> p c x", c=2)
        oo += 4 * NI
        parts = [region[:, oo:oo + 6 * NI].bitcast(BF16).rearrange("p (c a x) -> p c a x", c=2, a=3)]
        oo += 6 * NI
        mask_a = region[:, oo:oo + 256].bitcast(BF16).rearrange("p (h k) -> p h k", h=4)
        mask_b = region[:, oo + 256:oo + 512].bitcast(BF16).rearrange("p (h k) -> p h k", h=2)
        assert oo + 512 <= o + 2 * B * T
        k_all = region[:, o + 2 * B * T:o + 4 * B * T].rearrange("p (f b t) -> p f b t", f=2, b=B)
        v_all = region[:, o + 4 * B * T:o + 4 * B * T + B * 3 * D].rearrange("p (b k d) -> p b k d", b=B, k=3)

        o += 4 * B * T + B * 3 * D
        hr = region[:, o:o + IT * D].rearrange("p (t d) -> p t d", t=IT)
        k_cur = region[:, o:o + 2 * T].rearrange("p (f t) -> p f t", f=2)

        h_all = sb("h_all", [P, TILES, D])
        scratch = sb("scratch", [P, E * FF])
        o = 2 * HH * NI
        q_st = scratch[:, 0:o // 2].bitcast(BF16).rearrange("p (f s t) -> p f s t", f=2, s=HH)
        k_st = scratch[:, o // 2:o].bitcast(BF16).rearrange("p (f s t) -> p f s t", f=2, s=HH)
        probs = scratch[:, o:o + 4 * 512].rearrange("p (s c) -> p s c", s=4)
        parts.append(scratch[:, o:o + 6 * NI].bitcast(BF16).rearrange("p (c a x) -> p c a x", c=2, a=3))
        o += 4 * 512
        v_mask = scratch[:, o:o + 3 * 2 * D].rearrange("p (k a d) -> p k a d", k=3, a=2)
        o = -(-2 * CHUNK // (DC * FF)) * DC * FF
        O_TXT = o
        q_txt = region[:, o:o + 2 * HH * B * NT].rearrange("p (f s b n) -> p f s b n", f=2, s=HH, b=B)
        o += 2 * HH * B * NT
        O_PT = o
        pt_img = region[:, o:o + 2 * HH * 3 * P].rearrange("p (f h c q) -> p f h c q", f=2, h=HH, c=3)
        o += 2 * HH * 3 * P
        pt_txt = region[:, o:o + 2 * 2 * 3 * P].rearrange("p (f g c q) -> p f g c q", f=2, g=2, c=3)

        o += 2 * 2 * 3 * P
        mask_d = region[:, o:o + T // 2].bitcast(BF16)
        assert o + T // 2 <= E * DC * FF

        work = sb("work", [P, 6544])
        used = [0]

        def carve(rows, *shape):
            n = 1
            for d in shape:
                n *= d
            v = work[0:rows, used[0]:used[0] + n]
            used[0] += n
            if len(shape) == 1:
                return v
            names = "abc"[:len(shape)]
            return v.rearrange(f"p ({' '.join(names)}) -> p {' '.join(names)}", **dict(zip(names, shape)))

        ctx_t = carve(P, 2, NI)
        ctx_txt = carve(P, 2, B, NT)
        xt = carve(P, 2, 3, NI)
        wtok = carve(P, 3, D)
        wq_sb = carve(P, DC, D)
        wo_sb = carve(P, DC, D)
        wdkv_sb = carve(P, DC, LAT)
        wuk_sb = carve(LAT, D)
        wuv_sb = carve(LAT, D)
        wr_sb = carve(P, DC, E)
        n_t = carve(P, DC, NI)
        c_t = carve(LAT, NI)
        gam_tok = carve(P, D)
        n1 = carve(P, IT, D)
        emb, tern = xt[:, 0, 0:2, :], xt[:, 1, 0:2, :]
        low = wtok[:, 0:2, :]
        q_cur = wtok.rearrange("p k d -> p (k d)")[:, 0:2 * HH * NT].rearrange("p (f s n) -> p f s n", f=2, s=HH)
        br_bc = sb("br_bc", [P, E])
        stats = sb("stats", [P, IT, 6])
        mv = sb("mv", [P, IT, 2])
        mv_emb = sb("mv_emb", [P, IT, 2])
        vare_emb = sb("vare_emb", [P, IT])
        stats_emb = sb("stats_emb", [P, IT, 6])
        vare = sb("vare", [P, IT])
        rstd = sb("rstd", [P, IT])
        rstd_emb = sb("rstd_emb", [P, IT])
        neghalf = sb("neghalf", [P, IT])
        eps = sb("eps", [P, IT])
        ident = sb("ident", [P, P])
        ident_bf = sb("ident_bf", [P, P], BF16)
        negm = sb("negm", [P, 4, 4])
        psums = sb("psums", [P, 4, 4])
        rsum = sb("rsum", [P, 4, 4])
        part = sb("part", [P, 2 * B + 4 * B])
        psum_abs = sb("psum_abs", [P, 1])
        scl = sb("scl", [P, 4])
        ones = sb("ones", [P, P])
        tid = sb("tid", [P, TT], I32)
        logit = sb("logit", [P, TILES, E])

        s_const, s_w, s_id, s_mask = sem("s_const"), sem("s_w"), sem("s_id"), sem("s_mask")
        s_chunk = [sem(f"s_chunk{i}") for i in range(2)]
        s_scan = [sem(f"s_scan{i}") for i in range(2)]
        s_xt = [sem(f"s_xt{i}") for i in range(2)]
        s_tok, s_mv, s_rstd = sem("s_tok"), sem("s_mv"), sem("s_rstd")
        s_n1, s_nt, s_nte, s_c, s_ce = sem("s_n1"), sem("s_nt"), sem("s_nte"), sem("s_c"), sem("s_ce")
        s_q, s_qe, s_k, s_ke, s_v, s_ve = (sem(f"s_{n}") for n in ("q", "qe", "k", "ke", "v", "ve"))
        s_emb, s_abs, s_scl, s_sclr = sem("s_emb"), sem("s_abs"), sem("s_scl"), sem("s_sclr")
        s_tq, s_tqk, s_gam = sem("s_tq"), sem("s_tqk"), sem("s_gam")
        s_k1, s_rq, s_parts = sem("s_k1"), sem("s_rq"), sem("s_parts")
        s_qst = [sem(f"s_qst{i}") for i in range(2)]
        s_qm = [sem(f"s_qm{i}") for i in range(2)]
        s_vm, s_S, s_max, s_exp, s_rc, s_P, s_T = (sem(f"s_{n}") for n in ("vm", "S", "max", "exp", "rc", "P", "T"))
        s_te_d, s_te_a, s_pv, s_cx, s_o = (sem(f"s_{n}") for n in ("te_d", "te_a", "pv", "cx", "o"))
        s_mv2, s_rstd2, s_n2, s_n2t, s_n2te, s_lg, s_lge, s_n2st = (
            sem(f"s_{n}") for n in ("mv2", "rstd2", "n2", "n2t", "n2te", "lg", "lge", "n2st"))

        NCONST = 8 * 16
        SC = float(HD) ** -0.5
        block = ctx.enter_context(nc.Block())
        UNITS = 12
        TUNITS = 4
        LAG, TLAG = 3, 2
        TXT = B * UNITS

        AT_PV0, AT_PV1 = (7, 7, 10, 10), (1, 2, 4, 4)
        AT_OUT, AT_SUM, AT_NORM, AT_N2T, AT_ROUTE = 6, 6, 7, 9, 11
        AT_SCAN = (3, 4, 9, 10)
        AT_STATS = 7
        AT_FILL = (2, 7)
        AT_ABS, AT_TERN, AT_TEXT = 0, 1, 7

        def unit(u):
            g, kind = u // 3, "ABC"[u % 3]
            return kind, 4 * g + (2 if kind == "C" else 0), {"A": 4, "B": 2, "C": 2}[kind]

        def load_x(eng, b, par):
            eng.dma_start(xt[:, par, 0:2, :], x_patches[b, 0:2 * P, :].rearrange("(k p) n -> p k n", p=P)
                          ).then_inc(s_xt[par], 16)
            eng.dma_start(xt[0:KF[2][1], par, 2, :], x_patches[b, 2 * P:FEAT, :]).then_inc(s_xt[par], 16)

        def turned_image(kind, h0, bk):
            hf, s = h0 // HH, h0 % HH
            if kind == "A":
                return pt_img[:, hf, s:s + 4, 0, :], bk[:].rearrange("p (h q) -> p h q", h=4)
            return pt_img[:, hf, s:s + 2, 1:3, :], bk[:].rearrange("p (h c q) -> p h c q", h=2, c=2)

        NV = TILES * E
        W1_EARLY = O_TXT // (DC * FF)
        W1_TXT = range(W1_EARLY, O_PT // (DC * FF))
        W1_MID = range(O_PT // (DC * FF), (O_PT + 2 * HH * 3 * P) // (DC * FF))
        W2_EARLY = 2 * B * T // (FC * D)
        W2_KEYS = 4 * B * T // (FC * D)
        W2_VALUES = (4 * B * T + B * 3 * D) // (FC * D)
        one_slot = work[:, 0:2304].bitcast(BF16).rearrange("p (n s) -> p n s", n=TOP * TILES)
        one_blk = work[:, 2304:2304 + TOP * TILES * NBLK].bitcast(BF16).rearrange(
            "p (n a b) -> p n a b", n=TOP * TILES, a=2)
        tmp = [work[:, 3888 + i * NV:3888 + (i + 1) * NV] for i in range(13)]
        keep = work[:, 5776:6032]
        gather_idx = keep[:, 0:NBLK].bitcast(I32)
        expert_of = keep[:, NBLK:2 * NBLK].bitcast(I32)
        scatter_idx = keep[:, 2 * NBLK:3 * NBLK].bitcast(I32)
        o = 3 * NBLK
        top_w = keep[:, o:o + TOP * TILES].rearrange("p (k t) -> p k t", k=TOP)
        o += TOP * TILES
        gi = keep[:, o:o + 2].bitcast(I32)
        RING = 3
        GROUPS = TILES // IT
        o += 2
        si = keep[:, o:o + 2].bitcast(I32)
        o += 2
        mvf = keep[:, o:o + RING * IT * 2].rearrange("p (s i k) -> p s i k", s=RING, i=IT)
        o += RING * IT * 2
        varf = keep[:, o:o + RING * IT].rearrange("p (s i) -> p s i", s=RING)
        o += RING * IT
        rstdf = keep[:, o:o + RING * IT].rearrange("p (s i) -> p s i", s=RING)
        o += RING * IT
        statf = keep[:, o:o + IT * 6].rearrange("p (i k) -> p i k", i=IT)
        assert o + IT * 6 <= 256 and GROUPS % RING == 0
        gam, bet = work[:, 6032:6032 + D], work[:, 6288:6288 + D]
        h_t = work[:, 0:2 * FF].rearrange("p (s c n) -> p s c n", s=2, c=FC)
        xg = work[:, 2 * FF:2 * FF + 2 * D].rearrange("p (s d) -> p s d", s=2)
        o = 2 * FF + 2 * D
        xg_t = work[:, o:o + DC * P].rearrange("p (k n) -> p k n", k=DC)
        ys = work[:, o + D:o + 3 * D].rearrange("p (s d) -> p s d", s=2)
        b2_bc = work[:, o + 3 * D:o + 3 * D + E * D].rearrange("p (e d) -> p e d", e=E)
        w1_cur = scratch[:, 0:2 * DC * FF].rearrange("p (s k f) -> p s k f", s=2, k=DC)
        o = 2 * DC * FF
        b1_sb = scratch[:, o:o + E * FC].rearrange("p (e c) -> p e c", e=E)
        o += E * FC
        b1_cur = scratch[:, o:o + 2 * FC].rearrange("p (s c) -> p s c", s=2)
        z = region[:, 0:TILES * D].rearrange("p (t d) -> p t d", t=TILES)
        o = TILES * D
        yg = region[:, o:o + RING * TOP * IT * D].rearrange("p (s k i d) -> p s k i d", s=RING, k=TOP, i=IT)
        o += RING * TOP * IT * D
        zn = region[:, o:o + RING * IT * D].rearrange("p (s i d) -> p s i d", s=RING, i=IT)
        assert o + RING * IT * D <= E * DC * FF

        s_lw, s_b2, s_dc, s_dp, s_dl, s_de = (sem(f"s_{n}") for n in ("lw", "b2", "dc", "dp", "dl", "de"))
        s_oh, s_ip, s_idx, s_blk = (sem(f"s_{n}") for n in ("oh", "ip", "idx", "blk"))
        s_xg = [sem(f"s_xg{i}") for i in range(2)]
        s_xgt, s_xgte, s_w1, s_wcur, s_ht, s_w2, s_ys = (
            sem(f"s_{n}") for n in ("xgt", "xgte", "w1", "wcur", "ht", "w2", "ys"))
        s_yst = [sem(f"s_yst{i}") for i in range(2)]
        s_g = [sem(f"s_g{i}") for i in range(RING)]
        s_ost = [sem(f"s_ost{i}") for i in range(RING)]
        s_gb, s_n2back = sem("s_gb"), sem("s_n2back")
        s_z, s_mvf, s_rf, s_zn, s_zo = (sem(f"s_{n}") for n in ("z", "mvf", "rf", "zn", "zo"))
        pref_ps, tot_ps, idx_ps = b_ctx[:, 0:NV], b_ctx[:, NV:2 * NV], b_misc[:, 0:2 * NBLK]
        hid, y_ps, xt_ps = (bank[0:2], bank[2:4]), (bank[4], bank[6]), bank[5]

        def load_w1(sp, experts):
            for e in experts:
                sp.dma_start(w1_sb[:, e], w1[:, e]).then_inc(s_lw, 16)

        def load_w2(sp, first, last):
            for e in range(first, last):
                sp.dma_start(w2_sb[:, e], w2[:, e]).then_inc(s_lw, 16)

        def tail_sp(sp):
            sp.wait_ge(s_tqk, 2 * B)
            load_w1(sp, W1_TXT)
            load_w2(sp, W2_EARLY, W2_KEYS)
            sp.wait_ge(s_vm, 4 * B)
            load_w2(sp, W2_KEYS, W2_VALUES)
            sp.wait_ge(s_pv, 4 * B)
            sp.wait_ge(s_cx, 4 * B)
            load_w1(sp, range(W1_MID[-1] + 1, E))
            load_w2(sp, W2_VALUES, E)
            sp.dma_start(b1_sb, b1).then_inc(s_lw, 16)
            sp.wait_ge(s_n2, B + 1)
            sp.dma_start(n2_dram[B * IT * P:, :].rearrange("(i p) d -> p i d", p=P), n1[:]).then_inc(s_n2st, 16)
            sp.wait_ge(s_n2st, 16 * (B + 1))
            sp.wait_ge(s_n2t, B + 1)
            sp.dma_start(gam, gamma.broadcast_to([P, D])).then_inc(s_gb, 16)
            sp.dma_start(bet, beta.broadcast_to([P, D])).then_inc(s_gb, 16)
            sp.wait_ge(s_idx, 2)
            sp.wait_ge(s_xg[0], 16)
            sp.dma_start(b2_bc, b2.broadcast_to([P, E * D])).then_inc(s_b2, 16)
            for par in range(2):
                sp.wait_ge(s_yst[par], 16 * ((NBLK + 1 - par) // 2))
            sp.wait_ge(s_w1, NBLK)

            def expert_rows(g, s, first):
                if not first:
                    sp.wait_ge(s_z, g - RING + 1)
                for k in range(TOP):
                    sp.dma_start(yg[:, s, k], y_dram[bass.ds(g * (IT * P) + k * TILES * P, IT * P), :].rearrange(
                        "(i p) d -> p i d", p=P)).then_inc(s_g[s], 16)

            for s in range(RING):
                expert_rows(s, s, True)
            with sp.Fori(1, GROUPS // RING) as i:
                for s in range(RING):
                    expert_rows(i * RING + s, s, False)

        def tail_pool(pool):
            pool.wait_ge(s_lge, B + 1)
            io_i = tmp[0][:, 0:P].bitcast(I32)
            nc.gpsimd.iota(io_i, [[1, P]], base=0, channel_multiplier=0)
            nc.gpsimd.iota(tmp[1][:, 0:1].bitcast(I32), [[0, 1]], base=0, channel_multiplier=1)
            nc.gpsimd.memset(tmp[3], 1.0)
            pool.drain()
            nc.gpsimd.tensor_copy(tmp[2][:, 0:P], io_i)
            nc.gpsimd.tensor_copy(tmp[1][:, 1:2], tmp[1][:, 0:1].bitcast(I32))
            nc.gpsimd.affine_select(tmp[4][:, 0:P], ones[:], [[1, P]], ALU.is_ge, 0.0, base=-1, channel_multiplier=-1)
            nc.gpsimd.memset(tmp[3].rearrange("p (e t) -> p e t", e=E)[:, :, 0:1], 0.0)
            pool.drain()
            nc.gpsimd.tensor_scalar(tmp[5][:, 0:E], tmp[2][:, 0:E], -1.0, float(E), ALU.mult, ALU.add)
            nc.gpsimd.tensor_scalar(tmp[5][:, E:E + TILES], tmp[2][:, 0:TILES], float(P), None, ALU.mult
                                    ).then_inc(s_dc, 1)
            pool.wait_ge(s_gb, 32)
            nc.gpsimd.tensor_tensor(h_all[:], h_all[:], bet[:, None, :].broadcast_to([P, TILES, D]), ALU.add)

            def gather(n, par, first):
                if not first:
                    pool.wait_ge(s_xgt, n - 1)
                nc.gpsimd.tensor_copy(gi[:, par:par + 1], gather_idx[:, bass.ds(n, 1)])
                pool.drain()
                nc.gpsimd.indirect_dma_start(xg[:, par, :], None, n2_dram,
                                             bass.IndirectOffsetOnAxis(gi[:, par:par + 1], 0)).then_inc(s_xg[par], 16)

            def scatter(n, par):
                pool.wait_ge(s_ys, n + 1)
                nc.gpsimd.tensor_copy(si[:, par:par + 1], scatter_idx[:, bass.ds(n, 1)])
                pool.drain()
                nc.gpsimd.indirect_dma_start(y_dram, bass.IndirectOffsetOnAxis(si[:, par:par + 1], 0),
                                             ys[:, par, :], None).then_inc(s_yst[par], 16)

            pool.wait_ge(s_idx, 1)
            pool.wait_ge(s_n2st, 16 * (B + 1))
            gather(0, 0, True)
            gather(1, 1, True)
            gather(2, 0, False)
            with pool.Fori(0, (NBLK - 3) // 2) as i:
                for par in range(2):
                    gather(i * 2 + par + 3, 1 - par, False)
                    scatter(i * 2 + par, par)
            scatter(NBLK - 3, 0)
            scatter(NBLK - 2, 1)
            scatter(NBLK - 1, 0)

            def final_rstd(g, s):
                pool.wait_ge(s_mvf, g + 1)
                nc.gpsimd.tensor_tensor(rstdf[:, s, :], varf[:, s, :], neghalf[:], ALU.pow).then_inc(s_rf, 1)

            def final_scale(g, s):
                pool.wait_ge(s_zn, g + 1)
                nc.gpsimd.tensor_tensor(zn[:, s], zn[:, s], gam[:, None, :].broadcast_to([P, IT, D]), ALU.mult)
                pool.drain()
                nc.gpsimd.tensor_tensor(zn[:, s], zn[:, s], h_all[:, bass.ds(g * IT, IT), :], ALU.add
                                        ).then_inc(s_zo, 1)

            final_rstd(0, 0)
            with pool.Fori(0, GROUPS // RING - 1) as i:
                for s in range(RING):
                    final_rstd(i * RING + s + 1, (s + 1) % RING)
                    final_scale(i * RING + s, s)
            for s in range(RING):
                if s + 1 < RING:
                    final_rstd(GROUPS - RING + s + 1, s + 1)
                final_scale(GROUPS - RING + s, s)

        def tail_act(act):
            act.wait_ge(s_dl, 1)
            nc.scalar.activation(tmp[7][:, TILES:2 * TILES], tmp[7][:, 0:TILES], ACT.Exp).then_inc(s_de, 1)

            def rows_t(n, first):
                act.wait_ge(s_xgt, n + 1)
                if not first:
                    act.wait_ge(s_w1, n)
                nc.scalar.activation(xg_t.rearrange("p k n -> p (k n)"), xt_ps[:, 0:DC * P], ACT.Copy
                                     ).then_inc(s_xgte, 1)

            def hidden(n, par, first):
                act.wait_ge(s_w1, n + 1)
                if not first:
                    act.wait_ge(s_w2, n - 1)
                for c in range(FC):
                    last = nc.scalar.activation(h_t[:, par, c, :], hid[par][c // 4][:, c % 4 * P:c % 4 * P + P],
                                                ACT.Relu, bias=b1_cur[:, par, c:c + 1])
                last.then_inc(s_ht, 1)

            act.wait_ge(s_idx, 1)
            rows_t(0, True)
            rows_t(1, False)
            hidden(0, 0, True)
            rows_t(2, False)
            hidden(1, 1, True)
            with act.Fori(1, NBLK // 2) as i:
                for par in range(2):
                    rows_t(i * 2 + par + 1, False)
                    hidden(i * 2 + par, par, False)
            hidden(NBLK - 1, 0, False)
            act.wait_ge(s_w1, NBLK)
            act.dma_start(z, n2_dram.rearrange("(t p) d -> p t d", p=P)).then_inc(s_n2back, 16)

            def store_out(b, s):
                act.wait_ge(s_zo, b + 1)
                act.dma_start(out[b, 0:NI, :].rearrange("(i p) d -> p i d", p=P), zn[:, s]).then_inc(s_ost[s], 16)

            with act.Fori(0, GROUPS // RING - 1) as i:
                for s in range(RING):
                    store_out(i * RING + s, s)
            for s in range(RING - 1):
                store_out(GROUPS - RING + s, s)
            act.wait_ge(s_zo, GROUPS)
            for i in range(TT):
                for j in range(PB):
                    act.dma_start(out[i * PB + j, NI:T, :], zn[NT * j:NT * j + NT, RING - 1, i, :]
                                  ).then_inc(s_ost[RING - 1], 16)
            for s in range(RING):
                act.wait_ge(s_ost[s], 16 * (GROUPS // RING + (TT * PB - 1 if s == RING - 1 else 0)))

        def tail_dve(dve):
            A = "p (t e) -> p t e"
            iota, e8, thr = tmp[2][:, 0:P], tmp[5][:, 0:E], tmp[5][:, E:E + TILES]
            pcol, notfirst = tmp[1][:, 1:2], tmp[3]
            ones_p = (tmp[6], tmp[8])
            cut = tmp[9]
            m = tmp[7]
            small = tmp[10]
            row8 = e8[:, None, :].broadcast_to([P, TILES, E])
            dve.wait_ge(s_dc, 1)
            dve.drain()

            def pick(src, value, onehot):
                nc.vector.tensor_reduce(value, src, AX.X, ALU.max)
                dve.drain()
                nc.vector.tensor_tensor(onehot, src, value[:, :, None].broadcast_to([P, TILES, E]), ALU.is_ge)
                dve.drain()
                nc.vector.tensor_tensor(onehot, onehot, row8, ALU.mult)
                dve.drain()
                nc.vector.tensor_reduce(small[:, 0:TILES], onehot, AX.X, ALU.max)
                dve.drain()
                nc.vector.tensor_tensor(onehot, row8, small[:, 0:TILES, None].broadcast_to([P, TILES, E]),
                                        ALU.is_equal)
                dve.drain()

            o1, o2 = (t.rearrange(A, t=TILES) for t in ones_p)
            pick(logit[:], small[:, 36:36 + TILES], o1)
            nc.vector.scalar_tensor_tensor(cut, ones_p[0], -3e38, logit[:].rearrange("p t e -> p (t e)"),
                                           ALU.mult, ALU.add)
            dve.drain()
            pick(cut.rearrange(A, t=TILES), small[:, 72:72 + TILES], o2)
            nc.vector.tensor_tensor(cut, ones_p[0], ones_p[1], ALU.add).then_inc(s_oh, 1)
            nc.vector.tensor_tensor(m[:, 0:TILES], small[:, 72:72 + TILES], small[:, 36:36 + TILES], ALU.subtract
                                    ).then_inc(s_dl, 1)
            dve.wait_ge(s_de, 1)
            nc.vector.tensor_scalar(m[:, 36:36 + TILES], m[:, TILES:2 * TILES], 1.0, None, ALU.add)
            dve.drain()
            nc.vector.reciprocal(top_w[:, 0, :], m[:, 36:36 + TILES])
            dve.drain()
            nc.vector.tensor_tensor(top_w[:, 1, :], m[:, TILES:2 * TILES], top_w[:, 0, :], ALU.mult)
            dve.wait_ge(s_dp, 1)
            tot, incl, cnt = tmp[11], tmp[12], tmp[10][:, 0:E]
            nc.vector.tensor_copy(tot.rearrange("p (e t) -> p t e", e=E), tot_ps.rearrange(A, t=TILES))
            dve.drain()
            nc.vector.tensor_tensor_scan(incl, notfirst, tot, 0.0, ALU.mult, ALU.add)
            dve.drain()
            nc.vector.tensor_tensor(tot, incl, tot, ALU.subtract)
            nc.vector.tensor_copy(cnt, incl.rearrange("p (e t) -> p e t", e=E)[:, :, TILES - 1])
            dve.drain()
            nc.vector.tensor_tensor(cut.rearrange("p (e t) -> p e t", e=E), cnt[:, :, None].broadcast_to([P, E, TILES]),
                                    thr[:, None, :].broadcast_to([P, E, TILES]), ALU.is_gt)
            dve.drain()
            nb, ends, base = small[:, E:2 * E], small[:, 2 * E:3 * E], small[:, 3 * E:4 * E]
            nc.vector.tensor_reduce(nb, cut.rearrange("p (e t) -> p e t", e=E), AX.X, ALU.add)
            dve.drain()
            nc.vector.tensor_tensor_scan(ends, ones[:, 0:E], nb, 0.0, ALU.mult, ALU.add)
            dve.drain()
            nc.vector.tensor_tensor(base, ends, nb, ALU.subtract)
            dve.drain()
            nc.vector.scalar_tensor_tensor(tot.rearrange("p (e t) -> p e t", e=E),
                                           base[:, :, None].broadcast_to([P, E, TILES]), float(P),
                                           tot.rearrange("p (e t) -> p e t", e=E), ALU.mult, ALU.add)
            dve.drain()
            nc.vector.tensor_tensor(cut.rearrange(A, t=TILES), pref_ps.rearrange(A, t=TILES),
                                    tot.rearrange("p (e t) -> p t e", e=E), ALU.add)
            dve.drain()
            for k in range(TOP):
                nc.vector.tensor_tensor(ones_p[k], ones_p[k], cut, ALU.mult)
            dve.drain()
            for k in range(TOP):
                nc.vector.tensor_reduce(m[:, k * TILES:(k + 1) * TILES], (o1, o2)[k], AX.X, ALU.add)
            dve.drain()
            flat = tmp[11][:, 0:TOP * TILES].bitcast(I32)
            nc.vector.tensor_copy(flat, m[:, 0:TOP * TILES])
            dve.drain()
            ti = tmp[12].bitcast(I32)
            nc.vector.tensor_scalar(ti[:, 0:36], flat, P - 1, None, ALU.bitwise_and)
            nc.vector.tensor_scalar(ti[:, 36:72], flat, 7, None, ALU.logical_shift_right)
            dve.drain()
            nc.vector.tensor_copy(m[:, 0:72], ti[:, 0:72])
            dve.drain()
            N = TOP * TILES
            nc.vector.tensor_tensor(one_slot, iota[:, None, :].broadcast_to([P, N, P]),
                                    m[:, 0:N, None].broadcast_to([P, N, P]), ALU.is_equal)
            nc.vector.tensor_tensor(one_blk[:, :, 0, :], iota[:, None, 0:NBLK].broadcast_to([P, N, NBLK]),
                                    m[:, N:2 * N, None].broadcast_to([P, N, NBLK]), ALU.is_equal)
            dve.drain()
            nc.vector.tensor_scalar(one_blk[:, :, 1, :], one_blk[:, :, 0, :], pcol, None, ALU.mult)
            dve.drain()
            nc.vector.tensor_tensor(one_blk[:, :, 0, :], one_blk[:, :, 0, :],
                                    iota[:, 1:N + 1, None].broadcast_to([P, N, NBLK]), ALU.mult).then_inc(s_ip, 1)
            for b0, bn, dst in ((0, TILES, 0), (TILES, TILES, TILES), (2 * TILES, NBLK - 2 * TILES, 2 * TILES)):
                nc.vector.tensor_tensor(cut[:, 0:bn * E].rearrange("p (b e) -> p b e", e=E),
                                        iota[:, b0:b0 + bn, None].broadcast_to([P, bn, E]),
                                        ends[:, None, :].broadcast_to([P, bn, E]), ALU.is_ge)
                dve.drain()
                nc.vector.tensor_reduce(small[:, 40 + b0:40 + b0 + bn],
                                        cut[:, 0:bn * E].rearrange("p (b e) -> p b e", e=E), AX.X, ALU.add)
                dve.drain()
            nc.vector.tensor_scalar(expert_of, small[:, 40:40 + NBLK], float(E - 1), None, ALU.min).then_inc(s_blk, 1)
            spare = tmp[8][:, 0:NBLK]
            nc.vector.tensor_scalar(spare, iota[:, 0:NBLK], float(P), pcol, ALU.mult, ALU.add)
            dve.drain()
            nc.vector.tensor_scalar(spare, spare, float(PAIRS + P), None, ALU.add)
            dve.wait_ge(s_ip, 2)
            nc.vector.tensor_copy(m[:, 0:2 * NBLK], idx_ps)
            dve.drain()
            row, full = tmp[6][:, 0:NBLK], tmp[9][:, 0:NBLK]
            nc.vector.scalar_tensor_tensor(row, m[:, 0:NBLK], float(P), m[:, NBLK:2 * NBLK], ALU.mult, ALU.add)
            nc.vector.tensor_scalar(full, m[:, 0:NBLK], float(TILES) + 0.5, float(-TILES * P), ALU.is_ge, ALU.mult)
            dve.drain()
            nc.vector.tensor_tensor(full, full, row, ALU.add)
            nc.vector.tensor_scalar(m[:, 0:NBLK], m[:, 0:NBLK], 0.5, None, ALU.is_lt)
            dve.drain()
            nc.vector.tensor_scalar(gather_idx, full, float(-P), 0.0, ALU.add, ALU.max).then_inc(s_idx, 1)
            nc.vector.tensor_tensor(spare, spare, m[:, 0:NBLK], ALU.mult)
            dve.drain()
            nc.vector.scalar_tensor_tensor(scatter_idx, row, float(-P), spare, ALU.add, ALU.add
                                           ).then_inc(s_idx, 1)

            def weights_of(n, par, first):
                e = dve.value_load(expert_of[0:1, bass.ds(n, 1)], min_val=0, max_val=E - 1)
                if not first:
                    dve.wait_ge(s_ht, n - 1)
                nc.vector.tensor_scalar(b1_cur[:, par, :], b1_sb[:, e, :], 1.0, None, ALU.mult)
                nc.vector.tensor_scalar(w1_cur[:, par], w1_sb[:, e], 1.0, None, ALU.mult).then_inc(s_wcur, 1)

            def rows_out(n, par, first):
                e = dve.value_load(expert_of[0:1, bass.ds(n, 1)], min_val=0, max_val=E - 1)
                dve.wait_ge(s_w2, n + 1)
                if not first:
                    dve.wait_ge(s_yst[par], n // 2 * 16 if isinstance(n, int) else (n - par) * 8)
                nc.vector.tensor_tensor(ys[:, par, :], y_ps[par][:, 0:D], b2_bc[:, e, :], ALU.add).then_inc(s_ys, 1)

            dve.wait_ge(s_blk, 1)
            dve.wait_ge(s_lw, 16 * (2 * E + 1))
            weights_of(0, 0, True)
            weights_of(1, 1, True)
            dve.wait_ge(s_b2, 16)
            weights_of(2, 0, False)
            rows_out(0, 0, True)
            weights_of(3, 1, False)
            rows_out(1, 1, True)
            with dve.Fori(1, (NBLK - 3) // 2) as i:
                for par in range(2):
                    n = i * 2 + par
                    weights_of(n + 2, par, False)
                    rows_out(n, par, False)
            weights_of(NBLK - 1, 0, False)
            rows_out(NBLK - 3, 0, False)
            rows_out(NBLK - 2, 1, False)
            rows_out(NBLK - 1, 0, False)

            def combine(g, s, i):
                dve.wait_ge(s_g[s], (i + 1) * (16 * TOP))
                for k in range(TOP):
                    for j in range(IT):
                        t = g * IT + j
                        last = nc.vector.scalar_tensor_tensor(z[:, t, :], yg[:, s, k, j, :],
                                                              top_w[:, k, bass.ds(t, 1)], z[:, t, :],
                                                              ALU.mult, ALU.add)
                    if k == TOP - 1:
                        last.then_inc(s_z, 1)
                    dve.drain()
                for j in range(IT):
                    nc.vector.bn_stats(statf[:, j, :], z[:, g * IT + j, :])
                dve.drain()
                for j in range(IT):
                    nc.vector.bn_aggr(mvf[:, s, j, :], statf[:, j, :])
                dve.drain()
                nc.vector.tensor_tensor(varf[:, s, :], mvf[:, s, :, 1], eps[:], ALU.add).then_inc(s_mvf, 1)

            def finish(g, s, i):
                dve.wait_ge(s_rf, g + 1)
                if i is not None:
                    dve.wait_ge(s_ost[s], i * 16)
                for j in range(IT):
                    last = nc.vector.tensor_scalar(zn[:, s, j, :], z[:, g * IT + j, :], mvf[:, s, j, 0:1],
                                                   rstdf[:, s, j:j + 1], ALU.subtract, ALU.mult)
                last.then_inc(s_zn, 1)

            dve.wait_ge(s_n2back, 16)
            combine(0, 0, 0)
            for g in range(RING):
                combine(g + 1, (g + 1) % RING, (g + 1) // RING)
                finish(g, g, None)
            with dve.Fori(1, GROUPS // RING - 1) as i:
                for s in range(RING):
                    g = i * RING + s
                    combine(g + 1, (s + 1) % RING, i + (s + 1) // RING)
                    finish(g, s, i)
            for s in range(RING):
                g = GROUPS - RING + s
                if s + 1 < RING:
                    combine(g + 1, s + 1, GROUPS // RING - 1)
                finish(g, s, GROUPS // RING - 1)

        def tail_pe(pe):
            pe.wait_ge(s_oh, 1)
            nc.tensor.matmul(pref_ps, tmp[4][:, 0:P], tmp[9], start=True, stop=True)
            nc.tensor.matmul(tot_ps, ones[:], tmp[9], start=True, stop=True).then_inc(s_dp, 1)
            pe.wait_ge(s_ip, 1)
            N = TOP * TILES
            for n in range(N):
                last = nc.tensor.matmul(idx_ps, one_slot[:, n, :], one_blk[:, n, :, :], start=(n == 0), stop=(n == N - 1))
            last.then_inc(s_ip, 1)

            def rows_t(n, par):
                pe.wait_ge(s_xg[par], n // 2 * 16 + 16 if isinstance(n, int) else (n - par) * 8 + 16)
                if not (isinstance(n, int) and n == 0):
                    pe.wait_ge(s_xgte, n)
                for k in range(DC):
                    last = nc.tensor.transpose(xt_ps[:, k * P:k * P + P], xg[:, par, k * P:k * P + P], ident[:])
                last.then_inc(s_xgt, 1)

            def up(n, par, first):
                pe.wait_ge(s_xgte, n + 1)
                pe.wait_ge(s_wcur, n + 1)
                if not first:
                    pe.wait_ge(s_ht, n - 1)
                for c in range(FC):
                    for k in range(DC):
                        last = nc.tensor.matmul(hid[par][c // 4][:, c % 4 * P:c % 4 * P + P],
                                                w1_cur[:, par, k, c * P:c * P + P], xg_t[:, k, :],
                                                start=(k == 0), stop=(k == DC - 1))
                last.then_inc(s_w1, 1)

            def down(n, par, first):
                e = pe.value_load(expert_of[0:1, bass.ds(n, 1)], min_val=0, max_val=E - 1)
                pe.wait_ge(s_ht, n + 1)
                if not first:
                    pe.wait_ge(s_ys, n - 1)
                for c in range(FC):
                    last = nc.tensor.matmul(y_ps[par][:, 0:D], h_t[:, par, c, :], w2_sb[:, e, c, :], start=(c == 0),
                                            stop=(c == FC - 1))
                last.then_inc(s_w2, 1)

            pe.wait_ge(s_blk, 1)
            pe.wait_ge(s_lw, 16 * (2 * E + 1))
            rows_t(0, 0)
            up(0, 0, True)
            rows_t(1, 1)
            up(1, 1, True)
            rows_t(2, 0)
            down(0, 0, True)
            up(2, 0, False)
            rows_t(3, 1)
            down(1, 1, True)
            with pe.Fori(1, (NBLK - 3) // 2) as i:
                for par in range(2):
                    n = i * 2 + par
                    up(n + 1, 1 - par, False)
                    rows_t(n + 2, par)
                    down(n, par, False)
            up(NBLK - 2, 1, False)
            rows_t(NBLK - 1, 0)
            down(NBLK - 3, 0, False)
            up(NBLK - 1, 0, False)
            down(NBLK - 2, 1, False)
            down(NBLK - 1, 0, False)

        @block.sync
        def _(sp):
            load_x(sp, 0, 0)
            for kc, (f0, fn) in enumerate(KF):
                sp.dma_start(wtok[0:fn, kc, :], tok_w[f0:f0 + fn, :]).then_inc(s_w, 16)
            sp.dma_start(gam_tok[:], tok_gamma.broadcast_to([P, D])).then_inc(s_gam, 16)
            load_x(sp, 1, 1)
            sp.dma_start(wdkv_sb[:], w_dkv.rearrange("(k p) n -> p k n", p=P)).then_inc(s_const, 16)
            sp.dma_start(wq_sb[:], w_uq.rearrange("(k p) n -> p k n", p=P)).then_inc(s_const, 16)
            sp.dma_start(wuk_sb[:], w_uk).then_inc(s_const, 16)
            sp.dma_start(wuv_sb[:], w_uv).then_inc(s_const, 16)
            sp.dma_start(wo_sb[:], w_o.rearrange("(k p) n -> p k n", p=P)).then_inc(s_const, 16)
            sp.dma_start(wr_sb[:], w_router).then_inc(s_const, 16)
            sp.dma_start(br_bc[:], b_router.broadcast_to([P, E])).then_inc(s_const, 16)
            sp.dma_start(tid[:], text_ids).then_inc(s_const, 16)

            table_c = table.rearrange("(c r) d -> c (r d)", c=NCH).rearrange("c (p x) -> c p x", p=P)

            def load_chunks(t, first):
                for s in range(2):
                    if not first:
                        sp.wait_ge(s_scan[s], t)
                    sp.dma_start(chunk[:, s, :], table_c[t * 2 + s]).then_inc(s_chunk[s], 16)

            load_chunks(0, True)

            def store_parts(b):
                sp.wait_ge(s_parts, b + 1)
                sp.dma_start(qk_dram[b].rearrange("c (f p) t -> p c f t", p=P),
                             parts[b % 2].rearrange("p c a (f t) -> p (c a) f t", f=2)).then_inc(s_qst[b % 2], 16)

            def fill_q(b, hf, first, groups=range(P // HD)):
                if not first:
                    sp.wait_ge(s_S, (b - 1) * UNITS + (hf + 1) * (UNITS // 2))
                for g in groups:
                    r = slice(HD * g, HD * g + HD)
                    for dst, c in ((q_st, Q_PART[g]), (k_st, K_PART[g])):
                        sp.dma_start(dst[r, hf], qk_dram[b, c, hf * P:hf * P + P, :].rearrange(
                            "(s d) t -> d s t", d=HD)).then_inc(s_qm[hf], 16)

            for t in range(1, B + 1):
                load_chunks(t, False)
                if t >= 2:
                    store_parts(t - 2)
                if t == 3:
                    sp.wait_ge(s_qst[0], 16)
                if t in range(3, 7):
                    fill_q(0, (t - 3) // 2, True, range((t - 3) % 2 * 4, (t - 3) % 2 * 4 + 4))
            store_parts(B - 1)

            def store_n2(b):
                sp.wait_ge(s_n2, b + 1)
                sp.dma_start(n2_dram[bass.ds(b * (IT * P), IT * P), :].rearrange("(i p) d -> p i d", p=P),
                             n1[:]).then_inc(s_n2st, 16)

            for par in range(2):
                sp.wait_ge(s_qst[par], 16 * (B // 2))
            fill_q(1, 0, False)
            with sp.Fori(1, B - 1) as b:
                load_chunks(b + B, False)
                fill_q(b, 1, False)
                fill_q(b + 1, 0, False)
                store_n2(b - 1)
            load_chunks(2 * B - 1, False)
            fill_q(B - 1, 1, False)
            store_n2(B - 2)
            for s in range(2):
                sp.wait_ge(s_scan[s], 2 * B)
            load_w1(sp, range(W1_EARLY))
            sp.wait_ge(s_mask, 1)
            sp.wait_ge(s_qe, B + 1)
            for hf in range(2):
                for s in range(HH):
                    r = slice(HD * s, HD * s + HD)
                    sp.dma_start(q_txt[r, hf, s, :, :], q_text[r, hf]).then_inc(s_tq, 16)
            store_n2(B - 1)
            sp.wait_ge(s_pv, 2 * B)
            load_w1(sp, W1_MID)
            sp.wait_ge(s_tq, 16 * 2 * HH)
            load_w2(sp, 0, W2_EARLY)
            tail_sp(sp)

        @block.gpsimd
        def _(pool):
            nc.gpsimd.memset(neghalf[:], -0.5)
            nc.gpsimd.memset(eps[:], EPS)
            nc.gpsimd.memset(ident[:], 0.0)
            pool.drain()
            nc.gpsimd.affine_select(ident[:], ident[:], [[-1, P]], ALU.not_equal, 1.0, base=0, channel_multiplier=1
                                    ).then_inc(s_id, 1)

            def masks():
                nc.gpsimd.memset(ones[:], 1.0)
                nc.gpsimd.memset(mask_a[:], 0.0)
                nc.gpsimd.memset(mask_b[:], 0.0)
                nc.gpsimd.memset(mask_d[:], 0.0)
                nc.gpsimd.tensor_copy(ident_bf[:], ident[:])
                nc.gpsimd.memset(v_mask, 0.0)
                pool.drain()
                nc.gpsimd.affine_select(mask_a[:], mask_a[:], [[0, 4], [-1, P]], ALU.is_ge, NEG, base=0,
                                        channel_multiplier=1)
                nc.gpsimd.affine_select(mask_b[:], mask_b[:], [[0, 2], [-1, 2 * P]], ALU.is_ge, NEG, base=P,
                                        channel_multiplier=1)
                for j in range(4):
                    r = slice(NT * j, NT * j + NT)
                    pool.drain()
                    nc.gpsimd.affine_select(mask_d[r, :], mask_d[r, :], [[-1, T]], ALU.is_ge, NEG, base=NI,
                                            channel_multiplier=1)
                pool.drain()
                nc.gpsimd.memset(q_txt, 0.0).then_inc(s_mask, 1)

            def inv_std(var, via, res):
                nc.gpsimd.tensor_tensor(via[:], var, eps[:], ALU.add)
                pool.drain()
                return nc.gpsimd.tensor_tensor(res, via[:], neghalf[:], ALU.pow)

            def norm_rstds(b, prev, par=0):
                if b is not None:
                    pool.wait_ge(s_mv, 2 * b + 1)
                    inv_std(mv_emb[:, :, 1], vare_emb, rstd_emb[:]).then_inc(s_rstd, 1)
                if prev is not None:
                    pool.wait_ge(s_ke, prev + 1)
                    nc.gpsimd.tensor_tensor(parts[par][:, :, 1, :], rest, ones[:, 0:1, None].broadcast_to(
                        [P, 2, 2 * NI]), ALU.mult)
                    pool.drain()
                    nc.gpsimd.tensor_tensor(parts[par][:, :, 2, :], rest, parts[par][:, :, 1, :], ALU.subtract
                                            ).then_inc(s_parts, 1)
                if b is not None:
                    pool.wait_ge(s_mv, 2 * b + 2)
                    inv_std(mv[:, :, 1], vare, rstd[:]).then_inc(s_rstd, 1)

            norm_rstds(0, None)
            masks()
            norm_rstds(1, None)
            with pool.Fori(1, B // 2) as i:
                for par in range(2):
                    norm_rstds(i * 2 + par, i * 2 + par - 2, par)
            norm_rstds(None, B - 2, 0)
            norm_rstds(None, B - 1, 1)
            pool.wait_ge(s_const, NCONST)
            pool.wait_ge(s_tok, B)
            for j in range(TT):
                nc.gpsimd.indirect_dma_start(emb[:, j, :], None, table, bass.IndirectOffsetOnAxis(tid[:, j:j + 1], 0)
                                             ).then_inc(s_emb, 16)

            def fill_v(b, hf, part, count):
                if part == 0 and count is not None:
                    pool.wait_ge(s_pv, count)
                par, (rows, kt) = part % 2, ((slice(0, P), slice(0, 2)), (slice(0, NT), slice(2, 3)))[part // 2]
                return nc.gpsimd.tensor_copy(
                    v_mask[rows, kt, par, hf * P:hf * P + P].rearrange("p k (j z) -> p k j z", z=32)[
                        :, :, :, HD * par:HD * par + HD],
                    v_all[rows, b, kt, hf * P:hf * P + P].rearrange("p k (j z) -> p k j z", z=32)[
                        :, :, :, HD * par:HD * par + HD])

            def body(b, cur, prev):
                for u in range(UNITS):
                    if u == AT_NORM and prev:
                        pool.wait_ge(s_mv2, b)
                        inv_std(mv[:, :, 1], vare, rstd[:]).then_inc(s_rstd2, 1)
                    if cur:
                        kind, h0, n = unit(u)
                        w = P if kind == "A" else 2 * P
                        pool.wait_ge(s_rc, b * UNITS + u + 1)
                        p = probs[:, u % 4, 0:n * w].rearrange("p (h k) -> p h k", h=n)
                        nc.gpsimd.tensor_tensor(p, p, rsum[:, u % 4, 0:n, None].broadcast_to([P, n, w]), ALU.mult
                                                ).then_inc(s_P, 1)
                        for hf, at in enumerate(AT_FILL):
                            if u in (at, at + 1):
                                c = fill_v(b, hf, u - at, 2 * (b - 1) + hf + 1 if prev else None)
                                if u == at + 1:
                                    c.then_inc(s_vm, 1)
                    if u == AT_TERN and not cur:
                        pool.wait_ge(s_mv, 2 * B + 1)
                        inv_std(mv_emb[:, :, 1], vare_emb, rstd_emb[:]).then_inc(s_rstd, 1)

            pool.wait_ge(s_ve, B)
            body(0, True, False)
            with pool.Fori(1, B) as b:
                body(b, True, True)
            body(B, False, True)
            pool.wait_ge(s_ve, B + 1)
            with pool.Fori(0, B) as b:
                for hf in range(2):
                    for part in range(4):
                        c = fill_v(b, hf, part, 2 * B + 2 * (b - 1) + hf + 1)
                    c.then_inc(s_vm, 1)
            pool.wait_ge(s_mv2, B + 1)
            inv_std(mv[:, :, 1], vare, rstd[:]).then_inc(s_rstd2, 1)
            tail_pool(pool)

        @block.scalar
        def _(act):
            def scan(t, s):
                act.wait_ge(s_chunk[s], 16 * (t + 1))
                nc.scalar.activation(chunk[:, s, :], chunk[:, s, :], ACT.Abs,
                                     accum_out=part[:, bass.ds(t * 2 + s, 1)]).then_inc(s_scan[s], 1)

            def evacuate(b):
                act.wait_ge(s_nt, b + 1)
                nc.scalar.activation(n_t[:].rearrange("p k n -> p (k n)"), b_turn[0][:], ACT.Copy).then_inc(s_nte, 1)
                act.wait_ge(s_c, b + 1)
                nc.scalar.activation(c_t[:], b_ctx[0:LAT, 0:NI], ACT.Copy).then_inc(s_ce, 1)
                act.wait_ge(s_q, b + 1)

            def load_next_x(b, par):
                act.wait_ge(s_tok, b - 1)
                load_x(act, b, par)

            def front(b, par, first):
                evacuate(b)
                if not first:
                    act.wait_ge(s_qst[par], (b - par) * 8)
                nc.scalar.activation(parts[par][:, 0, 0, :], b_score[0][:], ACT.Copy, scale=SC).then_inc(s_qe, 1)
                act.wait_ge(s_k, b + 1)
                nc.scalar.activation(k_all[:, :, b, 0:NI], b_score[1][:].rearrange("p (f n) -> p f n", f=2), ACT.Copy)
                nc.scalar.activation(parts[par][:, 1, 0, :], b_score[1][:], ACT.Copy).then_inc(s_k1, 1)
                scan(b, 1)

            load_next_x(2, 0)
            for b in range(2):
                load_next_x(b + 3, 1 - b)
                front(b, b, True)
            with act.Fori(1, B // 2 - 2) as i:
                for par in range(2):
                    load_next_x(i * 2 + par + 3, 1 - par)
                    front(i * 2 + par, par, False)
            load_next_x(B - 1, 1)
            with act.Fori(B // 2 - 2, B // 2) as i:
                for par in range(2):
                    front(i * 2 + par, par, False)
            act.wait_ge(s_qst[1], 16 * (B // 2))

            def body(b, cur, prev):
                for u in range(UNITS):
                    bb, v = (b, u - 4) if u >= 4 else (b - 1, u - 4 + UNITS)
                    if v % 2 == 1 and (cur if u >= 4 else prev):
                        hf = v // (UNITS // 2)
                        act.wait_ge(s_T, bb * UNITS + v + 1)
                        if not (isinstance(bb, int) and bb == 0):
                            act.wait_ge(s_pv, 2 * (bb - 1) + hf + 1)
                        kind, h0, n = unit(v)
                        dst, src = turned_image(kind, h0, b_turn[1])
                        nc.scalar.activation(dst, src, ACT.Copy).then_inc(s_te_a, 1)
                    if u == 0 and prev:
                        evac_ctx(b - 1, 0)
                    if u == AT_PV1[3] + 1 and prev:
                        evac_ctx(b - 1, 1)
                    kind, h0, n = unit(u)
                    if cur:
                        act.wait_ge(s_max, b * UNITS + u + 1)
                        if prev or u >= 4:
                            act.wait_ge(s_T, b * UNITS + u - 3)
                        w = P if kind == "A" else 2 * P
                        for k in range(n):
                            last = nc.scalar.activation(probs[:, u % 4, k * w:k * w + w],
                                                        b_score[u % 4][:, k * w:k * w + w], ACT.Exp,
                                                        bias=negm[:, u % 4, k:k + 1],
                                                        accum_out=psums[:, u % 4, k:k + 1])
                        last.then_inc(s_exp, 1)
                    if u == AT_TEXT and not cur:
                        evacuate(B)
                        nc.scalar.activation(q_text, b_score[0][:].rearrange("p (f b n) -> p f b n", f=2, b=B),
                                             ACT.Copy, scale=SC).then_inc(s_qe, 1)
                    if u == AT_N2T and prev:
                        act.wait_ge(s_n2t, b)
                        nc.scalar.activation(n_t[:].rearrange("p k n -> p (k n)"), b_misc[:], ACT.Copy
                                             ).then_inc(s_n2te, 1)

            def evac_ctx(b, hf):
                act.wait_ge(s_pv, 2 * b + hf + 1)
                if not (isinstance(b, int) and b == 0):
                    act.wait_ge(s_o, b)
                nc.scalar.activation(ctx_t[:, hf, :], b_ctx[:, 0:NI], ACT.Copy).then_inc(s_cx, 1)

            def text_body(b, cur, prev):
                for u in range(TUNITS):
                    if u % 2 == 0 and prev:
                        v, hf = u + 1, u // 2
                        act.wait_ge(s_T, TXT + (b - 1) * TUNITS + v + 1)
                        act.wait_ge(s_pv, 2 * B + 2 * (b - 2) + hf + 1)
                        nc.scalar.activation(pt_txt[:, hf, 1, 0:2, :], b_turn[1][:, 0:2 * P].rearrange(
                            "p (c q) -> p c q", c=2), ACT.Copy)
                        nc.scalar.activation(pt_txt[0:NT, hf, 1, 2, :], b_turn[1][0:NT, 2 * P:3 * P], ACT.Copy
                                             ).then_inc(s_te_a, 1)
                    if cur:
                        act.wait_ge(s_max, TXT + b * TUNITS + u + 1)
                        act.wait_ge(s_T, TXT + b * TUNITS + u - 3)
                        nc.scalar.activation(probs[:, u, 0:T], b_score[u][:, 0:T], ACT.Exp, bias=negm[:, u, 0:1],
                                             accum_out=psums[:, u, 0:1]).then_inc(s_exp, 1)
                    if u % 2 == 1 and prev:
                        hf = u // 2
                        act.wait_ge(s_pv, 2 * B + 2 * (b - 1) + hf + 1)
                        nc.scalar.activation(ctx_txt[:, hf, b - 1, :], b_ctx[:, NI + NT * hf:NI + NT * hf + NT],
                                             ACT.Copy).then_inc(s_cx, 1)

            body(0, True, False)
            body(1, True, True)
            with act.Fori(2, B) as b:
                body(b, True, True)
            body(B, False, True)
            text_body(0, True, False)
            with act.Fori(1, B) as b:
                text_body(b, True, True)
            text_body(B, False, True)
            act.wait_ge(s_n2t, B + 1)
            nc.scalar.activation(n_t[:].rearrange("p k n -> p (k n)"), b_misc[:], ACT.Copy).then_inc(s_n2te, 1)
            tail_act(act)

        @block.vector
        def _(dve):
            def scan(t, s):
                dve.wait_ge(s_chunk[s], 16 * (t + 1))
                nc.vector.tensor_reduce(part[:, bass.ds(t * 2 + s, 1)], chunk[:, s, :], AX.X, ALU.add,
                                        apply_absolute_value=True).then_inc(s_scan[s], 1)

            def scan_half(b, i):
                s, half = i // 2, CHUNK // 2
                if i % 2 == 0:
                    dve.wait_ge(s_chunk[s], 16 * (b + B + 1))
                last = nc.vector.tensor_reduce(part[:, bass.ds(b * 4 + 2 * B + i, 1)],
                                               chunk[:, s, i % 2 * half:(i % 2 + 1) * half], AX.X, ALU.add,
                                               apply_absolute_value=True)
                if i % 2 == 1:
                    last.then_inc(s_scan[s], 1)

            def norm_stats(src, via, into):
                for i in range(IT):
                    nc.vector.bn_stats(via[:, i, :], src[i])
                dve.drain()
                for i in range(IT):
                    last = nc.vector.bn_aggr(into[:, i, :], via[:, i, :])
                return last

            def embed_stats(b, par):
                dve.wait_ge(s_tok, b + 1)
                norm_stats([b_emb[par][:, i * D:i * D + D] for i in range(IT)], stats_emb, mv_emb).then_inc(s_mv, 1)

            def embed_norm(b, par):
                dve.wait_ge(s_rstd, 2 * b + 1)
                for i in range(IT):
                    nc.vector.tensor_scalar(hr[:, i, :], b_emb[par][:, i * D:i * D + D], mv_emb[:, i, 0:1],
                                            rstd_emb[:, i:i + 1], ALU.subtract, ALU.mult)
                dve.drain()
                nc.vector.tensor_tensor(h_all[:, bass.ds(b * IT, IT), :], hr[:],
                                        gam_tok[:, None, :].broadcast_to([P, IT, D]), ALU.mult)
                dve.drain()
                h_stats(b * IT)

            def h_stats(t0):
                norm_stats([h_all[:, t0 + i, :] for i in range(IT)], stats, mv).then_inc(s_mv, 1)

            def attention_norm(t0, count):
                dve.wait_ge(s_rstd, count)
                for i in range(IT):
                    last = nc.vector.tensor_scalar(n1[:, i, :], h_all[:, t0 + i, :], mv[:, i, 0:1],
                                                   rstd[:, i:i + 1], ALU.subtract, ALU.mult)
                last.then_inc(s_n1, 1)

            def keys_values(b, par):
                if not (isinstance(b, int) and b == 0):
                    dve.wait_ge(s_parts, b)
                dve.wait_ge(s_qe, b + 1)
                nc.vector.scalar_tensor_tensor(rest[:, 0, :], b_score[0][:], SC, parts[par][:, 0, 0, :],
                                               ALU.mult, ALU.subtract).then_inc(s_rq, 1)
                dve.wait_ge(s_k1, b + 1)
                nc.vector.tensor_tensor(rest[:, 1, :], b_score[1][:], parts[par][:, 1, 0, :], ALU.subtract
                                        ).then_inc(s_ke, 1)
                dve.wait_ge(s_v, b + 1)
                nc.vector.tensor_copy(v_all[:, b, 0:2, :], b_score[2][:].rearrange("p (k d) -> p k d", k=2)
                                      ).then_inc(s_ve, 1)

            def front(b, par, first, last):
                if not first:
                    dve.wait_ge(s_nt, b)
                attention_norm(b * IT, 2 * b + 2)
                if not first:
                    keys_values(b - 1, 1 - par)
                if not last:
                    embed_stats(b + 1, 1 - par)
                scan(b, 0)
                if not last:
                    embed_norm(b + 1, 1 - par)

            embed_stats(0, 0)
            dve.wait_ge(s_gam, 16)
            embed_norm(0, 0)
            dve.wait_ge(s_const, NCONST)
            front(0, 0, True, False)
            front(1, 1, False, False)
            with dve.Fori(1, B // 2 - 1) as i:
                front(i * 2, 0, False, False)
                front(i * 2 + 1, 1, False, False)
            front(B - 2, 0, False, False)
            front(B - 1, 1, False, True)
            keys_values(B - 1, 1)

            def abs_sum():
                for s in range(2):
                    dve.wait_ge(s_scan[s], 2 * B)
                dve.drain()
                nc.vector.tensor_reduce(psum_abs[:], part[:], AX.X, ALU.add).then_inc(s_abs, 1)

            def quantise():
                dve.wait_ge(s_scl, 1)
                nc.vector.tensor_scalar(scl[:, 0:1], b_misc[:, 0:1], 1.0 / (V * D), EPS, ALU.mult, ALU.max
                                        ).then_inc(s_sclr, 1)
                dve.drain()
                nc.vector.reciprocal(scl[:, 1:2], scl[:, 0:1])
                dve.drain()
                nc.vector.reciprocal(scl[:, 2:3], scl[:, 1:2])
                dve.wait_ge(s_emb, 16 * TT)
                dve.drain()
                nc.vector.tensor_scalar(tern, emb, scl[:, 1:2], 0.5, ALU.mult, ALU.is_gt)
                nc.vector.tensor_scalar(low, emb, scl[:, 1:2], -0.5, ALU.mult, ALU.is_lt)
                dve.drain()
                nc.vector.tensor_tensor(tern, tern, low, ALU.subtract)
                dve.drain()
                nc.vector.tensor_scalar(h_all[:, B * IT:TILES, :], tern, scl[:, 2:3], None, ALU.mult)
                dve.drain()
                norm_stats([h_all[:, B * IT + i, :] for i in range(TT)], stats_emb, mv_emb).then_inc(s_mv, 1)

            def text_keys_values():
                dve.wait_ge(s_k, B + 1)
                nc.vector.tensor_copy(k_all[:, :, :, NI:T], b_score[1][:].rearrange("p (f b n) -> p f b n", f=2, b=B)
                                      ).then_inc(s_ke, 1)
                dve.wait_ge(s_v, B + 1)
                for i, bk in enumerate(b_text_v):
                    last = nc.vector.tensor_copy(v_all[0:NT, 2 * i:2 * i + 2, 2, :],
                                                 bk[0:NT, :].rearrange("p (k d) -> p k d", k=2))
                last.then_inc(s_ve, 1)

            def body(b, cur, prev):
                for u in range(UNITS):
                    bb, v = (b, u - 4) if u >= 4 else (b - 1, u - 4 + UNITS)
                    if v % 2 == 0 and (cur if u >= 4 else prev):
                        hf = v // (UNITS // 2)
                        dve.wait_ge(s_T, bb * UNITS + v + 1)
                        if not (isinstance(bb, int) and bb == 0):
                            dve.wait_ge(s_pv, 2 * (bb - 1) + hf + 1)
                        kind, h0, n = unit(v)
                        dst, src = turned_image(kind, h0, b_turn[0])
                        nc.vector.tensor_copy(dst, src).then_inc(s_te_d, 1)
                    kind, h0, n = unit(u)
                    if cur:
                        dve.wait_ge(s_S, b * UNITS + u + 1)
                        nc.vector.tensor_reduce(negm[:, u % 4, 0:n], b_score[u % 4][:].rearrange(
                            "p (h k) -> p h k", h=n), AX.X, ALU.max, negate=True).then_inc(s_max, 1)
                        if u > 0:
                            recip(b, u - 1)
                    if u == 0 and prev:
                        recip(b - 1, UNITS - 1)
                    if cur and u in AT_SCAN:
                        scan_half(b, AT_SCAN.index(u))
                    if not cur and u == AT_ABS:
                        abs_sum()
                    if not cur and u == AT_TERN:
                        quantise()
                    if not cur and u == AT_TERN + 1:
                        dve.wait_ge(s_rstd, 2 * B + 1)
                        for i in range(TT):
                            last = nc.vector.tensor_scalar(tern[:, i, :], h_all[:, B * IT + i, :], mv_emb[:, i, 0:1],
                                                           rstd_emb[:, i:i + 1], ALU.subtract, ALU.mult)
                        last.then_inc(s_n1, 1)
                    if not cur and u == AT_TEXT + 1:
                        text_keys_values()
                    if prev and u == AT_SUM:
                        after_attention(b - 1, (b - 1) * IT)
                    if prev and u == AT_STATS:
                        attention_stats((b - 1) * IT)
                    if prev and u == AT_NORM + 1:
                        after_norm(b - 1, (b - 1) * IT)
                    if prev and u == AT_ROUTE:
                        router_logits(b - 1, (b - 1) * IT)

            def recip(b, u):
                dve.wait_ge(s_exp, b * UNITS + u + 1)
                if not (isinstance(b, int) and b == 0 and u < 4):
                    dve.wait_ge(s_P, b * UNITS + u - 3)
                n = unit(u)[2]
                nc.vector.reciprocal(rsum[:, u % 4, 0:n], psums[:, u % 4, 0:n]).then_inc(s_rc, 1)

            def text_operands(b, hf):
                nc.vector.tensor_scalar(q_cur[:, hf], q_txt[:, hf, :, b, :], 1.0, None, ALU.mult)
                nc.vector.tensor_scalar(k_cur[:, hf, :], k_all[:, hf, b, :], 1.0, None, ALU.mult).then_inc(s_tqk, 1)

            def text_scale(b, u):
                dve.wait_ge(s_exp, TXT + b * TUNITS + u + 1)
                nc.vector.reciprocal(rsum[:, u, 0:1], psums[:, u, 0:1])
                dve.drain()
                nc.vector.tensor_scalar(probs[:, u, 0:T], probs[:, u, 0:T], rsum[:, u, 0:1], None, ALU.mult
                                        ).then_inc(s_P, 1)

            def text_body(b, cur, prev, more):
                for u in range(TUNITS):
                    if (u == 1 and prev) or (u == 3 and cur):
                        bb, v = (b - 1, 2) if u == 1 else (b, 0)
                        hf = v // 2
                        dve.wait_ge(s_T, TXT + bb * TUNITS + v + 1)
                        dve.wait_ge(s_pv, 2 * B + 2 * (bb - 1) + hf + 1)
                        nc.vector.tensor_copy(pt_txt[:, hf, 0, 0:2, :], b_turn[0][:, 0:2 * P].rearrange(
                            "p (c q) -> p c q", c=2))
                        nc.vector.tensor_copy(pt_txt[0:NT, hf, 0, 2, :], b_turn[0][0:NT, 2 * P:3 * P]
                                              ).then_inc(s_te_d, 1)

                    if cur:
                        dve.wait_ge(s_S, TXT + b * TUNITS + u + 1)
                        nc.vector.tensor_reduce(negm[:, u, 0:1], b_score[u][:, 0:T], AX.X, ALU.max, negate=True
                                                ).then_inc(s_max, 1)
                        if u % 2 == 1 and more:
                            text_operands(b + 1, u // 2)
                        if u > 0:
                            text_scale(b, u - 1)
                    if u == 0 and prev:
                        text_scale(b - 1, TUNITS - 1)

            def after_attention(b, t0):
                dve.wait_ge(s_o, b + 1)
                for i in range(IT):
                    nc.vector.tensor_tensor(h_all[:, t0 + i, :], b_misc[:, i * D:i * D + D], h_all[:, t0 + i, :],
                                            ALU.add)

            def attention_stats(t0):
                dve.drain()
                for i in range(IT):
                    nc.vector.bn_stats(stats[:, i, :], h_all[:, t0 + i, :])
                dve.drain()
                for i in range(IT):
                    last = nc.vector.bn_aggr(mv[:, i, :], stats[:, i, :])
                last.then_inc(s_mv2, 1)

            def after_norm(b, t0):
                dve.wait_ge(s_rstd2, b + 1)
                if not (isinstance(b, int) and b == 0):
                    dve.wait_ge(s_n2st, 16 * b)
                for i in range(IT):
                    last = nc.vector.tensor_scalar(n1[:, i, :], h_all[:, t0 + i, :], mv[:, i, 0:1],
                                                   rstd[:, i:i + 1], ALU.subtract, ALU.mult)
                last.then_inc(s_n2, 1)

            def router_logits(b, t0):
                dve.wait_ge(s_lg, b + 1)
                for i in range(IT):
                    last = nc.vector.tensor_tensor(logit[:, t0 + i, :], b_misc[:, i * E:i * E + E], br_bc[:], ALU.add)
                last.then_inc(s_lge, 1)

            body(0, True, False)
            body(1, True, True)
            with dve.Fori(2, B) as b:
                body(b, True, True)
            body(B, False, True)
            dve.wait_ge(s_tq, 16 * 2 * HH)
            dve.drain()
            text_operands(0, 0)
            text_operands(0, 1)
            text_body(0, True, False, True)
            with dve.Fori(1, B - 1) as b:
                text_body(b, True, True, True)
            text_body(B - 1, True, True, False)
            text_body(B, False, True, False)
            after_attention(B, B * IT)
            attention_stats(B * IT)
            after_norm(B, B * IT)
            router_logits(B, B * IT)
            tail_dve(dve)

        @block.tensor
        def _(pe):
            pe.wait_ge(s_w, 16 * 3)

            def transposes(src, dst):
                for k in range(DC):
                    for i in range(IT):
                        last = nc.tensor.transpose(dst[:, k * NI + i * P:k * NI + i * P + P],
                                                   src[:, i, k * P:k * P + P], ident[:])
                return last

            def projections(b, embed_next=None, src=n1):
                pe.wait_ge(s_n1, b + 1)
                transposes(src, b_turn[0]).then_inc(s_nt, 1)
                if embed_next:
                    embed_next()
                pe.wait_ge(s_nte, b + 1)
                for k in range(DC):
                    last = nc.tensor.matmul(b_ctx[0:LAT, 0:NI], wdkv_sb[:, k, :], n_t[:, k, :],
                                            start=(k == 0), stop=(k == DC - 1))
                last.then_inc(s_c, 1)
                if not (isinstance(b, int) and b == 0):
                    pe.wait_ge(s_rq, b)
                    pe.wait_ge(s_ke, b)
                    pe.wait_ge(s_ve, b)
                for f in range(2):
                    for k in range(DC):
                        last = nc.tensor.matmul(b_score[0][:, f * NI:f * NI + NI], wq_sb[:, k, f * P:f * P + P],
                                                n_t[:, k, :], start=(k == 0), stop=(k == DC - 1))
                last.then_inc(s_q, 1)
                pe.wait_ge(s_ce, b + 1)
                for f in range(2):
                    last = nc.tensor.matmul(b_score[1][:, f * NI:f * NI + NI], wuk_sb[:, f * P:f * P + P], c_t[:],
                                            start=True, stop=True)
                last.then_inc(s_k, 1)

            def embed(b, par):
                pe.wait_ge(s_xt[par], (b - par) * 16 + 32)
                for t in range(IT):
                    for kc, (_, fn) in enumerate(KF):
                        last = nc.tensor.matmul(b_emb[par][:, t * D:t * D + D], xt[0:fn, par, kc, t * P:t * P + P],
                                                wtok[0:fn, kc, :], start=(kc == 0), stop=(kc == len(KF) - 1))
                last.then_inc(s_tok, 1)

            def values(b):
                for t in range(IT):
                    last = nc.tensor.matmul(b_score[2][:, t * D:t * D + D], c_t[:, t * P:t * P + P], wuv_sb[:],
                                            start=True, stop=True)
                last.then_inc(s_v, 1)

            embed(0, 0)
            embed(1, 1)
            pe.wait_ge(s_const, NCONST)
            pe.wait_ge(s_id, 1)
            projections(0, embed_next=lambda: embed(2, 0))
            values(0)
            projections(1, embed_next=lambda: embed(3, 1))
            values(1)
            with pe.Fori(1, B // 2 - 1) as i:
                for par in range(2):
                    b = i * 2 + par
                    projections(b, embed_next=lambda: embed(b + 2, par))
                    values(b)
            for b in (B - 2, B - 1):
                projections(b)
                values(b)

            def text_projections():
                projections(B, src=tern)
                for i, bk in enumerate(b_text_v):
                    for j in range(2):
                        b = 2 * i + j
                        last = nc.tensor.matmul(bk[0:NT, j * D:j * D + D], c_t[:, b * NT:b * NT + NT], wuv_sb[:],
                                                start=True, stop=True)
                last.then_inc(s_v, 1)

            pe.wait_ge(s_mask, 1)
            pe.wait_ge(s_rq, B)
            pe.wait_ge(s_ke, B)
            pe.wait_ge(s_ve, B)

            def scores(b, u, first):
                kind, h0, n = unit(u)
                hf = h0 // HH
                if not (first and u < 4):
                    pe.wait_ge(s_exp, b * UNITS + u - 3)
                if u % (UNITS // 2) == 0:
                    pe.wait_ge(s_qm[hf], (b + 1) * (16 * 2 * (P // HD)))
                bk = b_score[u % 4]
                mask = mask_a if kind == "A" else mask_b
                nc.tensor.matmul(bk[:], ident_bf[:], mask[:].rearrange("p h k -> p (h k)"), start=True,
                                 stop=False, skip_group_check=True)
                for j in range(n):
                    s = (h0 + j) % HH
                    if kind == "A":
                        last = nc.tensor.matmul(bk[:, j * P:j * P + P], q_st[:, hf, s, 0:P],
                                                k_st[:, hf, s, 0:P], start=False, stop=True, skip_group_check=True)
                    else:
                        last = nc.tensor.matmul(bk[:, j * NI:j * NI + NI], q_st[:, hf, s, P:NI],
                                                k_st[:, hf, s, :], start=False, stop=True, skip_group_check=True)
                last.then_inc(s_S, 1)

            def turn(b, u, first):
                pe.wait_ge(s_P, b * UNITS + u + 1)
                if not (first and u < 2):
                    pe.wait_ge(s_te_d if u % 2 == 0 else s_te_a, b * (UNITS // 2) + u // 2)
                bk = b_turn[u % 2]
                for j in range(4):
                    last = nc.tensor.transpose(bk[:, j * P:j * P + P], probs[:, u % 4, j * P:j * P + P], ident[:])
                last.then_inc(s_T, 1)

            def weigh_values(b, hf, first, step):
                four, kt = step // 2, step % 2
                if kt == 0:
                    done = hf * (UNITS // 2) + 3 * four + 3
                    pe.wait_ge(s_te_d, b * (UNITS // 2) + (done + 1) // 2)
                    pe.wait_ge(s_te_a, b * (UNITS // 2) + done // 2)
                if step == 0:
                    pe.wait_ge(s_vm, b * 2 + hf + 1)
                    if not (first and hf == 0):
                        pe.wait_ge(s_cx, b * 2 + hf)
                for par in range(2):
                    for j in (2 * four, 2 * four + 1):
                        w = v_mask[:, kt, par, hf * P + 32 * j:hf * P + 32 * j + 32]
                        r = slice(32 * j, 32 * j + 32)
                        if kt == 0:
                            nc.tensor.matmul(b_ctx[r, 0:NI], w, pt_img[:, hf, 2 * j + par, 0:2, :],
                                             start=(par == 0), stop=False, skip_group_check=True)
                        else:
                            last = nc.tensor.matmul(b_ctx[r, P:NI], w, pt_img[:, hf, 2 * j + par, 2, :],
                                                    start=False, stop=(par == 1), skip_group_check=True)
                if step == 3:
                    last.then_inc(s_pv, 1)

            def text_scores(b, u):
                pe.wait_ge(s_exp, TXT + b * TUNITS + u - 3)
                hf = u // 2
                if u % 2 == 0:
                    pe.wait_ge(s_tqk, 2 * b + hf + 1)
                bk = b_score[u]
                nc.tensor.matmul(bk[:, 0:T], ident_bf[:], mask_d[:], start=True, stop=False, skip_group_check=True)
                nc.tensor.matmul(bk[:, 0:T], q_cur[:, hf, 4 * (u % 2):4 * (u % 2) + 4, :].rearrange("p s n -> p (s n)"),
                                 k_cur[:, hf, :], start=False, stop=True, skip_group_check=True).then_inc(s_S, 1)

            def text_turn(b, u):
                pe.wait_ge(s_P, TXT + b * TUNITS + u + 1)
                pe.wait_ge(s_te_d if u % 2 == 0 else s_te_a, TXT // 2 + b * (TUNITS // 2) + u // 2)
                bk = b_turn[u % 2]
                nc.tensor.transpose(bk[:, 0:P], probs[:, u, 0:P], ident[:])
                nc.tensor.transpose(bk[:, P:2 * P], probs[:, u, P:2 * P], ident[:])
                nc.tensor.transpose(bk[0:NT, 2 * P:3 * P], probs[:, u, NI:T], ident[:]).then_inc(s_T, 1)

            def text_weigh_values(b, hf):
                pe.wait_ge(s_te_d, TXT // 2 + b * 2 + hf + 1)
                pe.wait_ge(s_te_a, TXT // 2 + b * 2 + hf + 1)
                pe.wait_ge(s_vm, 2 * B + b * 2 + hf + 1)
                pe.wait_ge(s_cx, 2 * B + 2 * (b - 1) + hf + 1)
                for kt in range(3):
                    n = P if kt < 2 else NT
                    for par in range(2):
                        for j in range(4):
                            h = 2 * j + par
                            last = nc.tensor.matmul(
                                b_ctx[32 * j:32 * j + 32, NI + NT * hf:NI + NT * hf + NT],
                                v_mask[0:n, kt, par, hf * P + 32 * j:hf * P + 32 * j + 32],
                                pt_txt[0:n, hf, h // 4, kt, NT * (h % 4):NT * (h % 4) + NT],
                                start=(kt == 0 and par == 0), stop=(kt == 2 and par == 1), skip_group_check=True)
                last.then_inc(s_pv, 1)

            def text_body(b, cur, prev):
                for u in range(TUNITS):
                    if u % 2 == 1 and prev:
                        text_weigh_values(b - 1, u // 2)
                    if cur:
                        text_scores(b, u)
                    if u < TLAG and prev:
                        text_turn(b - 1, TUNITS - TLAG + u)
                    if u >= TLAG and cur:
                        text_turn(b, u - TLAG)

            def project_out(b, src, first):
                pe.wait_ge(s_cx, b * 2 + 2)
                if isinstance(b, int) and b == B - 1:
                    pe.wait_ge(s_sclr, 1)
                if not first:
                    pe.wait_ge(s_lge, b)
                for i in range(IT):
                    for f in range(2):
                        last = nc.tensor.matmul(b_misc[:, i * D:i * D + D], src(f, i), wo_sb[:, f, :],
                                                start=(f == 0), stop=(f == 1))
                last.then_inc(s_o, 1)

            def turn_norm(b):
                pe.wait_ge(s_n2, b + 1)
                transposes(n1, b_misc).then_inc(s_n2t, 1)

            def router(b):
                pe.wait_ge(s_n2te, b + 1)
                for i in range(IT):
                    for k in range(DC):
                        last = nc.tensor.matmul(b_misc[:, i * E:i * E + E], n_t[:, k, i * P:i * P + P], wr_sb[:, k, :],
                                                start=(k == 0), stop=(k == DC - 1))
                last.then_inc(s_lg, 1)

            def body(b, cur, prev):
                for u in range(UNITS):
                    if cur:
                        scores(b, u, not prev)
                    if u < LAG and prev:
                        turn(b - 1, UNITS - LAG + u, False)
                    if u >= LAG and cur:
                        turn(b, u - LAG, not prev)
                    for step in range(4):
                        if u == AT_PV1[step] and prev:
                            weigh_values(b - 1, 1, False, step)
                        if u == AT_PV0[step] and cur:
                            weigh_values(b, 0, not prev, step)
                    if u == AT_TERN and not cur:
                        pe.wait_ge(s_abs, 1)
                        pe.wait_ge(s_lge, B - 1)
                        nc.tensor.matmul(b_misc[:, 0:1], ones[:], psum_abs[:], start=True, stop=True
                                         ).then_inc(s_scl, 1)
                    if u == AT_OUT and prev:
                        project_out(b - 1, lambda f, i: ctx_t[:, f, i * P:i * P + P], isinstance(b, int) and b == 1)
                    if u == AT_TEXT and not cur:
                        text_projections()
                    if u == AT_N2T and prev:
                        turn_norm(b - 1)
                    if u == AT_ROUTE and prev:
                        router(b - 1)

            body(0, True, False)
            body(1, True, True)
            with pe.Fori(2, B) as b:
                body(b, True, True)
            body(B, False, True)
            pe.wait_ge(s_qe, B + 1)
            pe.wait_ge(s_ke, B + 1)
            pe.wait_ge(s_ve, B + 1)
            text_body(0, True, False)
            with pe.Fori(1, B) as b:
                text_body(b, True, True)
            text_body(B, False, True)
            pe.wait_ge(s_cx, 4 * B)
            for i in range(TT):
                for f in range(2):
                    last = nc.tensor.matmul(b_misc[:, i * D:i * D + D],
                                            ctx_txt[:, f, i * PB:i * PB + PB, :].rearrange("p b n -> p (b n)"),
                                            wo_sb[:, f, :], start=(f == 0), stop=(f == 1))
            last.then_inc(s_o, 1)
            turn_norm(B)
            router(B)
            tail_pe(pe)


def kernel(**inputs):
    import numpy as np
    import concourse.bacc as bacc
    from concourse.bass_utils import run_bass_kernel_spmd

    lay = np.ascontiguousarray
    x = np.asarray(inputs["x"])
    B, C, HT, WD = x.shape
    p = 8
    rows, cols = HT // p, WD // p
    w1, w2 = np.asarray(inputs["L0_ffn_W1"]), np.asarray(inputs["L0_ffn_W2"])
    E, FF, D = w1.shape
    args = {
        "x_patches": x.reshape(B, C, rows, p, cols, p).transpose(0, 1, 3, 5, 2, 4).reshape(B, C * p * p, rows * cols),
        "text_ids": np.asarray(inputs["x_txt"]).reshape(-1, P).T,
        "tok_w": inputs["L0_tok_W"],
        "tok_gamma": np.asarray(inputs["L0_tok_gamma"]).reshape(1, -1),
        "table": inputs["L0_txt_weight"],
        "w_dkv": inputs["L0_attn_W_DKV"],
        "w_uk": inputs["L0_attn_W_UK"],
        "w_uv": inputs["L0_attn_W_UV"],
        "w_uq": inputs["L0_attn_W_UQ"],
        "w_o": inputs["L0_attn_W_O"],
        "w_router": np.asarray(inputs["L0_ffn_Wr"]).T.reshape(D // P, P, E).transpose(1, 0, 2),
        "b_router": np.asarray(inputs["L0_ffn_br"]).reshape(1, -1),
        "w1": w1.transpose(2, 0, 1).reshape(D // P, P, E, FF).transpose(1, 2, 0, 3),
        "b1": np.asarray(inputs["L0_ffn_b1"]).reshape(E, FF // P, P).transpose(2, 0, 1),
        "w2": w2.transpose(2, 0, 1).reshape(FF // P, P, E, D).transpose(1, 2, 0, 3),
        "b2": np.asarray(inputs["L0_ffn_b2"]).reshape(1, -1),
        "gamma": np.asarray(inputs["L0_ffn_gamma"]).reshape(1, -1),
        "beta": np.asarray(inputs["L0_ffn_beta"]).reshape(1, -1),
    }
    nc = bacc.Bacc("TRN2", target_bir_lowering=False, num_devices=1)
    arrays, aps = {}, {}
    for name, a in args.items():
        arrays[name] = lay(np.asarray(a))
        aps[name] = nc.dram_tensor(name, arrays[name].shape, mybir.dt.from_np(arrays[name].dtype),
                                   kind="ExternalInput").ap()
    T = rows * cols + np.asarray(inputs["x_txt"]).shape[1]
    out = nc.dram_tensor("out", (B, T, D), F32, kind="ExternalOutput").ap()
    early_fusion_kernel(nc, out=out, **aps)
    return run_bass_kernel_spmd(nc, [arrays], core_ids=[0]).results[0]["out"]
```
